# Optimizing a Trainium2 kernel written in Bass

```python
import numpy as np
import jax
import jax.numpy as jnp

def _softmax(x, axis=-1):
    return jax.nn.softmax(x, axis=axis)

def _gelu(x):
    return jax.nn.gelu(x, approximate=True)

def _silu(x):
    return jax.nn.silu(x)

def _sigmoid(x):
    return jax.nn.sigmoid(x)

def _layernorm(x, axis=-1, eps=1e-05):
    m = jnp.mean(x, axis=axis, keepdims=True)
    v = jnp.var(x, axis=axis, keepdims=True)
    return (x - m) / jnp.sqrt(v + eps)

def _scatter_add(tgt, idx, src, axis=0):
    return tgt.at[idx].add(src)

def _segment_sum(src, seg, n):
    return jax.ops.segment_sum(src, seg, n)
kernel_name = 'mk_perceiver_d2_seqx_r8_2b8e0d'

def setup_inputs(seed: int=0):
    np.random.seed(seed)
    _w = jnp.asarray

    def _rec_inputs():
        import jax
        import jax.numpy as jnp
        _rk = jax.random.key(seed)
        x = 7.22e-05 + 1 * jax.random.normal(jax.random.fold_in(_rk, 1), (128, 32, 128), jnp.float32)
        _lenS = 32 - jax.random.randint(jax.random.fold_in(_rk, 7), (128,), 0, max(1, 32 // 4) + 1, jnp.int32)
        _lenS2 = 257 - jax.random.randint(jax.random.fold_in(_rk, 8), (128,), 0, max(1, 257 // 4) + 1, jnp.int32)
        _ctx_1024P = jax.random.normal(jax.random.fold_in(_rk, 11), (128, 16, 128), jnp.float32)
        _ctx_1024c = jax.random.dirichlet(jax.random.fold_in(_rk, 511), 0.3 * jnp.ones((16,), jnp.float32), (128, 257))
        _ctx_1024t = jnp.einsum('bsk,bkd->bsd', _ctx_1024c, _ctx_1024P)
        _ctx_1024t = _ctx_1024t * jax.lax.rsqrt(jnp.mean(jnp.square(_ctx_1024t)) + 1e-12) * 0.953939
        ctx_1024 = 4.13588e-05 + 0.999923 * (_ctx_1024t + 0.3 * jax.random.normal(jax.random.fold_in(_rk, 611), (128, 257, 128), jnp.float32))
        return (x, ctx_1024)
    x, ctx_1024 = _rec_inputs()

    def _L0_xattn_setup():
        import jax, jax.numpy as jnp
        import numpy as np
        B, SQ, SK, D = (4, 256, 256, 128)
        key = jax.random.key(seed)
        ks = jax.random.split(key, 8)
        s = 1.0 / np.sqrt(D)
        return {'input_seq': jax.random.normal(ks[0], (B, SQ, D), jnp.float32), 'condition_seq': jax.random.normal(ks[1], (B, SK, D), jnp.float32), 'Wq': jax.random.normal(ks[2], (D, D), jnp.float32) * s, 'bq': jnp.zeros((D,), jnp.float32), 'Wk': jax.random.normal(ks[3], (D, D), jnp.float32) * s, 'bk': jnp.zeros((D,), jnp.float32), 'Wv': jax.random.normal(ks[4], (D, D), jnp.float32) * s, 'bv': jnp.zeros((D,), jnp.float32)}
    _L0_xattn_all = _L0_xattn_setup()
    _L0_xattn_in = {k: v for k, v in _L0_xattn_all.items() if k in ('Wq', 'bq', 'Wk', 'bk', 'Wv', 'bv')}
    del _L0_xattn_all

    def _L0_attn_setup():
        import jax, jax.numpy as jnp
        import numpy as np
        B, L, E, H = (1, 512, 128, 16)
        D = E // H
        EPS = 1e-06
        key = jax.random.key(seed)
        k1, k2, k3 = jax.random.split(key, 3)
        x = jax.random.normal(k1, (B, L, E), dtype=jnp.float32)
        qkv_w = jax.random.normal(k2, (E, 3 * E), dtype=jnp.float32) / np.sqrt(E)
        qkv_b = jnp.zeros((3 * E,), dtype=jnp.float32)
        out_w = jax.random.normal(k3, (E, E), dtype=jnp.float32) / np.sqrt(E)
        out_b = jnp.zeros((E,), dtype=jnp.float32)
        return {'x': x, 'qkv_w': qkv_w, 'qkv_b': qkv_b, 'out_w': out_w, 'out_b': out_b}
    _L0_attn_all = _L0_attn_setup()
    _L0_attn_in = {k: v for k, v in _L0_attn_all.items() if k in ('qkv_w', 'qkv_b', 'out_w', 'out_b')}
    del _L0_attn_all

    def _L0_ffn_setup():
        import jax, jax.numpy as jnp
        import numpy as np
        E = 8
        TOP_K = 2
        LN_EPS = 1e-05

        def _layernorm(x, g, b):
            mu = jnp.mean(x, axis=-1, keepdims=True)
            var = jnp.var(x, axis=-1, keepdims=True)
            return (x - mu) * jax.lax.rsqrt(var + LN_EPS) * g + b
        key = jax.random.key(seed)
        ks = jax.random.split(key, 4)
        B, T, H, HF = (4, 256, 128, 256)
        s_in = 1.0 / np.sqrt(H)
        s_hid = 1.0 / np.sqrt(HF)
        return {'x': jax.random.normal(ks[0], (B, T, H), dtype=jnp.float32), 'ln_g': jnp.ones((H,), dtype=jnp.float32), 'ln_b': jnp.zeros((H,), dtype=jnp.float32), 'rW': jax.random.normal(ks[1], (H, E), dtype=jnp.float32) * s_in, 'rb': jnp.zeros((E,), dtype=jnp.float32), 'W1': jax.random.normal(ks[2], (E, H, HF), dtype=jnp.float32) * s_in, 'b1': jnp.zeros((E, HF), dtype=jnp.float32), 'W2': jax.random.normal(ks[3], (E, HF, H), dtype=jnp.float32) * s_hid, 'b2': jnp.zeros((E, H), dtype=jnp.float32)}
    _L0_ffn_all = _L0_ffn_setup()
    _L0_ffn_in = {k: v for k, v in _L0_ffn_all.items() if k in ('ln_g', 'ln_b', 'rW', 'rb', 'W1', 'b1', 'W2', 'b2')}
    del _L0_ffn_all

    def _L1_xattn_setup():
        import jax, jax.numpy as jnp
        import numpy as np
        N_HEAD = 16
        key = jax.random.key(seed)
        ks = jax.random.split(key, 5)
        b, l, d = (4, 256, 128)
        dh = d // N_HEAD
        return {'q': jax.random.normal(ks[0], (b, l, d), dtype=jnp.float32), 'kv': jax.random.normal(ks[1], (b, l, d), dtype=jnp.float32), 'Wq': jax.random.normal(ks[2], (d, d), dtype=jnp.float32) * 0.02, 'Wkv': jax.random.normal(ks[3], (2 * dh, d), dtype=jnp.float32) * 0.02, 'Wc': jax.random.normal(ks[4], (d, d), dtype=jnp.float32) * 0.02}
    _L1_xattn_all = _L1_xattn_setup()
    _L1_xattn_in = {k: v for k, v in _L1_xattn_all.items() if k in ('Wq', 'Wkv', 'Wc')}
    del _L1_xattn_all

    def _L1_attn_setup():
        import jax, jax.numpy as jnp
        import numpy as np
        D_MODEL = 128
        N_HEADS = 16
        HEAD_DIM = D_MODEL // N_HEADS
        ROPE_BASE = 10000.0

        def _rope_tables(T, dtype=jnp.float32):
            half = HEAD_DIM // 2
            inv_freq = 1.0 / ROPE_BASE ** (jnp.arange(0, HEAD_DIM, 2, dtype=jnp.float32) / HEAD_DIM)
            t = jnp.arange(T, dtype=jnp.float32)
            freqs = jnp.einsum('i,j->ij', t, inv_freq)
            return (jnp.cos(freqs).astype(dtype), jnp.sin(freqs).astype(dtype))

        def _apply_rotary(x, cos, sin):
            B, T, H, D = x.shape
            xr = x.reshape(B, T, H, D // 2, 2)
            x0, x1 = (xr[..., 0], xr[..., 1])
            c = cos[None, :, None, :]
            s = sin[None, :, None, :]
            out = jnp.stack([x0 * c - x1 * s, x0 * s + x1 * c], axis=-1)
            return out.reshape(B, T, H, D)
        key = jax.random.key(seed)
        ks = jax.random.split(key, 5)
        x = jax.random.normal(ks[0], (4, 128, D_MODEL), dtype=jnp.float32)
        init = 1.0 / np.sqrt(D_MODEL)
        Wq = jax.random.uniform(ks[1], (D_MODEL, D_MODEL), jnp.float32, -init, init)
        Wk = jax.random.uniform(ks[2], (D_MODEL, D_MODEL), jnp.float32, -init, init)
        Wv = jax.random.uniform(ks[3], (D_MODEL, D_MODEL), jnp.float32, -init, init)
        Wo = jax.random.uniform(ks[4], (D_MODEL, D_MODEL), jnp.float32, -init, init)
        return {'x': x, 'Wq': Wq, 'Wk': Wk, 'Wv': Wv, 'Wo': Wo}
    _L1_attn_all = _L1_attn_setup()
    _L1_attn_in = {k: v for k, v in _L1_attn_all.items() if k in ('Wq', 'Wk', 'Wv', 'Wo')}
    del _L1_attn_all

    def _L1_ffn_setup():
        import math
        import jax, jax.numpy as jnp
        import numpy as np
        HIDDEN = 128
        INTER = 512
        EXPERTS = 8
        B, T = (4, 256)
        EPS = 1e-12
        CAP_FACTOR = 1.0
        MIN_CAP = 4

        def layer_norm(x, g, b, eps=EPS):
            m = jnp.mean(x, axis=-1, keepdims=True)
            v = jnp.var(x, axis=-1, keepdims=True)
            return (x - m) * jax.lax.rsqrt(v + eps) * g + b

        def top1_gate(x, wg, capacity):
            logits = x @ wg
            gates = jax.nn.softmax(logits, axis=-1)
            E = wg.shape[-1]
            idx = jnp.argmax(gates, axis=-1)
            mask1 = jax.nn.one_hot(idx, E, dtype=gates.dtype)
            locations = jnp.cumsum(mask1, axis=0) - mask1
            mask1 = mask1 * (locations < capacity).astype(gates.dtype)
            gates1_s = jnp.sum(gates * mask1, axis=-1)
            loc_s = jnp.sum(locations * mask1, axis=-1).astype(jnp.int32)
            loc_oh = jax.nn.one_hot(loc_s, capacity, dtype=gates.dtype)
            combine = gates1_s[:, None, None] * mask1[:, :, None] * loc_oh[:, None, :]
            dispatch = jax.lax.stop_gradient((combine > 0).astype(x.dtype))
            return (combine, dispatch)
        key = jax.random.key(seed)
        ks = jax.random.split(key, 8)
        s = 0.02
        return {'x': jax.random.normal(ks[0], (B, T, HIDDEN), jnp.float32), 'attn_nw': jnp.ones((HIDDEN,), jnp.float32), 'attn_nb': jnp.zeros((HIDDEN,), jnp.float32), 'wg': jax.random.normal(ks[1], (HIDDEN, EXPERTS), jnp.float32) * s, 'inter_w': jax.random.normal(ks[2], (EXPERTS, HIDDEN, INTER), jnp.float32) * s, 'inter_b': jnp.zeros((EXPERTS, INTER), jnp.float32), 'output_w': jax.random.normal(ks[3], (EXPERTS, INTER, HIDDEN), jnp.float32) * s, 'output_b': jnp.zeros((EXPERTS, HIDDEN), jnp.float32), 'res_inter_w': jax.random.normal(ks[4], (HIDDEN, INTER), jnp.float32) * s, 'res_inter_b': jnp.zeros((INTER,), jnp.float32), 'res_output_w': jax.random.normal(ks[5], (INTER, HIDDEN), jnp.float32) * s, 'res_output_b': jnp.zeros((HIDDEN,), jnp.float32), 'res_coef': jax.random.normal(ks[6], (HIDDEN, 2), jnp.float32) * s}
    _L1_ffn_all = _L1_ffn_setup()
    _L1_ffn_in = {k: v for k, v in _L1_ffn_all.items() if k in ('attn_nw', 'attn_nb', 'wg', 'inter_w', 'inter_b', 'output_w', 'output_b', 'res_inter_w', 'res_inter_b', 'res_output_w', 'res_output_b', 'res_coef')}
    del _L1_ffn_all
    return {'x': x, 'ctx_1024': ctx_1024, 'L0_xattn_Wq': _L0_xattn_in['Wq'], 'L0_xattn_bq': _L0_xattn_in['bq'], 'L0_xattn_Wk': _L0_xattn_in['Wk'], 'L0_xattn_bk': _L0_xattn_in['bk'], 'L0_xattn_Wv': _L0_xattn_in['Wv'], 'L0_xattn_bv': _L0_xattn_in['bv'], 'L0_attn_qkv_w': _L0_attn_in['qkv_w'], 'L0_attn_qkv_b': _L0_attn_in['qkv_b'], 'L0_attn_out_w': _L0_attn_in['out_w'], 'L0_attn_out_b': _L0_attn_in['out_b'], 'L0_ffn_ln_g': _L0_ffn_in['ln_g'], 'L0_ffn_ln_b': _L0_ffn_in['ln_b'], 'L0_ffn_rW': _L0_ffn_in['rW'], 'L0_ffn_rb': _L0_ffn_in['rb'], 'L0_ffn_W1': _L0_ffn_in['W1'], 'L0_ffn_b1': _L0_ffn_in['b1'], 'L0_ffn_W2': _L0_ffn_in['W2'], 'L0_ffn_b2': _L0_ffn_in['b2'], 'L1_xattn_Wq': _L1_xattn_in['Wq'], 'L1_xattn_Wkv': _L1_xattn_in['Wkv'], 'L1_xattn_Wc': _L1_xattn_in['Wc'], 'L1_attn_Wq': _L1_attn_in['Wq'], 'L1_attn_Wk': _L1_attn_in['Wk'], 'L1_attn_Wv': _L1_attn_in['Wv'], 'L1_attn_Wo': _L1_attn_in['Wo'], 'L1_ffn_attn_nw': _L1_ffn_in['attn_nw'], 'L1_ffn_attn_nb': _L1_ffn_in['attn_nb'], 'L1_ffn_wg': _L1_ffn_in['wg'], 'L1_ffn_inter_w': _L1_ffn_in['inter_w'], 'L1_ffn_inter_b': _L1_ffn_in['inter_b'], 'L1_ffn_output_w': _L1_ffn_in['output_w'], 'L1_ffn_output_b': _L1_ffn_in['output_b'], 'L1_ffn_res_inter_w': _L1_ffn_in['res_inter_w'], 'L1_ffn_res_inter_b': _L1_ffn_in['res_inter_b'], 'L1_ffn_res_output_w': _L1_ffn_in['res_output_w'], 'L1_ffn_res_output_b': _L1_ffn_in['res_output_b'], 'L1_ffn_res_coef': _L1_ffn_in['res_coef']}

def reference(x, ctx_1024, L0_xattn_Wq, L0_xattn_bq, L0_xattn_Wk, L0_xattn_bk, L0_xattn_Wv, L0_xattn_bv, L0_attn_qkv_w, L0_attn_qkv_b, L0_attn_out_w, L0_attn_out_b, L0_ffn_ln_g, L0_ffn_ln_b, L0_ffn_rW, L0_ffn_rb, L0_ffn_W1, L0_ffn_b1, L0_ffn_W2, L0_ffn_b2, L1_xattn_Wq, L1_xattn_Wkv, L1_xattn_Wc, L1_attn_Wq, L1_attn_Wk, L1_attn_Wv, L1_attn_Wo, L1_ffn_attn_nw, L1_ffn_attn_nb, L1_ffn_wg, L1_ffn_inter_w, L1_ffn_inter_b, L1_ffn_output_w, L1_ffn_output_b, L1_ffn_res_inter_w, L1_ffn_res_inter_b, L1_ffn_res_output_w, L1_ffn_res_output_b, L1_ffn_res_coef):
    import jax
    import jax.numpy as jnp

    def _L0_xattn_ref(input_seq, condition_seq, Wq, bq, Wk, bk, Wv, bv):
        import jax, jax.numpy as jnp
        import numpy as np
        B, SQ, SK, D = (4, 256, 256, 128)
        q = jnp.einsum('bsd,ed->bse', input_seq, Wq) + bq
        k = jnp.einsum('btd,ed->bte', condition_seq, Wk) + bk
        v = jnp.einsum('btd,ed->bte', condition_seq, Wv) + bv
        scores = jnp.einsum('bse,bte->bst', q, k)
        attn = jax.nn.softmax(scores, axis=-1)
        attended = jnp.einsum('bst,bte->bse', attn, v)
        return attended

    def _L0_attn_ref(x, qkv_w, qkv_b, out_w, out_b):
        import jax, jax.numpy as jnp
        import numpy as np
        B, L, E, H = (1, 512, 128, 16)
        D = E // H
        EPS = 1e-06
        b, l, e = x.shape
        qkv = x @ qkv_w + qkv_b
        q, k, v = jnp.split(qkv, 3, axis=-1)
        q = q.reshape(b, l, H, D).transpose(0, 2, 1, 3)
        k = k.reshape(b, l, H, D).transpose(0, 2, 1, 3)
        v = v.reshape(b, l, H, D).transpose(0, 2, 1, 3)
        q_prime = jax.nn.elu(q) + 1.0
        k_prime = jax.nn.elu(k) + 1.0
        kv_prod = jnp.einsum('bhld,bhle->bhlde', k_prime, v)
        kv_cumsum = jnp.cumsum(kv_prod, axis=2)
        context = jnp.einsum('bhld,bhlde->bhle', q_prime, kv_cumsum)
        k_cumsum = jnp.cumsum(k_prime, axis=2)
        norm = jnp.einsum('bhld,bhld->bhl', q_prime, k_cumsum)
        output = context / (norm[..., None] + EPS)
        output = output.transpose(0, 2, 1, 3).reshape(b, l, e)
        return output @ out_w + out_b

    def _L0_ffn_ref(x, ln_g, ln_b, rW, rb, W1, b1, W2, b2):
        import jax, jax.numpy as jnp
        import numpy as np
        E = 8
        TOP_K = 2
        LN_EPS = 1e-05

        def _layernorm(x, g, b):
            mu = jnp.mean(x, axis=-1, keepdims=True)
            var = jnp.var(x, axis=-1, keepdims=True)
            return (x - mu) * jax.lax.rsqrt(var + LN_EPS) * g + b
        z = _layernorm(x, ln_g, ln_b)
        logits = jnp.einsum('bth,he->bte', z, rW) + rb
        probs = jax.nn.softmax(logits, axis=-1)
        topv, topi = jax.lax.top_k(probs, TOP_K)
        mask = jnp.sum(jax.nn.one_hot(topi, E, dtype=probs.dtype) * topv[..., None], axis=-2)
        denom = jnp.maximum(jnp.sum(mask, axis=-1, keepdims=True), 1e-08)
        w = mask / denom
        hid = jax.nn.gelu(jnp.einsum('bth,ehf->btef', z, W1) + b1, approximate=False)
        outs = jnp.einsum('btef,efh->bteh', hid, W2) + b2
        mixed = jnp.sum(outs * w[..., None], axis=2)
        return x + mixed

    def _L1_xattn_ref(q, kv, Wq, Wkv, Wc):
        import jax, jax.numpy as jnp
        import numpy as np
        N_HEAD = 16
        b, l, d = q.shape
        h = N_HEAD
        dh = d // h
        qp = jnp.einsum('bld,ed->ble', q, Wq)
        scores = jnp.einsum('bld,bmd->blm', qp, kv)
        idx = jnp.argmax(scores, axis=-1)
        mem = jnp.take_along_axis(kv, idx[..., None], axis=1)
        mkv = jnp.einsum('bld,ed->ble', mem, Wkv)
        mk, mv = jnp.split(mkv, 2, axis=-1)
        qh = qp.reshape(b, l, h, dh).transpose(0, 2, 1, 3)
        scale = 1.0 / np.sqrt(dh).astype(np.float32)
        logits = jnp.einsum('bhld,bmd->bhlm', qh, mk) * scale
        attn = jax.nn.softmax(logits, axis=-1)
        out = jnp.einsum('bhlm,bmd->bhld', attn, mv)
        out = out.transpose(0, 2, 1, 3).reshape(b, l, d)
        return jnp.einsum('bld,ed->ble', out, Wc)

    def _L1_attn_ref(x, Wq, Wk, Wv, Wo):
        import jax, jax.numpy as jnp
        import numpy as np
        D_MODEL = 128
        N_HEADS = 16
        HEAD_DIM = D_MODEL // N_HEADS
        ROPE_BASE = 10000.0

        def _rope_tables(T, dtype=jnp.float32):
            half = HEAD_DIM // 2
            inv_freq = 1.0 / ROPE_BASE ** (jnp.arange(0, HEAD_DIM, 2, dtype=jnp.float32) / HEAD_DIM)
            t = jnp.arange(T, dtype=jnp.float32)
            freqs = jnp.einsum('i,j->ij', t, inv_freq)
            return (jnp.cos(freqs).astype(dtype), jnp.sin(freqs).astype(dtype))

        def _apply_rotary(x, cos, sin):
            B, T, H, D = x.shape
            xr = x.reshape(B, T, H, D // 2, 2)
            x0, x1 = (xr[..., 0], xr[..., 1])
            c = cos[None, :, None, :]
            s = sin[None, :, None, :]
            out = jnp.stack([x0 * c - x1 * s, x0 * s + x1 * c], axis=-1)
            return out.reshape(B, T, H, D)
        B, T, C = x.shape
        H, Dh = (N_HEADS, HEAD_DIM)
        scale = Dh ** (-0.5)
        q = (x @ Wq.T).reshape(B, T, H, Dh)
        k = (x @ Wk.T).reshape(B, T, H, Dh)
        v = (x @ Wv.T).reshape(B, T, H, Dh)
        cos, sin = _rope_tables(T, x.dtype)
        q = _apply_rotary(q, cos, sin)
        k = _apply_rotary(k, cos, sin)
        q = q.transpose(0, 2, 1, 3).astype(jnp.float32)
        k = k.transpose(0, 2, 1, 3).astype(jnp.float32)
        v = v.transpose(0, 2, 1, 3)
        scores = jnp.einsum('bhqd,bhkd->bhqk', q, k) * scale
        causal = jnp.triu(jnp.ones((T, T), dtype=bool), k=1)
        scores = jnp.where(causal[None, None], -jnp.inf, scores)
        attn = jax.nn.softmax(scores, axis=-1).astype(v.dtype)
        out = jnp.einsum('bhqk,bhkd->bhqd', attn, v)
        out = out.transpose(0, 2, 1, 3).reshape(B, T, C)
        return out @ Wo.T

    def _L1_ffn_ref(x, attn_nw, attn_nb, wg, inter_w, inter_b, output_w, output_b, res_inter_w, res_inter_b, res_output_w, res_output_b, res_coef):
        import math
        import jax, jax.numpy as jnp
        import numpy as np
        HIDDEN = 128
        INTER = 512
        EXPERTS = 8
        B, T = (4, 256)
        EPS = 1e-12
        CAP_FACTOR = 1.0
        MIN_CAP = 4

        def layer_norm(x, g, b, eps=EPS):
            m = jnp.mean(x, axis=-1, keepdims=True)
            v = jnp.var(x, axis=-1, keepdims=True)
            return (x - m) * jax.lax.rsqrt(v + eps) * g + b

        def top1_gate(x, wg, capacity):
            logits = x @ wg
            gates = jax.nn.softmax(logits, axis=-1)
            E = wg.shape[-1]
            idx = jnp.argmax(gates, axis=-1)
            mask1 = jax.nn.one_hot(idx, E, dtype=gates.dtype)
            locations = jnp.cumsum(mask1, axis=0) - mask1
            mask1 = mask1 * (locations < capacity).astype(gates.dtype)
            gates1_s = jnp.sum(gates * mask1, axis=-1)
            loc_s = jnp.sum(locations * mask1, axis=-1).astype(jnp.int32)
            loc_oh = jax.nn.one_hot(loc_s, capacity, dtype=gates.dtype)
            combine = gates1_s[:, None, None] * mask1[:, :, None] * loc_oh[:, None, :]
            dispatch = jax.lax.stop_gradient((combine > 0).astype(x.dtype))
            return (combine, dispatch)
        Bx, Tx, M = x.shape
        S = Bx * Tx
        E = wg.shape[-1]
        capacity = max(MIN_CAP, math.ceil(S / E * CAP_FACTOR))
        residual = x.reshape(S, M)
        attn_out = layer_norm(residual, attn_nw, attn_nb)
        combine, dispatch = top1_gate(attn_out, wg, capacity)
        dispatched = jnp.einsum('sec,sm->ecm', dispatch, attn_out)
        h = jax.nn.gelu(jnp.einsum('ecm,emi->eci', dispatched, inter_w) + inter_b[:, None, :], approximate=True)
        expert_out = jnp.einsum('eci,eim->ecm', h, output_w) + output_b[:, None, :]
        moe_out = jnp.einsum('sec,ecm->sm', combine, expert_out)
        rh = jax.nn.gelu(attn_out @ res_inter_w + res_inter_b, approximate=True)
        res_mlp_out = rh @ res_output_w + res_output_b
        coef = jax.nn.softmax(attn_out @ res_coef, axis=-1)
        out = res_mlp_out * coef[:, :1] + moe_out * coef[:, 1:]
        out = out + residual
        return out.reshape(Bx, Tx, M)
    x = x + _L0_xattn_ref(_layernorm(x, axis=-1), ctx_1024, L0_xattn_Wq, L0_xattn_bq, L0_xattn_Wk, L0_xattn_bk, L0_xattn_Wv, L0_xattn_bv)
    x = x + _L0_attn_ref(_layernorm(x, axis=-1), L0_attn_qkv_w, L0_attn_qkv_b, L0_attn_out_w, L0_attn_out_b)
    x = x + _L0_ffn_ref(_layernorm(x, axis=-1), L0_ffn_ln_g, L0_ffn_ln_b, L0_ffn_rW, L0_ffn_rb, L0_ffn_W1, L0_ffn_b1, L0_ffn_W2, L0_ffn_b2)
    x = x + _L1_xattn_ref(_layernorm(x, axis=-1), ctx_1024, L1_xattn_Wq, L1_xattn_Wkv, L1_xattn_Wc)
    x = x + _L1_attn_ref(_layernorm(x, axis=-1), L1_attn_Wq, L1_attn_Wk, L1_attn_Wv, L1_attn_Wo)
    x = x + _L1_ffn_ref(_layernorm(x, axis=-1), L1_ffn_attn_nw, L1_ffn_attn_nb, L1_ffn_wg, L1_ffn_inter_w, L1_ffn_inter_b, L1_ffn_output_w, L1_ffn_output_b, L1_ffn_res_inter_w, L1_ffn_res_inter_b, L1_ffn_res_output_w, L1_ffn_res_output_b, L1_ffn_res_coef)
    return x

_drawn_inputs = setup_inputs


def setup_inputs(seed=0):
    import zlib

    import numpy as np

    out = dict(_drawn_inputs(seed))
    spreads = {'L0_xattn_bq': (0.0, 0.1),
     'L0_xattn_bk': (0.0, 0.8),
     'L0_xattn_bv': (0.0, 0.1),
     'L0_attn_qkv_b': (0.0, 0.1),
     'L0_attn_out_b': (0.0, 0.1),
     'L0_ffn_ln_g': (1.0, 0.2),
     'L0_ffn_ln_b': (0.0, 0.1),
     'L0_ffn_rb': (0.0, 0.1),
     'L0_ffn_b1': (0.0, 0.423),
     'L0_ffn_b2': (0.0, 0.295),
     'L1_ffn_attn_nw': (1.0, 0.6),
     'L1_ffn_attn_nb': (0.0, 0.8),
     'L1_ffn_inter_b': (0.0, 0.8),
     'L1_ffn_output_b': (0.0, 0.8),
     'L1_ffn_res_inter_b': (0.0, 0.8),
     'L1_ffn_res_output_b': (0.0, 0.653)}
    factors = {'L1_xattn_Wq': 7.595,
     'L1_xattn_Wkv': 4.528,
     'L1_xattn_Wc': 4.343,
     'L1_attn_Wq': 5.336,
     'L1_attn_Wk': 5.373,
     'L1_ffn_wg': 8.0,
     'L1_ffn_inter_w': 8.0,
     'L1_ffn_output_w': 8.0,
     'L1_ffn_res_inter_w': 7.325,
     'L1_ffn_res_output_w': 6.748,
     'L1_ffn_res_coef': 8.0}
    for name, (base, spread) in spreads.items():
        noise = np.random.default_rng([zlib.crc32(name.encode()), seed]).standard_normal(out[name].shape)
        drawn = base * np.exp(spread * noise) if base else spread * noise
        out[name] = jnp.asarray(drawn.astype(out[name].dtype))
    for name, factor in factors.items():
        out[name] = (out[name] * factor).astype(out[name].dtype)
    return out
```

```python
from contextlib import ExitStack

import numpy as np

import concourse.bass as bass
from concourse import mybir

F32 = mybir.dt.float32
BF16 = mybir.dt.bfloat16
U32 = mybir.dt.uint32
ALU = mybir.AluOpType
ACT = mybir.ActivationFunctionType
AX_X = mybir.AxisListType.X

P = 128
BATCH, SEQ, D = 128, 32, 128
KEYS = 257
TOKENS = BATCH * SEQ
TILES = TOKENS // P
TPG = 4
GROUPS = TILES // TPG
GT = TPG * P
BPT = P // SEQ
HEADS, DH = 16, 8
Q4, H4 = 4, 4
QW = H4 * DH
VW = QW + H4
E0, F0 = 8, 256
E1, F1 = 8, 512
CAP = TOKENS // E1
LOADS = 32
STAGES = 6
ONLY = None


def columns(widths):
    at, out = 0, {}
    for name, w in widths:
        out[name] = (at, w)
        at += w
    return out, at


CONST, CONST_W = columns([
    ("ident", 128), ("batch4", 4), ("quarter4", 4), ("head4", 4), ("headblock", 32), ("causal", 32),
    ("cos", 32), ("sin", 32), ("maskneg", 32), ("spread", 128), ("before", 128), ("ones", 128),
    ("keybase", 32), ("headcol", 4), ("rank8", 8), ("expertbase", 8), ("tokenid", 32), ("restart", 256), ("minushalf", 4)])
SMALL, SMALL_W = columns([
    ("x_wqT", 128), ("x_wk", 128), ("x_wvT", 128), ("x_bq", 1), ("x_bk", 1), ("x_bv", 128),
    ("a_w", 256), ("a_bq", 1), ("a_bk", 1), ("a_wv", 128), ("a_bvh", 32), ("a_wo", 128), ("a_bo", 128),
    ("f_g", 1), ("f_b", 1), ("f_rw", 8), ("f_rb", 8), ("f_b1", 16), ("f_b2", 128),
    ("y_wqT", 128), ("y_wkrepT", 128), ("y_wvT", 8), ("y_wcT", 128),
    ("b_wqT", 128), ("b_wqsT", 128), ("b_wkT", 128), ("b_wksT", 128), ("b_wvT", 128), ("b_woT", 128),
    ("g_nw", 128), ("g_nb", 128), ("g_w", 10), ("g_rb1", 4), ("g_rb2", 128), ("g_b1", 32)])


class Steps:

    def __init__(self, eng, sem, per):
        self.eng, self.sem, self.per = eng, sem, per

    def start(self, g):
        self.before, self.n = g * self.per, 0

    def end(self):
        assert self.n == self.per, ("steps of a group", self.n)

    def did(self, ins):
        ins.then_inc(self.sem, 1)
        self.n += 1

    def settle(self):
        self.eng.wait_ge(self.sem, self.before + self.n)


def build(nc, a, out):
    with ExitStack() as ctx:
        def sb(name, shape, dt=F32):
            return ctx.enter_context(nc.sbuf_tensor(name, shape, dt))

        def sem(name):
            return ctx.enter_context(nc.semaphore(name))

        bank = [ctx.enter_context(nc.psum_tensor(f"bank{k}", [P, 512], F32)) for k in range(8)]

        X = sb("X", [P, TILES * D])
        const = sb("const", [P, CONST_W])
        small = sb("small", [P, SMALL_W])
        Z = sb("Z", [P, TPG, D])
        zT = sb("zT", [P, GT])
        stats = sb("stats", [P, TPG, 6])
        moments = sb("moments", [P, TPG, 2])
        rstd = sb("rstd", [P, TPG])
        keysT = sb("keysT", [P, TPG, BPT * KEYS])
        variance = sb("variance", [P, TPG])
        zeros = sb("zeros", [P, D])
        ew1 = sb("ew1", [P, E0 * F0])
        ew2 = sb("ew2", [P, E0 * 2 * D])

        def C(name):
            at, w = CONST[name]
            return const[:, at:at + w]

        def W(name):
            at, w = SMALL[name]
            return small[:, at:at + w]

        def x_tile(i, t):
            return X[:, bass.ds(i * GT + t * D, D)]

        def x_group(i):
            return X[:, bass.ds(i * GT, GT)].rearrange("p (t d) -> p t d", t=TPG)

        loaded = sem("loaded")
        x_first = sem("x_first")
        x_loaded = sem("x_loaded")
        weights_loaded = sem("weights_loaded")
        first_keys_loaded = sem("first_keys_loaded")
        x_out = sem("x_out")
        zeros_ready = sem("zeros_ready")
        places_cleared = sem("places_cleared")

        norms = [0]
        stage_sems = []

        def stage_sem(name):
            stage_sems.append(nc.alloc_semaphore(name))
            return stage_sems[-1]

        moments_ready = sem("moments_ready")
        variance_ready = sem("variance_ready")
        rstd_ready = sem("rstd_ready")

        def wait_alone(eng, s, value):
            eng.wait_ge(s, value)
            eng.nop(nofuse=True)

        def layernorm_moments(dve, steps, source):
            for t in range(TPG):
                steps.did(nc.vector.bn_stats(out=stats[:, t, :], in_=source(t)))
            for t in range(TPG):
                if t == 0:
                    steps.settle()
                    dve.nop(nofuse=True)
                ins = nc.vector.bn_aggr(out=moments[:, t, :], in_=stats[:, t, :])
                if t < TPG - 1:
                    steps.did(ins)
            ins.then_inc(moments_ready, 1)

        def layernorm_output(dve, n, source, target, target_free, done):
            dve.wait_ge(rstd_ready, n + 1)
            target_free()
            for t in range(TPG):
                nc.vector.tensor_scalar(target(t), source(t), moments[:, t, 0:1], rstd[:, t:t + 1],
                                        ALU.subtract, ALU.mult).then_inc(done, 1)

        def layernorm(dve, steps, n, source, target, target_free, done):
            layernorm_moments(dve, steps, source)
            layernorm_output(dve, n, source, target, target_free, done)

        def layernorm_rstd(pool, n, eps):
            wait_alone(pool, moments_ready, n + 1)
            nc.gpsimd.tensor_scalar(variance[:, :], moments[:, :, 1], eps, None, ALU.add).then_inc(variance_ready, 1)
            pool.wait_ge(variance_ready, n + 1)
            nc.gpsimd.tensor_tensor(rstd[:, :], variance[:, :], C("minushalf"), ALU.pow).then_inc(rstd_ready, 1)

        attention_buffers = ExitStack()

        def shared(name, shape, dt=F32):
            return attention_buffers.enter_context(nc.sbuf_tensor(name, shape, dt))

        QX = shared("QX", [P, 2, TPG * BPT, Q4, SEQ])
        KX = shared("KX", [P, 2, TPG * BPT, H4, SEQ])
        VX = shared("VX", [P, 2, TPG * BPT, Q4, VW])
        V = shared("V", [P, TPG * BPT, Q4, DH])
        qT = shared("qT", [P, GT])
        kT = shared("kT", [P, GT])
        spare = shared("spare", [P, GT])
        spare2 = shared("spare2", [P, GT])
        S = shared("S", [P, 2, GT])
        ST = shared("ST", [P, 2, GT])
        top16 = shared("top16", [P, TPG, HEADS])
        rsum16 = shared("rsum16", [P, TPG, HEADS])
        O = shared("O", [P, TPG, D])
        OT = shared("OT", [P, GT])
        maskneg16 = shared("maskneg16", [P, SEQ], BF16)
        spread16 = shared("spread16", [P, P], BF16)
        eps16 = 1e-6

        def batch_of(ap, t, b):
            return ap[:, t * BPT + b, :, :].rearrange("p g s -> p (g s)")

        def by_batch(ap):
            return ap.rearrange("p (b s) -> p b s", s=SEQ)

        def turns(eng, front, turn, last):
            front(0)
            turn(0, 0, True, True)
            with eng.Fori(0, (GROUPS - 4) // 2) as i:
                turn(2 * i + 1, 1, True, True)
                turn(2 * i + 2, 0, True, True)
            turn(GROUPS - 3, 1, True, True)
            turn(GROUPS - 2, 0, True, False)
            turn(GROUPS - 1, 1, False, False)
            last(GROUPS)

        class Output:

            def __init__(self, sem):
                self.o_ready = sem("o_ready")
                self.OT_ready = sem("OT_ready")
                self.OT_copied = sem("OT_copied")
                self.y_ready = sem("y_ready")
                self.x_done = sem("x_done")

            def pe_OT(self, pe, g):
                pe.wait_ge(self.o_ready, TPG * g)
                for t in range(TPG):
                    mm = nc.tensor.transpose(bank[7][:, t * P:(t + 1) * P], O[:, t, :], C("ident"))
                mm.then_inc(self.OT_ready, 1)

            def act_copy_OT(self, act, g):
                act.wait_ge(self.OT_ready, g)
                nc.scalar.copy(OT[:, :], bank[7][:, :]).then_inc(self.OT_copied, 1)

            def pe_y(self, pe, g, w):
                pe.wait_ge(self.OT_copied, g)
                for t in range(TPG):
                    mm = nc.tensor.matmul(bank[7][:, t * D:(t + 1) * D], OT[:, t * P:(t + 1) * P], w, start=True, stop=True)
                mm.then_inc(self.y_ready, 1)

            def dve_add(self, dve, g, bias_added=None):
                dve.wait_ge(self.y_ready, g)
                if bias_added is not None:
                    dve.wait_ge(bias_added, g)
                nc.vector.tensor_tensor(x_group(g - 1), x_group(g - 1), bank[7][:, :].rearrange("p (t d) -> p t d", d=D), ALU.add
                                        ).then_inc(self.x_done, 1)

        class Attention(Output):

            def __init__(self, sem, softmax, causal, values):
                self.softmax, self.causal, self.values = softmax, causal, values
                self.logits_ready = [sem(f"logits_ready{k}") for k in range(2)]
                self.logits_used = [sem(f"logits_used{k}") for k in range(2)]
                self.exp_done = sem("exp_done")
                self.ST_ready = [sem(f"ST_ready{k}") for k in range(2)]
                self.ST_copied = [sem(f"ST_copied{k}") for k in range(2)]
                self.pv_ready = sem("pv_ready")
                Output.__init__(self, sem)
                self.steps = sem("back_steps")
                self.per = TPG * 2


            def pe_logits(self, pe, g, s, t):
                k, out_ = t % 2, bank[3 + t % 2]
                pe.wait_ge(self.logits_used[k], 2 * g + t // 2)
                if self.softmax:
                    if self.causal:
                        nc.tensor.matmul(out_[:, :], spread16[0:SEQ, :],
                                         maskneg16[0:SEQ, :].unsqueeze(1).to_broadcast([SEQ, HEADS, SEQ]),
                                         start=True, stop=True, skip_group_check=True)
                    for b in range(BPT):
                        mm = nc.tensor.matmul(out_[:, b * P:(b + 1) * P], batch_of(QX[:, s], t, b), batch_of(KX[:, s], t, b),
                                              start=not self.causal, stop=True, skip_group_check=True)
                else:
                    for b in range(BPT):
                        mm = nc.tensor.matmul(out_[:, b * P:(b + 1) * P], batch_of(KX[:, s], t, b), batch_of(QX[:, s], t, b),
                                              start=True, stop=True)
                mm.then_inc(self.logits_ready[k], 1)

            def dve_weigh(self, dve, steps, g, t):
                k, in_ = t % 2, bank[3 + t % 2]
                dve.wait_ge(self.logits_ready[k], 2 * g + t // 2 + 1)
                if self.softmax:
                    view = in_[:, :].rearrange("p (h m) -> p h m", m=SEQ)
                    steps.did(nc.vector.reduce_max(top16[:, t, :], view, AX_X))
                    steps.settle()
                    dve.wait_ge(self.ST_ready[k], 2 * g + t // 2)
                    nc.vector.tensor_tensor(S[:, k, :].rearrange("p (h m) -> p h m", m=SEQ), view,
                                            top16[:, t, :].unsqueeze(2).to_broadcast([P, HEADS, SEQ]), ALU.subtract
                                            ).then_inc(self.logits_used[k], 1)
                else:
                    if t >= 2 or not is_first(g):
                        dve.wait_ge(self.pv_ready, TPG * g + t - 1)
                    nc.vector.tensor_tensor(ST[:, k, :].rearrange("p (g l) -> p g l", l=SEQ),
                                            in_[:, :].rearrange("p (g l) -> p g l", l=SEQ),
                                            C("causal").unsqueeze(1).to_broadcast([P, HEADS, SEQ]), ALU.mult
                                            ).then_inc(self.logits_used[k], 1)

            def act_exp(self, act, g, t):
                k = t % 2
                act.wait_ge(self.logits_used[k], 2 * g + t // 2 + 1)
                nc.scalar.activation(S[:, k, :], S[:, k, :], ACT.Exp).then_inc(self.exp_done, 1)

            def pe_transpose(self, pe, g, t):
                k, out_ = t % 2, bank[5 + t % 2]
                pe.wait_ge(self.exp_done, TPG * g + t + 1)
                pe.wait_ge(self.ST_copied[k], 2 * g + t // 2)
                for b in range(BPT):
                    mm = nc.tensor.transpose(out_[:, b * P:(b + 1) * P], S[:, k, b * P:(b + 1) * P], C("ident"))
                mm.then_inc(self.ST_ready[k], 1)

            def act_copy_ST(self, act, g, t):
                k = t % 2
                act.wait_ge(self.ST_ready[k], 2 * g + t // 2 + 1)
                if t >= 2 or not is_first(g):
                    act.wait_ge(self.pv_ready, TPG * g + t - 1)
                nc.scalar.copy(ST[:, k, :], bank[5 + k][:, :]).then_inc(self.ST_copied[k], 1)

            def pe_values(self, pe, g, s, t):
                k = t % 2
                if self.softmax:
                    pe.wait_ge(self.ST_copied[k], 2 * g + t // 2 + 1)
                else:
                    pe.wait_ge(self.logits_used[k], 2 * g + t // 2 + 1)
                pe.wait_ge(self.o_ready, TPG * g + t)
                if t == 0:
                    pe.wait_ge(self.x_done, g)
                for q in range(Q4):
                    for b in range(BPT):
                        at = b * P + q * SEQ
                        mm = nc.tensor.matmul(bank[7][b * SEQ:(b + 1) * SEQ, q * VW:(q + 1) * VW], ST[:, k, at:at + SEQ],
                                              self.values(s, t * BPT + b, q), start=True, stop=True)
                mm.then_inc(self.pv_ready, 1)

            def dve_normalise(self, dve, steps, g, t):
                pv = bank[7][:, 0:Q4 * VW].rearrange("p (q w) -> p q w", w=VW)
                dve.wait_ge(self.pv_ready, TPG * g + t + 1)
                if t == 0:
                    dve.wait_ge(self.OT_ready, g)
                rsum = rsum16[:, t, :].rearrange("p (q h) -> p q h", h=H4)
                if self.softmax:
                    steps.did(nc.vector.reciprocal(rsum, pv[:, :, QW:VW]))
                else:
                    steps.did(nc.vector.tensor_scalar(rsum, pv[:, :, QW:VW], eps16, None, ALU.add))
                    steps.settle()
                    steps.did(nc.vector.reciprocal(rsum, rsum))
                steps.settle()
                nc.vector.tensor_tensor(O[:, t, :].rearrange("p (q h d) -> p q h d", q=Q4, h=H4),
                                        pv[:, :, 0:QW].rearrange("p q (h d) -> p q h d", d=DH),
                                        rsum.unsqueeze(3).to_broadcast([P, Q4, H4, DH]), ALU.mult).then_inc(self.o_ready, 1)

        def is_first(g):
            return isinstance(g, int) and g == 0

        def pe_zT(pe, g, z_ready, bank_read, zT_ready, z=Z):
            pe.wait_ge(z_ready, TPG * g + TPG)
            pe.wait_ge(bank_read, g)
            for t in range(TPG):
                mm = nc.tensor.transpose(bank[0][:, t * P:(t + 1) * P], z[:, t, :], C("ident"))
            mm.then_inc(zT_ready, 1)

        def pe_values_of_batches(z, w, width):
            for b in range(TPG * BPT):
                for h in range(H4):
                    at = h * QW if width == QW else 0
                    mm = nc.tensor.matmul(bank[1][h * SEQ:(h + 1) * SEQ, b * width:(b + 1) * width],
                                          z[:, b * SEQ:(b + 1) * SEQ], w[:, at:at + width], start=True, stop=True)
            return mm

        def spread_values(eng, s, done):
            eng.tensor_tensor(VX[:, s, :, :, 0:QW].rearrange("p b q (h d) -> p (b q) h d", d=DH),
                              V[:, :, :, :].rearrange("p b q d -> p (b q) d").unsqueeze(2).to_broadcast([P, TPG * BPT * Q4, H4, DH]),
                              C("headcol").unsqueeze(1).unsqueeze(3).to_broadcast([P, TPG * BPT * Q4, H4, DH]),
                              ALU.mult).then_inc(done, 1)

        def dve_spread_queries(s, q, scale, done):
            nc.vector.tensor_scalar(QX[:, s, :, q, :], by_batch(qT[:, :]), C("quarter4")[:, q:q + 1], scale,
                                    ALU.mult, ALU.mult).then_inc(done, 1)

        def act_spread_keys(s, source, h, done):
            nc.scalar.activation(KX[:, s, :, h, :], by_batch(source[:, :]), ACT.Copy, scale=C("head4")[:, h:h + 1]
                                 ).then_inc(done, 1)

        def block_mask(n):
            return C("headblock").unsqueeze(1).to_broadcast([P, n, QW])

        def cross_attention_0():
            norm0 = norms[0]
            norms[0] += GROUPS
            with ExitStack() as mine:
                def sb(name, shape, dt=F32):
                    return mine.enter_context(nc.sbuf_tensor("c0_" + name, shape, dt))

                def sem(name):
                    return stage_sem("c0_" + name)

                att = Output(sem)
                keysN = sb("keysN", [P, TPG, BPT, 2, D])
                lastkeys = sb("lastkeys", [1, TPG * BPT * D])
                qT2 = sb("qT2", [P, 2, GT])
                qkT = sb("qkT", [P, 2, GT])
                probs = sb("probs", [P, 2, KEYS])
                probsT = sb("probsT", [P, 2, 2, P])
                lastprobT = sb("lastprobT", [1, 2, P])
                top = sb("top", [P, TPG])
                shift = sb("shift", [P, TPG])
                total = sb("total", [P, TPG])
                rtotal = sb("rtotal", [P, TPG])

                z_ready, zT_ready, zT_copied = sem("z_ready"), sem("zT_ready"), sem("zT_copied")
                q_ready, q_copied, qk_ready, qk_copied = (sem(n) for n in ("q_ready", "q_copied", "qk_ready", "qk_copied"))
                bias_added = sem("bias_added")
                keysT_loaded = [sem(f"keysT_loaded{t}") for t in range(TPG)]
                keysN_loaded = [sem(f"keysN_loaded{t}") for t in range(TPG)]
                lastkeys_loaded = sem("lastkeys_loaded")
                scores_ready = [sem(f"scores_ready{t}") for t in range(TPG)]
                shift_ready = sem("shift_ready")
                exp_done = [sem(f"exp_done{k}") for k in range(2)]
                probsT_ready = [sem(f"probsT_ready{k}") for k in range(2)]
                probsT_copied = [sem(f"probsT_copied{k}") for k in range(2)]
                tile_attended = [sem(f"tile_attended{t}") for t in range(TPG)]
                front_steps, back_steps = sem("front_steps"), sem("back_steps")

                scores_bank, probsT_bank = [bank[2], bank[3]], [bank[4], bank[5]]

                with nc.Block() as block:
                    @block.sync
                    def _(sp):
                        def load(g):
                            if not is_first(g):
                                sp.wait_ge(tile_attended[TPG - 1], g)
                            sp.dma_start(lastkeys[:, :], a["lastkeys"][:, bass.ds(g * (GT // SEQ * D), GT // SEQ * D)]
                                         ).then_inc(lastkeys_loaded, 16)

                        def load_tile(g, t):
                            b0 = g * (TPG * BPT) + t * BPT
                            if not is_first(g):
                                sp.wait_ge(scores_ready[t], g)
                            sp.dma_start(keysT[:, t, :], a["ctxT"][:, bass.ds(b0 * KEYS, BPT * KEYS)]
                                         ).then_inc(keysT_loaded[t], 16)
                            if not is_first(g):
                                sp.wait_ge(tile_attended[t], g)
                            sp.dma_start(keysN[:, t, :, :, :].rearrange("p j c d -> p (j c d)"),
                                         a["ctxN"][:, bass.ds(b0 * (2 * D), BPT * 2 * D)]
                                         ).then_inc(keysN_loaded[t], 16)

                        for t in range(TPG):
                            load_tile(0, t)
                            if t == 0:
                                sp.dma_start(X[:, GT:], a["xt"][:, GT:]).then_inc(x_loaded, 16)
                                load(0)
                        with sp.Fori(1, GROUPS) as g:
                            for t in range(TPG):
                                load_tile(g, t)
                            load(g)
                        sp.dma_start(ew1[:, :], a["f_w1"][:, :]).then_inc(weights_loaded, 16)
                        sp.dma_start(ew2[:, :], a["f_w2"][:, :]).then_inc(weights_loaded, 16)

                    @block.tensor
                    def _(pe):
                        def query(g, s):
                            pe.wait_ge(zT_copied, g + 1)
                            pe.wait_ge(qk_copied, g)
                            nc.tensor.matmul(bank[1][:, :], W("x_wqT"), zT[:, :], start=True, stop=True).then_inc(q_ready, 1)

                        def query_key(g, s):
                            pe.wait_ge(q_copied, g + 1)
                            nc.tensor.matmul(bank[1][:, :], W("x_wk"), qT2[:, s, :], start=True, stop=True).then_inc(qk_ready, 1)

                        def scores(g, s, t):
                            b = scores_bank[t % 2]
                            if t == 0:
                                pe.wait_ge(qk_copied, g + 1)
                            pe.wait_ge(keysT_loaded[t], 16 * g + 16)
                            pe.wait_ge(exp_done[t % 2], 2 * g + t // 2)
                            for j in range(BPT):
                                at = t * P + j * SEQ
                                nc.tensor.matmul(b[j * SEQ:(j + 1) * SEQ, 0:KEYS], qkT[:, s, at:at + SEQ],
                                                 keysT[:, t, j * KEYS:(j + 1) * KEYS], start=True, stop=True)
                            nc.tensor.matmul(b[:, KEYS:KEYS + 1], qT2[:, s, t * P:(t + 1) * P], W("x_bk"),
                                             start=True, stop=True).then_inc(scores_ready[t], 1)

                        def transpose_probs(g, t):
                            b = probsT_bank[t % 2]
                            pe.wait_ge(exp_done[t % 2], 2 * g + t // 2 + 1)
                            pe.wait_ge(probsT_copied[t % 2], 2 * g + t // 2)
                            for c in range(2):
                                nc.tensor.transpose(b[:, c * P:(c + 1) * P], probs[:, t % 2, c * P:(c + 1) * P], C("ident"))
                            nc.tensor.transpose(b[0:1, 2 * P:3 * P], probs[:, t % 2, KEYS - 1:KEYS], C("ident")
                                                ).then_inc(probsT_ready[t % 2], 1)

                        def attend(g, t):
                            pe.wait_ge(probsT_copied[t % 2], 2 * g + t // 2 + 1)
                            pe.wait_ge(keysN_loaded[t], 16 * g + 16)
                            if t == 0:
                                pe.wait_ge(lastkeys_loaded, 16 * g + 16)
                            pe.wait_ge(att.o_ready, TPG * g + t)
                            for c in range(3):
                                for j in range(BPT):
                                    now = slice(j * SEQ, (j + 1) * SEQ)
                                    if c < 2:
                                        ps, ks = probsT[:, t % 2, c, now], keysN[:, t, j, c, :]
                                    else:
                                        at = (t * BPT + j) * D
                                        ps, ks = lastprobT[:, t % 2, now], lastkeys[:, at:at + D]
                                    mm = nc.tensor.matmul(bank[6][now, 0:D], ps, ks, start=(c == 0), stop=(c == 2),
                                                          skip_group_check=True)
                            mm.then_inc(tile_attended[t], 1)

                        def front(g):
                            pe_zT(pe, g, z_ready, zT_copied, zT_ready)
                            query(g, 0)
                            query_key(g, 0)

                        def turn(g, s, more, ahead):
                            scores(g, s, 0)
                            scores(g, s, 1)
                            if not is_first(g):
                                att.pe_OT(pe, g)
                            if more:
                                pe_zT(pe, g + 1, z_ready, zT_copied, zT_ready)
                            transpose_probs(g, 0)
                            scores(g, s, 2)
                            if more:
                                query(g + 1, 1 - s)
                            if not is_first(g):
                                att.pe_y(pe, g, W("x_wvT"))
                            transpose_probs(g, 1)
                            attend(g, 0)
                            if more:
                                query_key(g + 1, 1 - s)
                            scores(g, s, 3)
                            attend(g, 1)
                            transpose_probs(g, 2)
                            transpose_probs(g, 3)
                            attend(g, 2)
                            attend(g, 3)
                            if not is_first(g):
                                pe.wait_ge(att.x_done, g)

                        def last(g):
                            att.pe_OT(pe, g)
                            att.pe_y(pe, g, W("x_wvT"))

                        pe.wait_ge(loaded, LOADS)
                        turns(pe, front, turn, last)

                    @block.scalar
                    def _(act):
                        def copy_zT(g):
                            act.wait_ge(zT_ready, g + 1)
                            act.wait_ge(q_ready, g)
                            nc.scalar.copy(zT[:, :], bank[0][:, :]).then_inc(zT_copied, 1)

                        def copy_q(g, s):
                            act.wait_ge(q_ready, g + 1)
                            if not is_first(g):
                                act.wait_ge(scores_ready[TPG - 1], g - 1)
                            nc.scalar.activation(qT2[:, s, :], bank[1][:, :], ACT.Identity, bias=W("x_bq")).then_inc(q_copied, 1)

                        def copy_qk(g, s):
                            act.wait_ge(qk_ready, g + 1)
                            nc.scalar.copy(qkT[:, s, :], bank[1][:, :]).then_inc(qk_copied, 1)

                        def exponential(g, t):
                            act.wait_ge(shift_ready, TPG * g + t + 1)
                            act.wait_ge(probsT_ready[t % 2], 2 * g + t // 2)
                            nc.scalar.activation(probs[:, t % 2, :], scores_bank[t % 2][:, 0:KEYS], ACT.Exp,
                                                 bias=shift[:, t:t + 1], accum_out=total[:, t:t + 1]
                                                 ).then_inc(exp_done[t % 2], 1)

                        def copy_probsT(g, t):
                            act.wait_ge(probsT_ready[t % 2], 2 * g + t // 2 + 1)
                            if t >= 2:
                                act.wait_ge(tile_attended[t - 2], g + 1)
                            elif not is_first(g):
                                act.wait_ge(tile_attended[t + 2], g)
                            nc.scalar.copy(lastprobT[:, t % 2, :], probsT_bank[t % 2][0:1, 2 * P:3 * P])
                            nc.scalar.copy(probsT[:, t % 2, :, :],
                                           probsT_bank[t % 2][:, 0:2 * P].rearrange("p (c k) -> p c k", c=2)
                                           ).then_inc(probsT_copied[t % 2], 1)

                        def front(g):
                            copy_zT(g)
                            copy_q(g, 0)
                            copy_qk(g, 0)

                        def turn(g, s, more, ahead):
                            exponential(g, 0)
                            if more:
                                copy_zT(g + 1)
                            exponential(g, 1)
                            if not is_first(g):
                                att.act_copy_OT(act, g)
                            copy_probsT(g, 0)
                            exponential(g, 2)
                            copy_probsT(g, 1)
                            if more:
                                copy_q(g + 1, 1 - s)
                            exponential(g, 3)
                            if more:
                                copy_qk(g + 1, 1 - s)
                            copy_probsT(g, 2)
                            copy_probsT(g, 3)

                        act.wait_ge(loaded, LOADS)
                        turns(act, front, turn, lambda g: att.act_copy_OT(act, g))

                    @block.vector
                    def _(dve):
                        fsteps = Steps(dve, front_steps, 7)
                        bsteps = Steps(dve, back_steps, 2 * TPG)

                        def moments_of_x(g):
                            fsteps.start(g)
                            layernorm_moments(dve, fsteps, lambda t: x_tile(g, t))
                            fsteps.end()

                        def normalise_x(g):
                            layernorm_output(dve, norm0 + g, lambda t: x_tile(g, t), lambda t: Z[:, t, :],
                                             lambda: dve.wait_ge(zT_ready, g), z_ready)

                        def find_shift(g, t):
                            b = scores_bank[t % 2]
                            dve.wait_ge(scores_ready[t], g + 1)
                            bsteps.did(nc.vector.reduce_max(top[:, t:t + 1], b[:, 0:KEYS], AX_X))
                            bsteps.settle()
                            nc.vector.scalar_tensor_tensor(
                                out=shift[:, t:t + 1], in0=top[:, t:t + 1], scalar=b[:, KEYS:KEYS + 1],
                                in1=b[:, KEYS:KEYS + 1], op0=ALU.add, op1=ALU.subtract, reverse1=True
                            ).then_inc(shift_ready, 1)

                        def normalise(g, t):
                            dve.wait_ge(tile_attended[t], g + 1)
                            dve.wait_ge(exp_done[t % 2], 2 * g + t // 2 + 1)
                            if t == 0:
                                dve.wait_ge(att.OT_ready, g)
                            bsteps.did(nc.vector.reciprocal(rtotal[:, t:t + 1], total[:, t:t + 1]))
                            bsteps.settle()
                            nc.vector.tensor_scalar(O[:, t, :], bank[6][:, 0:D], rtotal[:, t:t + 1], None, ALU.mult
                                                    ).then_inc(att.o_ready, 1)

                        def turn(g, s, more, ahead):
                            bsteps.start(g)
                            find_shift(g, 0)
                            find_shift(g, 1)
                            if ahead:
                                moments_of_x(g + 2)
                            find_shift(g, 2)
                            if not is_first(g):
                                att.dve_add(dve, g, bias_added)
                            normalise(g, 0)
                            find_shift(g, 3)
                            if ahead:
                                normalise_x(g + 2)
                            normalise(g, 1)
                            normalise(g, 2)
                            normalise(g, 3)
                            bsteps.end()

                        dve.wait_ge(x_first, 16)
                        dve.wait_ge(loaded, LOADS)
                        moments_of_x(0)
                        normalise_x(0)
                        for s in range(2):
                            nc.vector.tensor_copy(VX[:, s, :, :, QW:VW].rearrange("p b q w -> p (b q) w"),
                                                  C("headcol").unsqueeze(1).to_broadcast([P, TPG * BPT * Q4, H4]))
                        dve.wait_ge(x_loaded, 16)
                        moments_of_x(1)
                        normalise_x(1)
                        turns(dve, lambda g: None, turn, lambda g: att.dve_add(dve, g, bias_added))

                    @block.gpsimd
                    def _(pool):
                        def front(g):
                            layernorm_rstd(pool, norm0 + g, 1e-5)
                            pool.wait_ge(z_ready, TPG * g + TPG)
                            nc.gpsimd.tensor_tensor(x_group(g), x_group(g), W("x_bv").unsqueeze(1).to_broadcast([P, TPG, D]),
                                                    ALU.add).then_inc(bias_added, 1)

                        pool.wait_ge(loaded, LOADS)
                        front(0)
                        turns(pool, lambda g: front(1), lambda g, s, more, ahead: front(g + 2) if ahead else None, lambda g: None)

        def linear_attention():
            norm0 = norms[0]
            norms[0] += GROUPS
            with ExitStack() as mine:
                def sem(name):
                    return stage_sem("l0_" + name)

                att = Attention(sem, softmax=False, causal=True, values=lambda s, b, q: VX[:, s, b, q, :])
                z_ready, zT_ready, zT_copied = (sem(n) for n in ("z_ready", "zT_ready", "zT_copied"))
                v_ready, v_copied = sem("v_ready"), sem("v_copied")
                proj_ready = [sem(f"proj_ready{k}") for k in range(2)]
                proj_used = [sem(f"proj_used{k}") for k in range(2)]
                below_ready, exp_ready, qT_ready, kT_ready = (sem(n) for n in (
                    "below_ready", "exp_ready", "qT_ready", "kT_ready"))
                KX_ready, VX_ready, QX_ready = sem("KX_ready"), sem("VX_ready"), sem("QX_ready")
                front_steps = sem("front_steps")
                bias_added = sem("bias_added")

                with nc.Block() as block:
                    @block.tensor
                    def _(pe):
                        def project(g):
                            pe.wait_ge(zT_copied, g + 1)
                            for k in range(2):
                                if k == 0:
                                    pe.wait_ge(v_copied, g)
                                else:
                                    pe.wait_ge(proj_used[k], g)
                                nc.tensor.matmul(bank[1 + k][:, :], W("a_w")[:, k * D:(k + 1) * D], zT[:, :],
                                                 start=True, stop=True).then_inc(proj_ready[k], 1)

                        def values(g):
                            pe.wait_ge(proj_used[0], g + 1)
                            pe_values_of_batches(zT, W("a_wv"), QW).then_inc(v_ready, 1)

                        def front(g):
                            pe_zT(pe, g, z_ready, zT_copied, zT_ready)
                            project(g)
                            values(g)

                        def turn(g, s, more, ahead):
                            pe.wait_ge(QX_ready, Q4 * g + Q4)
                            pe.wait_ge(KX_ready, H4 * g + H4)
                            att.pe_logits(pe, g, s, 0)
                            if not is_first(g):
                                att.pe_OT(pe, g)
                            att.pe_logits(pe, g, s, 1)
                            if more:
                                pe_zT(pe, g + 1, z_ready, zT_copied, zT_ready)
                            if not is_first(g):
                                att.pe_y(pe, g, W("a_wo"))
                            if more:
                                project(g + 1)
                            pe.wait_ge(VX_ready, g + 1)
                            for t in range(TPG):
                                att.pe_values(pe, g, s, t)
                                if t + 2 < TPG:
                                    att.pe_logits(pe, g, s, t + 2)
                                if more and t == 0:
                                    values(g + 1)

                        def last(g):
                            att.pe_OT(pe, g)
                            att.pe_y(pe, g, W("a_wo"))

                        turns(pe, front, turn, last)

                    @block.scalar
                    def _(act):
                        def front_1(g):
                            act.wait_ge(zT_ready, g + 1)
                            act.wait_ge(v_ready, g)
                            nc.scalar.copy(zT[:, :], bank[0][:, :]).then_inc(zT_copied, 1)

                        def front_2(g):
                            act.wait_ge(proj_ready[0], g + 1)
                            act.wait_ge(QX_ready, Q4 * g)
                            nc.scalar.activation(qT[:, :], bank[1][:, :], ACT.Identity, bias=W("a_bq")).then_inc(proj_used[0], 1)
                            act.wait_ge(proj_ready[1], g + 1)
                            act.wait_ge(KX_ready, H4 * g)
                            nc.scalar.activation(kT[:, :], bank[2][:, :], ACT.Identity, bias=W("a_bk")).then_inc(proj_used[1], 1)

                        def front_3(g):
                            act.wait_ge(below_ready, 2 * g + 1)
                            nc.scalar.activation(spare[:, :], spare[:, :], ACT.Exp).then_inc(exp_ready, 1)
                            act.wait_ge(below_ready, 2 * g + 2)
                            nc.scalar.activation(spare2[:, :], spare2[:, :], ACT.Exp).then_inc(exp_ready, 1)

                        def front_4(g, s):
                            act.wait_ge(kT_ready, g + 1)
                            if not is_first(g):
                                act.wait_ge(att.OT_ready, g - 1)
                            for h in range(H4):
                                act_spread_keys(s, kT, h, KX_ready)

                        def front(g, s=0):
                            front_1(g)
                            front_2(g)
                            front_3(g)
                            front_4(g, s)

                        def turn(g, s, more, ahead):
                            if not is_first(g):
                                att.act_copy_OT(act, g)
                            if more:
                                front(g + 1, 1 - s)

                        turns(act, front, turn, lambda g: att.act_copy_OT(act, g))

                    @block.vector
                    def _(dve):
                        fsteps = Steps(dve, front_steps, 7)
                        bsteps = Steps(dve, att.steps, att.per)
                        def front_1(g):
                            fsteps.start(g)
                            layernorm(dve, fsteps, norm0 + g, lambda t: x_tile(g, t), lambda t: Z[:, t, :],
                                      lambda: dve.wait_ge(zT_ready, g), z_ready)
                            fsteps.end()

                        def front_2(g, s):
                            for k, (x_, low) in enumerate(((qT, spare), (kT, spare2))):
                                dve.wait_ge(proj_used[k], g + 1)
                                nc.vector.tensor_scalar(low[:, :], x_[:, :], 0.0, None, ALU.min).then_inc(below_ready, 1)

                        def front_3(g, s):
                            for k, (x_, low, done) in enumerate(((qT, spare, qT_ready), (kT, spare2, kT_ready))):
                                dve.wait_ge(exp_ready, 2 * g + k + 1)
                                nc.vector.scalar_tensor_tensor(out=x_[:, :], in0=x_[:, :], scalar=0.0, in1=low[:, :],
                                                               op0=ALU.max, op1=ALU.add).then_inc(done, 1)
                            dve.wait_ge(qT_ready, g + 1)
                            if not is_first(g):
                                dve.wait_ge(att.OT_ready, g - 1)
                            for q in range(Q4):
                                dve_spread_queries(s, q, 1.0, QX_ready)

                        def front_4(g):
                            dve.wait_ge(v_ready, g + 1)
                            dve.wait_ge(VX_ready, g)
                            nc.vector.tensor_tensor(V[:, :, :, :].rearrange("p b q d -> p b (q d)"),
                                                    bank[1][:, :].rearrange("p (b w) -> p b w", w=QW),
                                                    W("a_bvh").unsqueeze(1).to_broadcast([P, TPG * BPT, QW]), ALU.add
                                                    ).then_inc(v_copied, 1)

                        def front(g):
                            front_1(g)
                            front_2(g, 0)
                            front_3(g, 0)
                            front_4(g)

                        def turn(g, s, more, ahead):
                            if more:
                                front_1(g + 1)
                            bsteps.start(g)
                            att.dve_weigh(dve, bsteps, g, 0)
                            att.dve_weigh(dve, bsteps, g, 1)
                            if not is_first(g):
                                att.dve_add(dve, g, bias_added)
                            if more:
                                front_2(g + 1, 1 - s)
                            for t in range(TPG):
                                att.dve_normalise(dve, bsteps, g, t)
                                if t + 2 < TPG:
                                    att.dve_weigh(dve, bsteps, g, t + 2)
                                if more and t == 0:
                                    front_3(g + 1, 1 - s)
                                if more and t == 1:
                                    front_4(g + 1)
                            bsteps.end()

                        turns(dve, front, turn, lambda g: att.dve_add(dve, g, bias_added))

                    @block.gpsimd
                    def _(pool):
                        def front(g, s=0):
                            layernorm_rstd(pool, norm0 + g, 1e-5)
                            pool.wait_ge(z_ready, TPG * g + TPG)
                            nc.gpsimd.tensor_tensor(x_group(g), x_group(g), W("a_bo").unsqueeze(1).to_broadcast([P, TPG, D]),
                                                    ALU.add).then_inc(bias_added, 1)
                            if not is_first(g):
                                pool.wait_ge(att.OT_ready, g - 1)
                            pool.wait_ge(v_copied, g + 1)
                            spread_values(nc.gpsimd, s, VX_ready)

                        turns(pool, front, lambda g, s, more, ahead: front(g + 1, 1 - s) if more else None, lambda g: None)

        def experts_0():
            norm0 = norms[0]
            norms[0] += 2 * GROUPS
            with ExitStack() as mine:
                def sb(name, shape, dt=F32):
                    return mine.enter_context(nc.sbuf_tensor("f0_" + name, shape, dt))

                def sem(name):
                    return stage_sem("f0_" + name)

                Z2 = sb("Z2", [P, TPG, D])
                zT2 = sb("zT2", [P, 2, GT])
                hidden = sb("hidden", [P, 4, 2, GT])
                prob = sb("prob", [P, TPG, E0])
                left = sb("left", [P, TPG, E0])
                hit = sb("hit", [P, TPG, E0])
                first = sb("first", [P, TPG, E0])
                second = sb("second", [P, TPG, E0])
                share = sb("share", [P, 2, TPG, E0])
                shareT = sb("shareT", [E0, GT])
                one = sb("one", [P, TPG])

                z_ready, z2_ready, zT_ready, zT_copied = sem("z_ready"), sem("z2_ready"), sem("zT_ready"), sem("zT_copied")
                residual_added = sem("residual_added")
                route_ready, low_ready, exp_done = sem("route_ready"), sem("low_ready"), sem("exp_done")
                share_ready, shareT_ready, shareT_copied = sem("share_ready"), sem("shareT_ready"), sem("shareT_copied")
                bias_ready, bias_used = sem("bias_ready"), sem("bias_used")
                up_ready = [sem(f"up_ready{f}") for f in range(2)]
                gelu_done = [sem(f"gelu_done{f}") for f in range(2)]
                down_ready = [sem(f"down_ready{k}") for k in range(2)]
                down_used = [sem(f"down_used{k}") for k in range(2)]
                front_steps = sem("front_steps")

                def spread8(v):
                    return v.unsqueeze(2).to_broadcast([P, TPG, E0])


                with nc.Block() as block:
                    @block.sync
                    def _(sp):
                        sp.wait_ge(zeros_ready, 1)
                        sp.dma_start(a["rowspace"][0:E1 * CAP, :].rearrange("(p r) d -> p r d", p=P),
                                     zeros[:, :].unsqueeze(1).to_broadcast([P, E1 * CAP // P, D])).then_inc(places_cleared, 16)
                        for t in range(TPG):
                            sp.dma_start(keysT[:, t, :], a["ctxT"][:, t * (BPT * KEYS):(t + 1) * (BPT * KEYS)]
                                         ).then_inc(first_keys_loaded, 16)
                        sp.wait_ge(places_cleared, 16)

                    @block.tensor
                    def _(pe):
                        def route(g, s):
                            pe.wait_ge(zT_copied, g + 1)
                            pe.wait_ge(bias_used, g)
                            for t in range(TPG):
                                mm = nc.tensor.matmul(bank[1][:, t * E0:(t + 1) * E0], zT2[:, s, t * P:(t + 1) * P], W("f_rw"),
                                                      start=True, stop=True)
                            mm.then_inc(route_ready, 1)

                        def transpose_shares(g, s):
                            pe.wait_ge(share_ready, g + 1)
                            for t in range(TPG):
                                mm = nc.tensor.transpose(bank[1][0:E0, t * P:(t + 1) * P], share[:, s, t, :], C("ident"))
                            mm.then_inc(shareT_ready, 1)

                        def bias(g):
                            pe.wait_ge(shareT_copied, g + 1)
                            for t in range(TPG):
                                mm = nc.tensor.matmul(bank[1][:, t * D:(t + 1) * D], shareT[:, t * P:(t + 1) * P],
                                                      W("f_b2")[0:E0, :], start=True, stop=True)
                            mm.then_inc(bias_ready, 1)

                        def up(g, s, e):
                            if e == 0:
                                pe.wait_ge(zT_copied, g + 1)
                            for f in range(2):
                                if e >= 2 or not is_first(g):
                                    pe.wait_ge(gelu_done[f], E0 * g + e - 1)
                                at = e * F0 + f * P
                                nc.tensor.matmul(bank[2 + 2 * (e % 2) + f][:, :], ew1[:, at:at + P], zT2[:, s, :],
                                                 start=True, stop=True).then_inc(up_ready[f], 1)

                        def down(g, e):
                            k = e % 2
                            for f in range(2):
                                pe.wait_ge(gelu_done[f], E0 * g + e + 1)
                            pe.wait_ge(down_used[k], E0 // 2 * g + e // 2)
                            for t in range(TPG):
                                for f in range(2):
                                    at = (2 * e + f) * D
                                    mm = nc.tensor.matmul(bank[6 + k][:, t * D:(t + 1) * D],
                                                          hidden[:, e % 4, f, t * P:(t + 1) * P], ew2[:, at:at + D],
                                                          start=(f == 0), stop=(f == 1))
                            mm.then_inc(down_ready[k], 1)

                        def front(g):
                            pe_zT(pe, g, z2_ready, zT_copied, zT_ready, Z2)
                            route(g, 0)
                            pe.wait_ge(weights_loaded, 32)
                            up(g, 0, 0)
                            up(g, 0, 1)
                            transpose_shares(g, 0)
                            bias(g)

                        def turn(g, s, more, ahead):
                            for e in range(E0):
                                if e + 2 < E0:
                                    up(g, s, e + 2)
                                elif more:
                                    up(g + 1, 1 - s, e + 2 - E0)
                                down(g, e)
                                if more:
                                    if e == 2:
                                        pe_zT(pe, g + 1, z2_ready, zT_copied, zT_ready, Z2)
                                    if e == 3:
                                        route(g + 1, 1 - s)
                                    if e == 6:
                                        transpose_shares(g + 1, 1 - s)
                                    if e == 7:
                                        bias(g + 1)

                        turns(pe, front, turn, lambda g: None)

                    @block.scalar
                    def _(act):
                        def copy_zT(g, s):
                            act.wait_ge(zT_ready, g + 1)
                            if not is_first(g):
                                act.wait_ge(up_ready[1], E0 * (g - 1))
                            nc.scalar.activation(zT2[:, s, :], bank[0][:, :], ACT.Identity, bias=W("f_b"), scale=W("f_g")
                                                 ).then_inc(zT_copied, 1)

                        def exponential(g):
                            act.wait_ge(low_ready, g + 1)
                            nc.scalar.activation(prob[:, :, :], prob[:, :, :], ACT.Exp).then_inc(exp_done, 1)

                        def copy_shareT(g):
                            act.wait_ge(shareT_ready, g + 1)
                            act.wait_ge(bias_ready, g)
                            nc.scalar.copy(shareT[:, :], bank[1][0:E0, :]).then_inc(shareT_copied, 1)

                        def gelu(g, e):
                            for f in range(2):
                                act.wait_ge(up_ready[f], E0 * g + e + 1)
                                if e >= 4 or not is_first(g):
                                    act.wait_ge(down_ready[e % 2], E0 // 2 * g + e // 2 - 1)
                                nc.scalar.activation(hidden[:, e % 4, f, :], bank[2 + 2 * (e % 2) + f][:, :], ACT.Gelu,
                                                     bias=W("f_b1")[:, 2 * e + f:2 * e + f + 1]).then_inc(gelu_done[f], 1)

                        def front(g):
                            copy_zT(g, 0)
                            exponential(g)
                            copy_shareT(g)

                        def turn(g, s, more, ahead):
                            for e in range(E0):
                                gelu(g, e)
                                if more:
                                    if e == 4:
                                        copy_zT(g + 1, 1 - s)
                                    if e == 6:
                                        exponential(g + 1)
                            if more:
                                copy_shareT(g + 1)

                        turns(act, front, turn, lambda g: None)

                    @block.vector
                    def _(dve):
                        steps = Steps(dve, front_steps, 14 + 2 + 3 + 10 + 1 + 5)

                        def do(ins):
                            steps.did(ins)
                            steps.settle()

                        def pick(values, to):
                            do(nc.vector.reduce_max(one[:, :], values[:, :, :], AX_X))
                            do(nc.vector.tensor_tensor(hit[:, :, :], values[:, :, :], spread8(one[:, :]), ALU.is_equal))
                            do(nc.vector.tensor_tensor(hit[:, :, :], hit[:, :, :],
                                                       C("rank8").unsqueeze(1).to_broadcast([P, TPG, E0]), ALU.mult))
                            do(nc.vector.reduce_max(one[:, :], hit[:, :, :], AX_X))
                            do(nc.vector.tensor_tensor(to[:, :, :], hit[:, :, :], spread8(one[:, :]), ALU.is_equal))

                        def layernorm_1(g):
                            steps.start(g)
                            layernorm(dve, steps, norm0 + 2 * g, lambda t: x_tile(g, t), lambda t: Z[:, t, :],
                                      lambda: dve.wait_ge(residual_added, g), z_ready)

                        def layernorm_2(g):
                            dve.wait_ge(z_ready, TPG * g + TPG)
                            layernorm(dve, steps, norm0 + 2 * g + 1, lambda t: Z[:, t, :], lambda t: Z2[:, t, :],
                                      lambda: dve.wait_ge(zT_ready, g), z2_ready)

                        def logits_less_peak(g):
                            dve.wait_ge(route_ready, g + 1)
                            do(nc.vector.tensor_tensor(prob[:, :, :], bank[1][:, 0:TPG * E0].rearrange("p (t e) -> p t e", e=E0),
                                                       W("f_rb").unsqueeze(1).to_broadcast([P, TPG, E0]), ALU.add))
                            do(nc.vector.reduce_max(one[:, :], prob[:, :, :], AX_X))
                            nc.vector.tensor_tensor(prob[:, :, :], prob[:, :, :], spread8(one[:, :]), ALU.subtract
                                                    ).then_inc(low_ready, 1)

                        def shares(g, s):
                            dve.wait_ge(exp_done, g + 1)
                            do(nc.vector.reduce_sum(one[:, :], prob[:, :, :], AX_X))
                            do(nc.vector.reciprocal(one[:, :], one[:, :]))
                            do(nc.vector.tensor_tensor(prob[:, :, :], prob[:, :, :], spread8(one[:, :]), ALU.mult))
                            pick(prob, first)
                            do(nc.vector.scalar_tensor_tensor(out=left[:, :, :], in0=first[:, :, :], scalar=-2.0,
                                                              in1=prob[:, :, :], op0=ALU.mult, op1=ALU.add))
                            pick(left, second)
                            do(nc.vector.tensor_tensor(first[:, :, :], first[:, :, :], second[:, :, :], ALU.add))
                            do(nc.vector.tensor_tensor(first[:, :, :], first[:, :, :], prob[:, :, :], ALU.mult))
                            do(nc.vector.reduce_sum(one[:, :], first[:, :, :], AX_X))
                            do(nc.vector.tensor_scalar(one[:, :], one[:, :], 1e-8, None, ALU.max))
                            do(nc.vector.reciprocal(one[:, :], one[:, :]))
                            nc.vector.tensor_tensor(share[:, s, :, :], first[:, :, :], spread8(one[:, :]), ALU.mult
                                                    ).then_inc(share_ready, 1)
                            steps.end()

                        def add_bias(g):
                            dve.wait_ge(bias_ready, g + 1)
                            dve.wait_ge(residual_added, g + 1)
                            nc.vector.tensor_tensor(x_group(g), x_group(g), bank[1][:, :].rearrange("p (t d) -> p t d", d=D),
                                                    ALU.add).then_inc(bias_used, 1)

                        def mix(g, s, e):
                            k = e % 2
                            dve.wait_ge(down_ready[k], E0 // 2 * g + e // 2 + 1)
                            if e == 0:
                                dve.wait_ge(bias_used, g + 1)
                                dve.wait_ge(share_ready, g + 1)
                            else:
                                dve.wait_ge(down_used[1 - k], E0 // 2 * g + (e - 1) // 2 + 1)
                            for t in range(TPG):
                                ins = nc.vector.scalar_tensor_tensor(
                                    out=x_tile(g, t), in0=bank[6 + k][:, t * D:(t + 1) * D], scalar=share[:, s, t, e:e + 1],
                                    in1=x_tile(g, t), op0=ALU.mult, op1=ALU.add)
                            ins.then_inc(down_used[k], 1)

                        def front(g):
                            layernorm_1(g)
                            layernorm_2(g)
                            logits_less_peak(g)
                            shares(g, 0)

                        def turn(g, s, more, ahead):
                            add_bias(g)
                            for e in range(E0):
                                if more:
                                    if e == 0:
                                        layernorm_1(g + 1)
                                    if e == 1:
                                        layernorm_2(g + 1)
                                    if e == 4:
                                        logits_less_peak(g + 1)
                                    if e == 6:
                                        shares(g + 1, 1 - s)
                                mix(g, s, e)

                        turns(dve, front, turn, lambda g: None)

                    @block.gpsimd
                    def _(pool):
                        def front(g):
                            layernorm_rstd(pool, norm0 + 2 * g, 1e-5)
                            layernorm_rstd(pool, norm0 + 2 * g + 1, 1e-5)
                            pool.wait_ge(z_ready, TPG * g + TPG)
                            nc.gpsimd.tensor_tensor(x_group(g), x_group(g), Z[:, :, :], ALU.add).then_inc(residual_added, 1)

                        turns(pool, front, lambda g, s, more, ahead: front(g + 1) if more else None, lambda g: None)

        def cross_attention_1():
            norm0 = norms[0]
            norms[0] += GROUPS
            with ExitStack() as mine:
                def sb(name, shape, dt=F32):
                    return mine.enter_context(nc.sbuf_tensor("c1_" + name, shape, dt))

                def sem(name):
                    return stage_sem("c1_" + name)

                att = Attention(sem, softmax=True, causal=False, values=lambda s, b, q: VX[:, s, b, 0, :])
                memory = sb("memory", [P, TPG, D])
                memoryT = sb("memoryT", [P, GT])
                best = sb("best", [P, TPG, 8])
                place = sb("place", [P, TPG, 8], U32)
                keyid = sb("keyid", [P, TPG], U32)

                z_ready, zT_ready, zT_copied = sem("z_ready"), sem("zT_ready"), sem("zT_copied")
                q_ready, q_copied = sem("q_ready"), sem("q_copied")
                keys_loaded = [sem(f"keys_loaded{t}") for t in range(TPG)]
                scores_ready = [sem(f"scores_ready{k}") for k in range(2)]
                scores_used = [sem(f"scores_used{k}") for k in range(2)]
                best_found = [sem(f"best_found{t}") for t in range(TPG)]
                gathered = sem("gathered")
                memoryT_ready, memoryT_copied = sem("memoryT_ready"), sem("memoryT_copied")
                k_ready, v_ready = sem("k_ready"), sem("v_ready")
                QX_ready, KX_ready, VX_ready = (sem(n) for n in ("QX_ready", "KX_ready", "VX_ready"))
                front_steps, match_steps = sem("front_steps"), sem("match_steps")
                scores_bank = [bank[2], bank[1]]

                with nc.Block() as block:
                    @block.sync
                    def _(sp):
                        def load(g):
                            for t in range(TPG):
                                sp.wait_ge(best_found[t], g)
                                sp.dma_start(keysT[:, t, :], a["ctxT"][:, bass.ds((g * TPG + t) * (BPT * KEYS), BPT * KEYS)]
                                             ).then_inc(keys_loaded[t], 16)

                        with sp.Fori(1, GROUPS) as g:
                            load(g)

                    @block.tensor
                    def _(pe):
                        def query(g):
                            pe.wait_ge(zT_copied, g + 1)
                            pe.wait_ge(VX_ready, g)
                            nc.tensor.matmul(bank[1][:, :], W("y_wqT"), zT[:, :], start=True, stop=True).then_inc(q_ready, 1)

                        def scores(g, t):
                            pe.wait_ge(q_copied, g + 1)
                            if is_first(g):
                                pe.wait_ge(first_keys_loaded, 16 * TPG)
                            else:
                                pe.wait_ge(keys_loaded[t], 16 * g)
                            if t == 0:
                                pe.wait_ge(KX_ready, H4 * g)
                            if t >= 2:
                                pe.wait_ge(scores_used[t % 2], 2 * g + 1)
                            for j in range(BPT):
                                at = t * P + j * SEQ
                                mm = nc.tensor.matmul(scores_bank[t % 2][j * SEQ:(j + 1) * SEQ, 0:KEYS], qT[:, at:at + SEQ],
                                                      keysT[:, t, j * KEYS:(j + 1) * KEYS], start=True, stop=True)
                            mm.then_inc(scores_ready[t % 2], 1)

                        def transpose_memory(g):
                            pe.wait_ge(gathered, 16 * (TPG * g + TPG))
                            for t in range(TPG):
                                mm = nc.tensor.transpose(bank[0][:, t * P:(t + 1) * P], memory[:, t, :], C("ident"))
                            mm.then_inc(memoryT_ready, 1)

                        def keys_values(g):
                            pe.wait_ge(memoryT_copied, g + 1)
                            pe.wait_ge(scores_used[0], 2 * g + 2)
                            nc.tensor.matmul(bank[2][:, :], W("y_wkrepT"), memoryT[:, :], start=True, stop=True
                                             ).then_inc(k_ready, 1)
                            pe.wait_ge(scores_used[1], 2 * g + 2)
                            pe_values_of_batches(memoryT, W("y_wvT"), DH).then_inc(v_ready, 1)

                        def front(g):
                            pe_zT(pe, g, z_ready, memoryT_copied, zT_ready)
                            query(g)
                            for t in range(TPG):
                                scores(g, t)
                            transpose_memory(g)
                            keys_values(g)

                        def turn(g, s, more, ahead):
                            if more:
                                pe_zT(pe, g + 1, z_ready, memoryT_copied, zT_ready)
                            pe.wait_ge(QX_ready, Q4 * g + Q4)
                            pe.wait_ge(KX_ready, H4 * g + H4)
                            att.pe_logits(pe, g, s, 0)
                            if more:
                                query(g + 1)
                            if not is_first(g):
                                att.pe_OT(pe, g)
                            if more:
                                scores(g + 1, 0)
                                scores(g + 1, 1)
                            att.pe_logits(pe, g, s, 1)
                            att.pe_transpose(pe, g, 0)
                            if more:
                                scores(g + 1, 2)
                                scores(g + 1, 3)
                            if not is_first(g):
                                att.pe_y(pe, g, W("y_wcT"))
                            att.pe_transpose(pe, g, 1)
                            att.pe_logits(pe, g, s, 2)
                            att.pe_values(pe, g, s, 0)
                            att.pe_logits(pe, g, s, 3)
                            att.pe_transpose(pe, g, 2)
                            if more:
                                transpose_memory(g + 1)
                            att.pe_values(pe, g, s, 1)
                            att.pe_transpose(pe, g, 3)
                            att.pe_values(pe, g, s, 2)
                            if more:
                                keys_values(g + 1)
                            att.pe_values(pe, g, s, 3)

                        def last(g):
                            att.pe_OT(pe, g)
                            att.pe_y(pe, g, W("y_wcT"))

                        turns(pe, front, turn, last)

                    @block.scalar
                    def _(act):
                        def copy_zT(g):
                            act.wait_ge(zT_ready, g + 1)
                            act.wait_ge(q_ready, g)
                            nc.scalar.copy(zT[:, :], bank[0][:, :]).then_inc(zT_copied, 1)

                        def copy_q(g):
                            act.wait_ge(q_ready, g + 1)
                            act.wait_ge(scores_ready[1], 2 * g)
                            act.wait_ge(QX_ready, Q4 * g)
                            nc.scalar.copy(qT[:, :], bank[1][:, :]).then_inc(q_copied, 1)

                        def copy_memory(g):
                            act.wait_ge(memoryT_ready, g + 1)
                            act.wait_ge(v_ready, g)
                            nc.scalar.copy(memoryT[:, :], bank[0][:, :]).then_inc(memoryT_copied, 1)

                        def spread_k(g, s):
                            act.wait_ge(k_ready, g + 1)
                            if not is_first(g):
                                act.wait_ge(att.OT_ready, g - 1)
                            for h in range(H4):
                                act_spread_keys(s, bank[2], h, KX_ready)

                        def front(g):
                            copy_zT(g)
                            copy_q(g)
                            copy_memory(g)
                            spread_k(g, 0)

                        def turn(g, s, more, ahead):
                            if more:
                                copy_zT(g + 1)
                                copy_q(g + 1)
                            att.act_exp(act, g, 0)
                            if not is_first(g):
                                att.act_copy_OT(act, g)
                            att.act_exp(act, g, 1)
                            att.act_copy_ST(act, g, 0)
                            att.act_copy_ST(act, g, 1)
                            att.act_exp(act, g, 2)
                            att.act_exp(act, g, 3)
                            att.act_copy_ST(act, g, 2)
                            if more:
                                copy_memory(g + 1)
                            att.act_copy_ST(act, g, 3)
                            if more:
                                spread_k(g + 1, 1 - s)

                        turns(act, front, turn, lambda g: att.act_copy_OT(act, g))

                    @block.vector
                    def _(dve):
                        fsteps = Steps(dve, front_steps, 7)
                        msteps = Steps(dve, match_steps, TPG)
                        bsteps = Steps(dve, att.steps, att.per)

                        def normalise_x(g):
                            fsteps.start(g)
                            layernorm(dve, fsteps, norm0 + g, lambda t: x_tile(g, t), lambda t: Z[:, t, :],
                                      lambda: dve.wait_ge(zT_ready, g), z_ready)
                            fsteps.end()

                        def queries(g, s):
                            dve.wait_ge(q_copied, g + 1)
                            if not is_first(g):
                                dve.wait_ge(att.OT_ready, g - 1)
                            for q in range(Q4):
                                dve_spread_queries(s, q, DH ** -0.5, QX_ready)

                        def find_best(g, t):
                            scores = scores_bank[t % 2][:, 0:KEYS]
                            wait_alone(dve, scores_ready[t % 2], 2 * g + t // 2 + 1)
                            nc.vector.max(out=best[:, t, :], in_=scores).then_inc(best_found[t], 1)
                            wait_alone(dve, best_found[t], g + 1)
                            if t == 0:
                                msteps.start(g)
                            msteps.did(nc.vector.max_index(out=place[:, t, :], in_max=best[:, t, :], in_values=scores))
                            msteps.settle()
                            dve.wait_ge(gathered, 16 * TPG * g)
                            nc.vector.tensor_tensor(keyid[:, t:t + 1], place[:, t, 0:1],
                                                    C("keybase")[:, bass.ds(g * TPG + t, 1)], ALU.add
                                                    ).then_inc(scores_used[t % 2], 1)

                        def values(g, s):
                            dve.wait_ge(v_ready, g + 1)
                            nc.vector.tensor_tensor(
                                VX[:, s, :, 0, 0:QW].rearrange("p b (h d) -> p b h d", d=DH),
                                bank[1][:, 0:TPG * BPT * DH].rearrange("p (b d) -> p b d", d=DH).unsqueeze(2).to_broadcast(
                                    [P, TPG * BPT, H4, DH]),
                                C("headcol").unsqueeze(1).unsqueeze(3).to_broadcast([P, TPG * BPT, H4, DH]), ALU.mult
                            ).then_inc(VX_ready, 1)

                        def front(g):
                            normalise_x(g)
                            normalise_x(g + 1)
                            queries(g, 0)
                            for t in range(TPG):
                                find_best(g, t)
                            values(g, 0)

                        def turn(g, s, more, ahead):
                            bsteps.start(g)
                            att.dve_weigh(dve, bsteps, g, 0)
                            if more:
                                find_best(g + 1, 0)
                                find_best(g + 1, 1)
                            att.dve_weigh(dve, bsteps, g, 1)
                            if more:
                                find_best(g + 1, 2)
                                find_best(g + 1, 3)
                            if not is_first(g):
                                att.dve_add(dve, g)
                            att.dve_weigh(dve, bsteps, g, 2)
                            if more:
                                queries(g + 1, 1 - s)
                            att.dve_normalise(dve, bsteps, g, 0)
                            att.dve_weigh(dve, bsteps, g, 3)
                            att.dve_normalise(dve, bsteps, g, 1)
                            if ahead:
                                normalise_x(g + 2)
                            att.dve_normalise(dve, bsteps, g, 2)
                            if more:
                                values(g + 1, 1 - s)
                            att.dve_normalise(dve, bsteps, g, 3)
                            bsteps.end()

                        turns(dve, front, turn, lambda g: att.dve_add(dve, g))

                    @block.gpsimd
                    def _(pool):
                        def gather(g):
                            wait_alone(pool, memoryT_ready, g)
                            for t in range(TPG):
                                wait_alone(pool, scores_used[t % 2], 2 * g + t // 2 + 1)
                                nc.gpsimd.indirect_dma_start(
                                    memory[:, t, :], None, a["ctx_1024"].rearrange("b k d -> (b k) d"),
                                    bass.IndirectOffsetOnAxis(ap=keyid[:, t:t + 1], axis=0)).then_inc(gathered, 16)

                        def front(g):
                            layernorm_rstd(pool, norm0 + g, 1e-5)
                            layernorm_rstd(pool, norm0 + g + 1, 1e-5)
                            gather(g)

                        def turn(g, s, more, ahead):
                            if more:
                                gather(g + 1)
                            if ahead:
                                layernorm_rstd(pool, norm0 + g + 2, 1e-5)

                        turns(pool, front, turn, lambda g: None)

        def rotary_attention():
            norm0 = norms[0]
            norms[0] += GROUPS
            with ExitStack() as mine:
                def sem(name):
                    return stage_sem("r1_" + name)

                att = Attention(sem, softmax=True, causal=True, values=lambda s, b, q: VX[:, s, b, q, :])
                z_ready, zT_ready, zT_copied = (sem(n) for n in ("z_ready", "zT_ready", "zT_copied"))
                v_ready, v_copied, VX_ready = sem("v_ready"), sem("v_copied"), sem("VX_ready")
                proj_ready = [sem(f"proj_ready{k}") for k in range(2)]
                proj_used = [sem(f"proj_used{k}") for k in range(2)]
                rotated, QX_ready, KX_ready = sem("rotated"), sem("QX_ready"), sem("KX_ready")
                masks_ready = sem("masks_ready")
                front_steps = sem("front_steps")

                with nc.Block() as block:
                    @block.tensor
                    def _(pe):
                        def project(g, u):
                            pe.wait_ge(zT_copied, g + 1)
                            if u == 0:
                                pe.wait_ge(v_copied, g)
                            else:
                                pe.wait_ge(proj_used[u % 2], 2 * g + u // 2)
                            nc.tensor.matmul(bank[1 + u % 2][:, :], W(("b_wqT", "b_wqsT", "b_wkT", "b_wksT")[u]), zT[:, :],
                                             start=True, stop=True).then_inc(proj_ready[u % 2], 1)

                        def values(g):
                            pe.wait_ge(proj_used[0], 2 * g + 2)
                            pe_values_of_batches(zT, W("b_wvT"), QW).then_inc(v_ready, 1)

                        def front(g):
                            pe_zT(pe, g, z_ready, zT_copied, zT_ready)
                            for u in range(4):
                                project(g, u)
                            values(g)

                        def turn(g, s, more, ahead):
                            if more:
                                pe_zT(pe, g + 1, z_ready, zT_copied, zT_ready)
                            pe.wait_ge(QX_ready, Q4 * g + Q4)
                            pe.wait_ge(KX_ready, H4 * g + H4)
                            att.pe_logits(pe, g, s, 0)
                            if more:
                                project(g + 1, 0)
                                project(g + 1, 1)
                            att.pe_logits(pe, g, s, 1)
                            if not is_first(g):
                                att.pe_OT(pe, g)
                            att.pe_transpose(pe, g, 0)
                            if more:
                                project(g + 1, 2)
                                project(g + 1, 3)
                            if not is_first(g):
                                att.pe_y(pe, g, W("b_woT"))
                            att.pe_logits(pe, g, s, 2)
                            att.pe_transpose(pe, g, 1)
                            if more:
                                values(g + 1)
                            pe.wait_ge(VX_ready, g + 1)
                            att.pe_values(pe, g, s, 0)
                            att.pe_logits(pe, g, s, 3)
                            att.pe_transpose(pe, g, 2)
                            att.pe_values(pe, g, s, 1)
                            att.pe_transpose(pe, g, 3)
                            att.pe_values(pe, g, s, 2)
                            att.pe_values(pe, g, s, 3)

                        def last(g):
                            att.pe_OT(pe, g)
                            att.pe_y(pe, g, W("b_woT"))

                        pe.wait_ge(masks_ready, 2)
                        turns(pe, front, turn, last)

                    @block.scalar
                    def _(act):
                        def front(g):
                            act.wait_ge(zT_ready, g + 1)
                            act.wait_ge(v_ready, g)
                            nc.scalar.copy(zT[:, :], bank[0][:, :]).then_inc(zT_copied, 1)

                        def copy_v(g):
                            act.wait_ge(v_ready, g + 1)
                            act.wait_ge(VX_ready, g)
                            nc.scalar.copy(V[:, :, :, :].rearrange("p b q d -> p (b q d)"), bank[1][:, :]).then_inc(v_copied, 1)

                        def spread_k(g, s, h):
                            act.wait_ge(rotated, 2 * g + 2)
                            if not is_first(g):
                                act.wait_ge(att.OT_ready, g - 1)
                            act_spread_keys(s, kT, h, KX_ready)

                        def turn(g, s, more, ahead):
                            if more:
                                front(g + 1)
                            att.act_exp(act, g, 0)
                            if not is_first(g):
                                att.act_copy_OT(act, g)
                            att.act_exp(act, g, 1)
                            att.act_copy_ST(act, g, 0)
                            att.act_exp(act, g, 2)
                            att.act_copy_ST(act, g, 1)
                            if more:
                                copy_v(g + 1)
                            att.act_exp(act, g, 3)
                            att.act_copy_ST(act, g, 2)
                            if more:
                                spread_k(g + 1, 1 - s, 0)
                                spread_k(g + 1, 1 - s, 1)
                            att.act_copy_ST(act, g, 3)
                            if more:
                                spread_k(g + 1, 1 - s, 2)
                                spread_k(g + 1, 1 - s, 3)

                        def front_0(g):
                            front(g)
                            for h in range(H4):
                                spread_k(g, 0, h)
                            copy_v(g)

                        turns(act, front_0, turn, lambda g: att.act_copy_OT(act, g))

                    @block.vector
                    def _(dve):
                        fsteps = Steps(dve, front_steps, 7)
                        bsteps = Steps(dve, att.steps, att.per)
                        nc.vector.tensor_copy(maskneg16[0:SEQ, :], C("maskneg")[0:SEQ, :]).then_inc(masks_ready, 1)
                        nc.vector.tensor_copy(spread16[0:SEQ, :], C("spread")[0:SEQ, :]).then_inc(masks_ready, 1)

                        def moments_of_x(g):
                            fsteps.start(g)
                            layernorm_moments(dve, fsteps, lambda t: x_tile(g, t))
                            fsteps.end()

                        def normalise_x(g):
                            layernorm_output(dve, norm0 + g, lambda t: x_tile(g, t), lambda t: Z[:, t, :],
                                             lambda: dve.wait_ge(zT_ready, g), z_ready)

                        def rotate(g, u):
                            if u == 0:
                                dve.wait_ge(QX_ready, Q4 * g)
                                dve.wait_ge(KX_ready, H4 * g)
                            for k, (to, table) in enumerate((((qT, kT)[u], "cos"), ((spare, spare2)[u], "sin"))):
                                dve.wait_ge(proj_ready[k], 2 * g + u + 1)
                                nc.vector.tensor_tensor(by_batch(to[:, :]), by_batch(bank[1 + k][:, :]),
                                                        C(table).unsqueeze(1).to_broadcast([P, TPG * BPT, SEQ]), ALU.mult
                                                        ).then_inc(proj_used[k], 1)

                        def queries(g, s):
                            dve.wait_ge(rotated, 2 * g + 1)
                            if not is_first(g):
                                dve.wait_ge(att.OT_ready, g - 1)
                            for q in range(Q4):
                                dve_spread_queries(s, q, DH ** -0.5, QX_ready)

                        def front(g):
                            for n in (g, g + 1):
                                moments_of_x(n)
                                normalise_x(n)
                            rotate(g, 0)
                            rotate(g, 1)
                            queries(g, 0)

                        def turn(g, s, more, ahead):
                            bsteps.start(g)
                            att.dve_weigh(dve, bsteps, g, 0)
                            if more:
                                rotate(g + 1, 0)
                            att.dve_weigh(dve, bsteps, g, 1)
                            if more:
                                rotate(g + 1, 1)
                            att.dve_weigh(dve, bsteps, g, 2)
                            if not is_first(g):
                                att.dve_add(dve, g)
                            att.dve_normalise(dve, bsteps, g, 0)
                            att.dve_weigh(dve, bsteps, g, 3)
                            if more:
                                queries(g + 1, 1 - s)
                            att.dve_normalise(dve, bsteps, g, 1)
                            if ahead:
                                moments_of_x(g + 2)
                            att.dve_normalise(dve, bsteps, g, 2)
                            if ahead:
                                normalise_x(g + 2)
                            att.dve_normalise(dve, bsteps, g, 3)
                            bsteps.end()

                        turns(dve, front, turn, lambda g: att.dve_add(dve, g))

                    @block.gpsimd
                    def _(pool):
                        def front(g, s):
                            for u, (to, part) in enumerate(((qT, spare), (kT, spare2))):
                                pool.wait_ge(proj_used[0], 2 * g + u + 1)
                                pool.wait_ge(proj_used[1], 2 * g + u + 1)
                                nc.gpsimd.tensor_tensor(to[:, :], to[:, :], part[:, :], ALU.add).then_inc(rotated, 1)
                            pool.wait_ge(v_copied, g + 1)
                            if not is_first(g):
                                pool.wait_ge(att.OT_ready, g - 1)
                            spread_values(nc.gpsimd, s, VX_ready)

                        def first(g):
                            layernorm_rstd(pool, norm0 + g, 1e-5)
                            layernorm_rstd(pool, norm0 + g + 1, 1e-5)
                            front(g, 0)

                        def turn(g, s, more, ahead):
                            if more:
                                front(g + 1, 1 - s)
                            if ahead:
                                layernorm_rstd(pool, norm0 + g + 2, 1e-5)

                        turns(pool, first, turn, lambda g: None)

        def experts_1():
            norm0 = norms[0]
            norms[0] += 2 * GROUPS
            with ExitStack() as mine:
                def sb(name, shape, dt=F32):
                    return mine.enter_context(nc.sbuf_tensor("f1_" + name, shape, dt))

                def sem(name):
                    return stage_sem("f1_" + name)

                Z1 = sb("Z1", [P, TPG, D])
                A = sb("A", [P, TILES * D])
                aT = sb("aT", [P, TOKENS])
                logit = sb("logit", [P, TILES * 10])
                r1 = sb("r1", [P, F1])
                r2 = sb("r2", [P, 4, D])
                w1 = sb("w1", [P, 2, F1])
                w2 = sb("w2", [P, 2, 4, D])
                b2 = sb("b2", [P, E1, D])
                hidden = sb("hidden", [P, 2, 4, GT])
                coef = sb("coef", [P, TILES, 2])
                coef0 = sb("coef0", [P, TILES])
                moe = sb("moe", [P, TILES])
                sent_all = sb("sent_all", [P, TILES], U32)
                fetch_all = sb("fetch_all", [P, TILES], U32)
                sent = sb("sent", [P, TPG], U32)
                fetch = sb("fetch", [P, TPG], U32)
                sending = sb("sending", [P, TPG, D])
                places = sb("places", [P, 2, TPG, D])
                placesT = sb("placesT", [P, 2, GT])
                result = sb("result", [P, 2, TPG, D])
                fetched = sb("fetched", [P, TPG, D])
                rowspace = a["rowspace"]
                results = a["results"]

                dve_steps = sem("dve_steps")
                wts_loaded = sem("wts_loaded")
                z_ready, a_scaled, a_ready, aT_ready, aT_copied = (sem(n) for n in (
                    "z_ready", "a_scaled", "a_ready", "aT_ready", "aT_copied"))
                gate_ready, gate_used, kept = sem("gate_ready"), sem("gate_used"), sem("kept")
                sending_copied, fetch_scaled = sem("sending_copied"), sem("fetch_scaled")

                with nc.Block() as block:
                    @block.sync
                    def _(sp):
                        sp.dma_start(r1[:, :], a["g_r1"][:, :]).then_inc(wts_loaded, 16)
                        sp.dma_start(r2[:, :, :], a["g_r2"].rearrange("(c p) d -> p c d", p=P)).then_inc(wts_loaded, 16)
                        sp.dma_start(b2[:, :, :], a["g_b2"].rearrange("e d -> (e d)").partition_broadcast(P)
                                     .rearrange("p (e d) -> p e d", d=D)).then_inc(wts_loaded, 16)
                        sp.wait_ge(wts_loaded, 48)

                    @block.vector
                    def _(dve):
                        steps = Steps(dve, dve_steps, 14 + 1)
                        with dve.Fori(0, GROUPS) as i:
                            steps.start(i)
                            layernorm(dve, steps, norm0 + 2 * i, lambda t: x_tile(i, t), lambda t: Z1[:, t, :],
                                      lambda: None, z_ready)
                            dve.wait_ge(z_ready, 2 * TPG * i + TPG)
                            layernorm(dve, steps, norm0 + 2 * i + 1, lambda t: Z1[:, t, :], lambda t: Z[:, t, :],
                                      lambda: dve.wait_ge(kept, i), z_ready)
                            steps.did(nc.vector.tensor_tensor(x_group(i), x_group(i), Z1[:, :, :], ALU.add))
                            steps.settle()
                            dve.wait_ge(z_ready, 2 * TPG * i + 2 * TPG)
                            nc.vector.tensor_tensor(Z[:, :, :], Z[:, :, :], W("g_nw").unsqueeze(1).to_broadcast([P, TPG, D]),
                                                    ALU.mult).then_inc(a_scaled, 1)
                            dve.wait_ge(a_scaled, i + 1)
                            nc.vector.tensor_tensor(Z[:, :, :], Z[:, :, :], W("g_nb").unsqueeze(1).to_broadcast([P, TPG, D]),
                                                    ALU.add).then_inc(a_ready, 1)
                            dve.wait_ge(gate_ready, i + 1)
                            nc.vector.tensor_copy(logit[:, bass.ds(i * (TPG * 10), TPG * 10)], bank[1][:, 0:TPG * 10]
                                                  ).then_inc(gate_used, 1)
                            steps.end()

                    @block.gpsimd
                    def _(pool):
                        with pool.Fori(0, GROUPS) as i:
                            layernorm_rstd(pool, norm0 + 2 * i, 1e-5)
                            layernorm_rstd(pool, norm0 + 2 * i + 1, 1e-12)

                    @block.tensor
                    def _(pe):
                        with pe.Fori(0, GROUPS) as i:
                            pe.wait_ge(a_ready, i + 1)
                            pe.wait_ge(aT_copied, 2 * i)
                            for t in range(TPG):
                                mm = nc.tensor.transpose(bank[0][:, t * P:(t + 1) * P], Z[:, t, :], C("ident"))
                            mm.then_inc(aT_ready, 1)
                            pe.wait_ge(aT_copied, 2 * i + 1)
                            pe.wait_ge(gate_used, i)
                            for t in range(TPG):
                                mm = nc.tensor.matmul(bank[1][:, t * 10:(t + 1) * 10], zT[:, t * P:(t + 1) * P], W("g_w"),
                                                      start=True, stop=True)
                            mm.then_inc(gate_ready, 1)

                    @block.scalar
                    def _(act):
                        with act.Fori(0, GROUPS) as i:
                            act.wait_ge(aT_ready, i + 1)
                            act.wait_ge(gate_ready, i)
                            nc.scalar.copy(zT[:, :], bank[0][:, :]).then_inc(aT_copied, 1)
                            nc.scalar.copy(aT[:, bass.ds(i * GT, GT)], bank[0][:, :]).then_inc(aT_copied, 1)
                            nc.scalar.copy(A[:, bass.ds(i * GT, GT)], Z[:, :, :].rearrange("p t d -> p (t d)")
                                           ).then_inc(kept, 1)

                def sb8(name):
                    return sb(name, [P, TILES, E1])

                prob, hit, onehot, where = sb8("prob"), sb8("hit"), sb8("onehot"), sb8("where")
                running, place = sb("running", [P, E1 * TILES]), sb("place", [P, E1, TILES])
                peak, total, rtotal, own, kept_, slot = (sb(n, [P, TILES]) for n in (
                    "peak", "total", "rtotal", "own", "kept", "slot"))
                low_ready, exp_done, onehot_ready, counts_ready = (sem(n) for n in (
                    "low_ready", "exp_done", "onehot_ready", "counts_ready"))
                routed = sem("routed")

                def by_tile(v):
                    return v.unsqueeze(2).to_broadcast([P, TILES, E1])

                with nc.Block() as block:
                    @block.scalar
                    def _(act):
                        act.wait_ge(low_ready, 2)
                        nc.scalar.activation(prob[:, :, :], prob[:, :, :], ACT.Exp).then_inc(exp_done, 1)
                        nc.scalar.activation(coef[:, :, :], coef[:, :, :], ACT.Exp).then_inc(exp_done, 1)

                    @block.tensor
                    def _(pe):
                        pe.wait_ge(onehot_ready, 1)
                        oh = onehot[:, :, :].rearrange("p t e -> p e t")
                        nc.tensor.matmul(bank[2][:, 0:E1 * TILES], C("before"), oh, start=True, stop=True)
                        nc.tensor.matmul(bank[3][:, 0:E1 * TILES], C("ones"), oh, start=True, stop=True).then_inc(counts_ready, 1)

                    @block.vector
                    def _(dve):
                        route_steps = sem("route_steps")
                        steps = Steps(dve, route_steps, 0)
                        steps.start(0)

                        def do(ins):
                            steps.did(ins)
                            steps.settle()

                        v = logit[:, :].rearrange("p (t w) -> p t w", w=10)
                        do(nc.vector.reduce_max(peak[:, :], v[:, :, 0:E1], AX_X))
                        nc.vector.tensor_tensor(prob[:, :, :], v[:, :, 0:E1], by_tile(peak[:, :]), ALU.subtract
                                                ).then_inc(low_ready, 1)
                        do(nc.vector.reduce_max(own[:, :], v[:, :, E1:E1 + 2], AX_X))
                        nc.vector.tensor_tensor(coef[:, :, :], v[:, :, E1:E1 + 2],
                                                own[:, :].unsqueeze(2).to_broadcast([P, TILES, 2]), ALU.subtract
                                                ).then_inc(low_ready, 1)
                        dve.wait_ge(exp_done, 2)
                        do(nc.vector.reduce_sum(total[:, :], prob[:, :, :], AX_X))
                        do(nc.vector.reciprocal(rtotal[:, :], total[:, :]))
                        do(nc.vector.tensor_tensor(prob[:, :, :], prob[:, :, :], by_tile(rtotal[:, :]), ALU.mult))
                        do(nc.vector.reduce_max(peak[:, :], prob[:, :, :], AX_X))
                        do(nc.vector.tensor_tensor(hit[:, :, :], prob[:, :, :], by_tile(peak[:, :]), ALU.is_equal))
                        do(nc.vector.tensor_tensor(hit[:, :, :], hit[:, :, :],
                                                   C("rank8").unsqueeze(1).to_broadcast([P, TILES, E1]), ALU.mult))
                        do(nc.vector.reduce_max(own[:, :], hit[:, :, :], AX_X))
                        nc.vector.tensor_tensor(onehot[:, :, :], hit[:, :, :], by_tile(own[:, :]), ALU.is_equal
                                                ).then_inc(onehot_ready, 1)
                        do(nc.vector.reduce_sum(total[:, :], coef[:, :, :], AX_X))
                        do(nc.vector.reciprocal(rtotal[:, :], total[:, :]))
                        do(nc.vector.tensor_tensor(coef[:, :, :], coef[:, :, :],
                                                   rtotal[:, :].unsqueeze(2).to_broadcast([P, TILES, 2]), ALU.mult))
                        do(nc.vector.tensor_copy(coef0[:, :], coef[:, :, 0]))
                        dve.wait_ge(counts_ready, 1)
                        dve.wait_ge(onehot_ready, 1)
                        do(nc.vector.tensor_tensor_scan(running[:, :], C("restart"), bank[3][:, 0:E1 * TILES], 0.0,
                                                        ALU.mult, ALU.add))
                        do(nc.vector.tensor_tensor(running[:, :], running[:, :], bank[3][:, 0:E1 * TILES], ALU.subtract))
                        do(nc.vector.tensor_tensor(place[:, :, :].rearrange("p e t -> p (e t)"), running[:, :],
                                                   bank[2][:, 0:E1 * TILES], ALU.add))
                        do(nc.vector.tensor_tensor(where[:, :, :], place[:, :, :].rearrange("p e t -> p t e"), onehot[:, :, :],
                                                   ALU.mult))
                        do(nc.vector.reduce_sum(own[:, :], where[:, :, :], AX_X))
                        do(nc.vector.tensor_scalar(kept_[:, :], own[:, :], float(CAP), None, ALU.is_lt))
                        do(nc.vector.tensor_tensor(hit[:, :, :], onehot[:, :, :],
                                                   C("expertbase").unsqueeze(1).to_broadcast([P, TILES, E1]), ALU.mult))
                        do(nc.vector.reduce_sum(slot[:, :], hit[:, :, :], AX_X))
                        do(nc.vector.tensor_tensor(slot[:, :], slot[:, :], own[:, :], ALU.add))
                        do(nc.vector.tensor_tensor(fetch_all[:, :], slot[:, :], kept_[:, :], ALU.mult))
                        do(nc.vector.tensor_tensor(slot[:, :], slot[:, :], C("tokenid"), ALU.subtract))
                        do(nc.vector.tensor_tensor(slot[:, :], slot[:, :], kept_[:, :], ALU.mult))
                        do(nc.vector.tensor_tensor(sent_all[:, :], slot[:, :], C("tokenid"), ALU.add))
                        do(nc.vector.tensor_tensor(moe[:, :], peak[:, :], kept_[:, :], ALU.mult))
                        do(nc.vector.tensor_tensor(moe[:, :], moe[:, :], coef[:, :, 1], ALU.mult))

                sending_ready, rows_sent = sem("sending_ready"), sem("rows_sent")
                up_ready = [sem(f"up_ready{k}") for k in range(2)]
                gelu_done = [sem(f"gelu_done{k}") for k in range(2)]
                down_ready, down_used = sem("down_ready"), sem("down_used")
                biased = sem("biased")
                residual_added = sem("residual_added")
                with nc.Block() as block:
                    @block.gpsimd
                    def _(pool):
                        with pool.Fori(0, GROUPS) as i:
                            wait_alone(pool, sending_ready, i + 1)
                            for t in range(TPG):
                                nc.gpsimd.indirect_dma_start(
                                    rowspace[:, :], bass.IndirectOffsetOnAxis(ap=sent[:, t:t + 1], axis=0),
                                    sending[:, t, :], None).then_inc(rows_sent, 16)
                        pool.wait_ge(rows_sent, 16 * TILES)

                    @block.tensor
                    def _(pe):
                        with pe.Fori(0, GROUPS) as i:
                            for f in range(4):
                                k = f % 2
                                pe.wait_ge(gelu_done[k], 2 * i + f // 2)
                                nc.tensor.matmul(bank[k][:, :], r1[:, f * P:(f + 1) * P], aT[:, bass.ds(i * GT, GT)],
                                                 start=True, stop=True).then_inc(up_ready[k], 1)
                            pe.wait_ge(gelu_done[0], 2 * i + 2)
                            pe.wait_ge(gelu_done[1], 2 * i + 2)
                            pe.wait_ge(down_used, i)
                            for t in range(TPG):
                                for f in range(4):
                                    mm = nc.tensor.matmul(bank[2][:, t * D:(t + 1) * D], hidden[:, 0, f, t * P:(t + 1) * P],
                                                          r2[:, f, :], start=(f == 0), stop=(f == 3))
                            mm.then_inc(down_ready, 1)

                    @block.scalar
                    def _(act):
                        with act.Fori(0, GROUPS) as i:
                            act.wait_ge(rows_sent, 16 * TPG * i)
                            nc.scalar.copy(sending[:, :, :].rearrange("p t d -> p (t d)"), A[:, bass.ds(i * GT, GT)]
                                           ).then_inc(sending_copied, 1)
                            act.wait_ge(down_ready, i)
                            for f in range(4):
                                k = f % 2
                                act.wait_ge(up_ready[k], 2 * i + f // 2 + 1)
                                nc.scalar.activation(hidden[:, 0, f, :], bank[k][:, :], ACT.Gelu_apprx_tanh,
                                                     bias=W("g_rb1")[:, f:f + 1]).then_inc(gelu_done[k], 1)

                    @block.vector
                    def _(dve):
                        with dve.Fori(0, GROUPS) as i:
                            dve.wait_ge(sending_copied, i + 1)
                            nc.vector.tensor_copy(sent[:, :], sent_all[:, bass.ds(i * TPG, TPG)]).then_inc(sending_ready, 1)
                            dve.wait_ge(down_ready, i + 1)
                            dve.wait_ge(residual_added, i)
                            nc.vector.tensor_tensor(result[:, 0, :, :], bank[2][:, :].rearrange("p (t d) -> p t d", d=D),
                                                    W("g_rb2").unsqueeze(1).to_broadcast([P, TPG, D]), ALU.add
                                                    ).then_inc(down_used, 1)
                            dve.wait_ge(down_used, i + 1)
                            nc.vector.tensor_tensor(result[:, 0, :, :], result[:, 0, :, :],
                                                    coef0[:, bass.ds(i * TPG, TPG)].unsqueeze(2).to_broadcast([P, TPG, D]),
                                                    ALU.mult).then_inc(biased, 1)
                            dve.wait_ge(biased, i + 1)
                            nc.vector.tensor_tensor(x_group(i), x_group(i), result[:, 0, :, :], ALU.add).then_inc(residual_added, 1)

                w_loaded = [sem(f"w_loaded{k}") for k in range(2)]
                placesT_ready, placesT_copied = ([sem(f"{n}{k}") for k in range(2)] for n in ("placesT_ready", "placesT_copied"))
                e_up_ready = [sem(f"e_up_ready{k}") for k in range(2)]
                e_gelu_done = [sem(f"e_gelu_done{k}") for k in range(2)]
                e_down_ready = [sem(f"e_down_ready{k}") for k in range(2)]
                result_ready = [sem(f"result_ready{k}") for k in range(2)]
                result_stored = [sem(f"result_stored{k}") for k in range(2)]
                with nc.Block() as block:
                    @block.sync
                    def _(sp):
                        with sp.Fori(0, E1 // 2) as i:
                            for k in range(2):
                                e = 2 * i + k
                                sp.wait_ge(e_down_ready[k], i)
                                sp.dma_start(places[:, k, :, :], rowspace[bass.ds(e * CAP, CAP), :].rearrange(
                                    "(t p) d -> p t d", p=P)).then_inc(w_loaded[k], 16)
                                sp.dma_start(w1[:, k, :], a["g_w1"][bass.ds(e, 1), :, :].rearrange("e p f -> p (e f)")
                                             ).then_inc(w_loaded[k], 16)
                                sp.dma_start(w2[:, k, :, :], a["g_w2"][bass.ds(e, 1), :, :].rearrange(
                                    "e (c p) d -> p (e c) d", p=P)).then_inc(w_loaded[k], 16)

                    @block.tensor
                    def _(pe):
                        def up(i, k):
                            pe.wait_ge(w_loaded[k], 48 * i + 48)
                            pe.wait_ge(placesT_copied[k], i)
                            for t in range(TPG):
                                mm = nc.tensor.transpose(bank[k][:, t * P:(t + 1) * P], places[:, k, t, :], C("ident"))
                            mm.then_inc(placesT_ready[k], 1)
                            pe.wait_ge(placesT_copied[k], i + 1)
                            for f in range(4):
                                pe.wait_ge(e_gelu_done[f % 2], 4 * i + 2 * k + f // 2)
                                nc.tensor.matmul(bank[2 + f % 2][:, :], w1[:, k, f * P:(f + 1) * P], placesT[:, k, :],
                                                 start=True, stop=True).then_inc(e_up_ready[f % 2], 1)

                        def down(i, k):
                            for m in range(2):
                                pe.wait_ge(e_gelu_done[m], 4 * i + 2 * k + 2)
                            pe.wait_ge(result_ready[k], i)
                            for t in range(TPG):
                                for f in range(4):
                                    mm = nc.tensor.matmul(bank[4 + k][:, t * D:(t + 1) * D], hidden[:, k, f, t * P:(t + 1) * P],
                                                          w2[:, k, f, :], start=(f == 0), stop=(f == 3))
                            mm.then_inc(e_down_ready[k], 1)

                        with pe.Fori(0, E1 // 2) as i:
                            for k in range(2):
                                up(i, k)
                                down(i, k)

                    @block.scalar
                    def _(act):
                        with act.Fori(0, E1 // 2) as i:
                            for k in range(2):
                                act.wait_ge(placesT_ready[k], i + 1)
                                nc.scalar.copy(placesT[:, k, :], bank[k][:, :]).then_inc(placesT_copied[k], 1)
                                act.wait_ge(e_down_ready[k], i)
                                for f in range(4):
                                    act.wait_ge(e_up_ready[f % 2], 4 * i + 2 * k + f // 2 + 1)
                                    nc.scalar.activation(hidden[:, k, f, :], bank[2 + f % 2][:, :], ACT.Gelu_apprx_tanh,
                                                         bias=W("g_b1")[:, bass.ds(i * 8 + 4 * k + f, 1)]
                                                         ).then_inc(e_gelu_done[f % 2], 1)

                    @block.vector
                    def _(dve):
                        with dve.Fori(0, E1 // 2) as i:
                            for k in range(2):
                                dve.wait_ge(e_down_ready[k], i + 1)
                                dve.wait_ge(result_stored[k], 16 * i)
                                nc.vector.tensor_tensor(result[:, k, :, :], bank[4 + k][:, :].rearrange("p (t d) -> p t d", d=D),
                                                        b2[:, bass.ds(2 * i + k, 1), :].to_broadcast([P, TPG, D]), ALU.add
                                                        ).then_inc(result_ready[k], 1)

                    @block.gpsimd
                    def _(pool):
                        with pool.Fori(0, E1 // 2) as i:
                            for k in range(2):
                                pool.wait_ge(result_ready[k], i + 1)
                                pool.dma_start(results[bass.ds((2 * i + k) * CAP, CAP), :].rearrange("(t p) d -> p t d", p=P),
                                               result[:, k, :, :]).then_inc(result_stored[k], 16)
                        for k in range(2):
                            pool.wait_ge(result_stored[k], 16 * (E1 // 2))

                fetch_ready, rows_fetched, x_ready = sem("fetch_ready"), sem("rows_fetched"), sem("x_ready")
                with nc.Block() as block:
                    @block.vector
                    def _(dve):
                        with dve.Fori(0, GROUPS) as i:
                            nc.vector.tensor_copy(fetch[:, :], fetch_all[:, bass.ds(i * TPG, TPG)]).then_inc(fetch_ready, 1)
                            dve.wait_ge(rows_fetched, 16 * (TPG * i + TPG))
                            nc.vector.tensor_tensor(fetched[:, :, :], fetched[:, :, :],
                                                    moe[:, bass.ds(i * TPG, TPG)].unsqueeze(2).to_broadcast([P, TPG, D]),
                                                    ALU.mult).then_inc(fetch_scaled, 1)
                            dve.wait_ge(fetch_scaled, i + 1)
                            nc.vector.tensor_tensor(x_group(i), x_group(i), fetched[:, :, :], ALU.add).then_inc(x_ready, 1)

                    @block.gpsimd
                    def _(pool):
                        with pool.Fori(0, GROUPS) as i:
                            wait_alone(pool, fetch_ready, i + 1)
                            wait_alone(pool, x_ready, i)
                            for t in range(TPG):
                                nc.gpsimd.indirect_dma_start(
                                    fetched[:, t, :], None, results[:, :],
                                    bass.IndirectOffsetOnAxis(ap=fetch[:, t:t + 1], axis=0)).then_inc(rows_fetched, 16)

        def setup():
            with nc.Block() as block:
                @block.sync
                def _(sp):
                    sp.dma_start(X[:, 0:GT], a["xt"][:, 0:GT]).then_inc(x_first, 16)
                    sp.dma_start(const[:, :], a["const"][:, :]).then_inc(loaded, 16)
                    sp.dma_start(small[:, :], a["small"][:, :]).then_inc(loaded, 16)
                    if ONLY not in (None, 1):
                        sp.dma_start(ew1[:, :], a["f_w1"][:, :]).then_inc(weights_loaded, 16)
                        sp.dma_start(ew2[:, :], a["f_w2"][:, :]).then_inc(weights_loaded, 16)
                        if ONLY == 4:
                            for t in range(TPG):
                                sp.dma_start(keysT[:, t, :], a["ctxT"][:, t * (BPT * KEYS):(t + 1) * (BPT * KEYS)]
                                             ).then_inc(first_keys_loaded, 16)
                        sp.dma_start(X[:, GT:], a["xt"][:, GT:]).then_inc(x_loaded, 16)
                        sp.wait_ge(x_first, 16)
                        sp.wait_ge(x_loaded, 16)
                        sp.wait_ge(loaded, LOADS)
                @block.vector
                def _(dve):
                    if ONLY not in (None, 1):
                        dve.wait_ge(loaded, LOADS)
                        for s in range(2):
                            nc.vector.tensor_copy(VX[:, s, :, :, QW:VW].rearrange("p b q w -> p (b q) w"),
                                                  C("headcol").unsqueeze(1).to_broadcast([P, TPG * BPT * Q4, H4]))

                @block.gpsimd
                def _(pool):
                    nc.gpsimd.memset(zeros[:, :], 0.0).then_inc(zeros_ready, 1)

        def store(sp):
            sp.dma_start(out.rearrange("b s d -> (b s) d").rearrange("(t p) d -> p t d", p=P),
                         X[:, :].rearrange("p (t d) -> p t d", d=D)).then_inc(x_out, 16)
            sp.wait_ge(x_out, 16)

        stages = [cross_attention_0, linear_attention, experts_0, cross_attention_1, rotary_attention, experts_1]
        setup()
        for stage in stages[:STAGES] if ONLY is None else [stages[ONLY - 1]]:
            if stage is experts_1:
                attention_buffers.close()
            stage()
            nc.clear_and_free_semaphores(stage_sems)
            stage_sems.clear()
            nc.all_engine_barrier()
        with nc.Block() as block:
            @block.sync
            def _(sp):
                store(sp)
        attention_buffers.close()


def constants():
    p = np.arange(P)
    c = np.zeros((P, CONST_W), np.float32)

    def put(name, v):
        at, w = CONST[name]
        c[:v.shape[0], at:at + w] = v

    put("ident", np.eye(P))
    put("batch4", p[:, None] // SEQ == np.arange(4))
    put("quarter4", p[:, None] // QW == np.arange(4))
    put("head4", p[:, None] % QW // DH == np.arange(4))
    put("headblock", p[:, None] // SEQ == np.arange(QW) // DH)
    put("headcol", p[:, None] // SEQ == np.arange(H4))
    put("causal", p[:, None] % SEQ <= np.arange(SEQ))
    half = (np.float32(1.0) / np.float32(10000.0) ** (np.arange(0, DH, 2, dtype=np.float32) / np.float32(DH))).astype(np.float32)
    angle = (half[p % DH // 2][:, None] * np.arange(SEQ, dtype=np.float32)).astype(np.float32)
    put("cos", np.cos(angle))
    put("sin", np.sin(angle) * np.where(p % 2 == 0, -1.0, 1.0)[:, None])
    put("maskneg", np.where(np.arange(SEQ)[None, :] > np.arange(SEQ)[:, None], -1e30, 0.0))
    put("spread", np.arange(SEQ)[:, None] == p % SEQ)
    put("minushalf", np.full((P, 4), -0.5))
    put("before", p[:, None] < p)
    put("ones", np.ones((P, P)))
    put("keybase", (np.arange(TILES) * BPT + p[:, None] // SEQ) * KEYS)
    put("rank8", np.broadcast_to(8.0 - np.arange(8), (P, 8)))
    put("expertbase", np.broadcast_to(CAP * np.arange(8.0), (P, 8)))
    put("tokenid", E1 * CAP + np.arange(TILES) * P + p[:, None])
    put("restart", np.broadcast_to(np.arange(256) % TILES != 0, (P, 256)))
    return c


def weights(v):
    s = np.zeros((P, SMALL_W), np.float32)

    def put(name, w):
        at, n = SMALL[name]
        s[:w.shape[0], at:at + n] = w

    def row(name, w):
        put(name, np.broadcast_to(w.reshape(1, -1), (P, w.size)))

    def col(name, w):
        put(name, w.reshape(P, -1) if w.ndim == 1 else w)

    put("x_wqT", v["L0_xattn_Wq"].T)
    put("x_wk", v["L0_xattn_Wk"])
    put("x_wvT", v["L0_xattn_Wv"].T)
    col("x_bq", v["L0_xattn_bq"])
    col("x_bk", v["L0_xattn_bk"])
    row("x_bv", v["L0_xattn_bv"])
    by_head = np.arange(D).reshape(Q4, H4, DH).transpose(1, 0, 2)
    put("a_w", v["L0_attn_qkv_w"][:, :2 * D])
    put("a_wv", v["L0_attn_qkv_w"][:, 2 * D:][:, by_head.ravel()])
    col("a_bq", v["L0_attn_qkv_b"][:D])
    col("a_bk", v["L0_attn_qkv_b"][D:2 * D])
    put("a_bvh", np.repeat(v["L0_attn_qkv_b"][2 * D:][by_head].reshape(H4, QW), SEQ, axis=0))
    put("a_wo", v["L0_attn_out_w"])
    row("a_bo", v["L0_attn_out_b"])
    col("f_g", v["L0_ffn_ln_g"])
    col("f_b", v["L0_ffn_ln_b"])
    put("f_rw", v["L0_ffn_rW"])
    row("f_rb", v["L0_ffn_rb"])
    put("f_b1", v["L0_ffn_b1"].reshape(E0, 2, P).transpose(2, 0, 1).reshape(P, 16))
    put("f_b2", v["L0_ffn_b2"])
    put("y_wqT", v["L1_xattn_Wq"].T)
    put("y_wkrepT", np.tile(v["L1_xattn_Wkv"][:DH].T, (1, HEADS)))
    put("y_wvT", v["L1_xattn_Wkv"][DH:].T)
    put("y_wcT", v["L1_xattn_Wc"].T)
    swap = np.arange(D) ^ 1
    put("b_wqT", v["L1_attn_Wq"].T)
    put("b_wqsT", v["L1_attn_Wq"][swap].T)
    put("b_wkT", v["L1_attn_Wk"].T)
    put("b_wksT", v["L1_attn_Wk"][swap].T)
    put("b_wvT", v["L1_attn_Wv"].T[:, by_head.ravel()])
    put("b_woT", v["L1_attn_Wo"].T)
    row("g_nw", v["L1_ffn_attn_nw"])
    row("g_nb", v["L1_ffn_attn_nb"])
    put("g_w", np.concatenate([v["L1_ffn_wg"], v["L1_ffn_res_coef"]], axis=1))
    put("g_rb1", v["L1_ffn_res_inter_b"].reshape(4, P).T)
    row("g_rb2", v["L1_ffn_res_output_b"])
    put("g_b1", v["L1_ffn_inter_b"].reshape(E1, 4, P).transpose(2, 0, 1).reshape(P, 32))
    return s


def kernel(**inputs):
    import concourse.bacc as bacc
    from concourse.bass_utils import run_bass_kernel_spmd

    v = {k: np.asarray(x) for k, x in inputs.items()}
    arrays = {
        "ctx_1024": v["ctx_1024"],
        "xt": np.ascontiguousarray(v["x"].reshape(TILES, P, D).transpose(1, 0, 2)).reshape(P, TILES * D),
        "ctxN": np.ascontiguousarray(v["ctx_1024"][:, :KEYS - 1].reshape(BATCH, 2, P, D).transpose(2, 0, 1, 3)
                                     ).reshape(P, BATCH * 2 * D),
        "lastkeys": np.ascontiguousarray(v["ctx_1024"][:, KEYS - 1]).reshape(1, BATCH * D),
        "ctxT": np.ascontiguousarray(v["ctx_1024"].transpose(2, 0, 1)).reshape(D, BATCH * KEYS),
        "const": constants(),
        "small": weights(v),
        "f_w1": np.ascontiguousarray(v["L0_ffn_W1"].transpose(1, 0, 2)).reshape(D, E0 * F0),
        "f_w2": np.ascontiguousarray(v["L0_ffn_W2"].reshape(E0, 2, P, D).transpose(2, 0, 1, 3)).reshape(P, E0 * 2 * D),
        "g_w1": v["L1_ffn_inter_w"],
        "g_w2": v["L1_ffn_output_w"],
        "g_b2": v["L1_ffn_output_b"],
        "g_r1": v["L1_ffn_res_inter_w"],
        "g_r2": v["L1_ffn_res_output_w"],
    }
    nc = bacc.Bacc("TRN2", target_bir_lowering=False, num_devices=1)
    aps = {}
    maps = {}
    for name, x in arrays.items():
        maps[name + "_dram"] = np.ascontiguousarray(x)
        aps[name] = nc.dram_tensor(name + "_dram", x.shape, mybir.dt.from_np(x.dtype), kind="ExternalInput").ap()
    aps["rowspace"] = nc.dram_tensor("rowspace_dram", (E1 * CAP + TOKENS, D), F32).ap()
    aps["results"] = nc.dram_tensor("results_dram", (E1 * CAP, D), F32).ap()
    out = nc.dram_tensor("out_dram", v["x"].shape, F32, kind="ExternalOutput").ap()
    build(nc, aps, out)
    r = run_bass_kernel_spmd(nc, [maps], core_ids=[0])
    return r.results[0]["out_dram"]
```

```python
from contextlib import ExitStack

import numpy as np

import concourse.bass as bass
from concourse import mybir

F32 = mybir.dt.float32
BF16 = mybir.dt.bfloat16
U32 = mybir.dt.uint32
ALU = mybir.AluOpType
ACT = mybir.ActivationFunctionType
AX_X = mybir.AxisListType.X

P = 128
BATCH, SEQ, D = 128, 32, 128
KEYS = 257
TOKENS = BATCH * SEQ
TILES = TOKENS // P
TPG = 4
GROUPS = TILES // TPG
GT = TPG * P
BPT = P // SEQ
HEADS, DH = 16, 8
Q4, H4 = 4, 4
QW = H4 * DH
VW = QW + H4
E0, F0 = 8, 256
E1, F1 = 8, 512
CAP = TOKENS // E1


def columns(widths):
    at, out = 0, {}
    for name, w in widths:
        out[name] = (at, w)
        at += w
    return out, at


CONST, CONST_W = columns([
    ("ident", 128), ("headcol", 4), ("minushalf", 4),
    ("quarter4", 4), ("quarter4scaled", 4), ("head4", 4), ("causal", 32),
    ("cos", 32), ("sin", 32), ("maskneg", 32), ("spread", 128), ("before", 128), ("ones", 128),
    ("keybase", 32), ("rank8", 8), ("expertbase", 8), ("tokenid", 32), ("restart", 256)])
SMALL, SMALL_W = columns([
    ("x_wqT", 128), ("x_wk", 128), ("x_wvT", 128), ("x_bq", 1), ("x_bk", 1), ("x_bv", 128),
    ("a_w", 256), ("a_bq", 1), ("a_bk", 1), ("a_wv", 128), ("a_bvh", 32), ("a_wo", 128), ("a_bo", 128),
    ("f_g", 1), ("f_b", 1), ("f_rw", 8), ("f_rb", 8), ("f_b1", 16), ("f_b2", 128),
    ("y_wqT", 128), ("y_wkrepT", 128), ("y_wvT", 8), ("y_wcT", 128),
    ("b_wqT", 128), ("b_wqsT", 128), ("b_wkT", 128), ("b_wksT", 128), ("b_wvT", 128), ("b_woT", 128),
    ("g_nw", 128), ("g_nb", 128), ("g_nwcol", 1), ("g_nbcol", 1), ("g_w", 10), ("g_rb1", 4), ("g_rb2", 128), ("g_b1", 32)])

CONST_FIRST = CONST["quarter4"][0]
SMALL_FIRST = SMALL["a_w"][0]


class Steps:

    def __init__(self, eng, sem, per):
        self.eng, self.sem, self.per = eng, sem, per

    def start(self, g):
        self.before, self.n = g * self.per, 0

    def end(self):
        assert self.n == self.per, ("steps of a group", self.n)

    def did(self, ins):
        ins.then_inc(self.sem, 1)
        self.n += 1

    def settle(self):
        self.eng.wait_ge(self.sem, self.before + self.n)


def build(nc, a, out):
    with ExitStack() as ctx:
        def sb(name, shape, dt=F32):
            return ctx.enter_context(nc.sbuf_tensor(name, shape, dt))

        def sem(name):
            return ctx.enter_context(nc.semaphore(name))

        bank = [ctx.enter_context(nc.psum_tensor(f"bank{k}", [P, 512], F32)) for k in range(8)]

        X = sb("X", [P, TILES * D])
        const = sb("const", [P, CONST_W])
        small = sb("small", [P, SMALL_W])
        Z = sb("Z", [P, TPG, D])
        zT = sb("zT", [P, GT])
        stats = sb("stats", [P, TPG, 6])
        moments = sb("moments", [P, TPG, 2])
        rstd = sb("rstd", [P, TPG])
        keysT = sb("keysT", [P, TPG, BPT * KEYS])
        variance = sb("variance", [P, TPG])
        zeros = sb("zeros", [P, D])
        rw1 = sb("rw1", [P, F1])
        rw2 = sb("rw2", [P, 4, D])
        ew1 = sb("ew1", [P, E0 * F0])
        ew2 = sb("ew2", [P, E0 * 2 * D])

        def C(name):
            at, w = CONST[name]
            return const[:, at:at + w]

        def W(name):
            at, w = SMALL[name]
            return small[:, at:at + w]

        def x_tile(i, t):
            return X[:, bass.ds(i * GT + t * D, D)]

        def x_group(i):
            return X[:, bass.ds(i * GT, GT)].rearrange("p (t d) -> p t d", t=TPG)

        loaded = sem("loaded")
        x_first = sem("x_first")
        x_loaded = sem("x_loaded")
        rest_loaded = sem("rest_loaded")
        weights_loaded = sem("weights_loaded")
        first_keys_loaded = sem("first_keys_loaded")
        residual_loaded = sem("residual_loaded")
        x_out = sem("x_out")
        zeros_ready = sem("zeros_ready")
        places_cleared = sem("places_cleared")

        norms = [0]
        stage_sems = []

        def stage_sem(name):
            stage_sems.append(nc.alloc_semaphore(name))
            return stage_sems[-1]

        moments_ready = sem("moments_ready")
        variance_ready = sem("variance_ready")
        rstd_ready = sem("rstd_ready")

        def wait_alone(eng, s, value):
            eng.wait_ge(s, value)
            eng.nop(nofuse=True)

        def layernorm_moments(dve, steps, source):
            for t in range(TPG):
                steps.did(nc.vector.bn_stats(out=stats[:, t, :], in_=source(t)))
            for t in range(TPG):
                if t == 0:
                    steps.settle()
                    dve.nop(nofuse=True)
                ins = nc.vector.bn_aggr(out=moments[:, t, :], in_=stats[:, t, :])
                if t < TPG - 1:
                    steps.did(ins)
            ins.then_inc(moments_ready, 1)

        def layernorm_output(dve, n, source, target, target_free, done):
            dve.wait_ge(rstd_ready, n + 1)
            target_free()
            for t in range(TPG):
                nc.vector.tensor_scalar(target(t), source(t), moments[:, t, 0:1], rstd[:, t:t + 1],
                                        ALU.subtract, ALU.mult).then_inc(done, 1)

        def layernorm(dve, steps, n, source, target, target_free, done):
            layernorm_moments(dve, steps, source)
            layernorm_output(dve, n, source, target, target_free, done)

        def layernorm_rstd(pool, n, eps):
            wait_alone(pool, moments_ready, n + 1)
            nc.gpsimd.tensor_scalar(variance[:, :], moments[:, :, 1], eps, None, ALU.add).then_inc(variance_ready, 1)
            pool.wait_ge(variance_ready, n + 1)
            nc.gpsimd.tensor_tensor(rstd[:, :], variance[:, :], C("minushalf"), ALU.pow).then_inc(rstd_ready, 1)

        attention_buffers = ExitStack()

        def shared(name, shape, dt=F32):
            return attention_buffers.enter_context(nc.sbuf_tensor(name, shape, dt))

        QX = shared("QX", [P, 2, TPG * BPT, Q4, SEQ])
        KX = shared("KX", [P, 2, TPG * BPT, H4, SEQ])
        VX = shared("VX", [P, 2, TPG * BPT, Q4, VW])
        V = shared("V", [P, TPG * BPT, Q4, DH])
        qT = shared("qT", [P, GT])
        kT = shared("kT", [P, GT])
        spare = shared("spare", [P, GT])
        spare2 = shared("spare2", [P, GT])
        S = shared("S", [P, 2, GT])
        ST = shared("ST", [P, 2, GT])
        top16 = shared("top16", [P, TPG, HEADS])
        rsum16 = shared("rsum16", [P, TPG, HEADS])
        O = shared("O", [P, TPG, D])
        OT = shared("OT", [P, GT])
        maskneg16 = shared("maskneg16", [P, SEQ], BF16)
        spread16 = shared("spread16", [P, P], BF16)
        eps16 = 1e-6

        def batch_of(ap, t, b):
            return ap[:, t * BPT + b, :, :].rearrange("p g s -> p (g s)")

        def by_batch(ap):
            return ap.rearrange("p (b s) -> p b s", s=SEQ)

        def turns(eng, front, turn, last):
            front(0)
            turn(0, 0, True, True)
            with eng.Fori(0, (GROUPS - 4) // 2) as i:
                turn(2 * i + 1, 1, True, True)
                turn(2 * i + 2, 0, True, True)
            turn(GROUPS - 3, 1, True, True)
            turn(GROUPS - 2, 0, True, False)
            turn(GROUPS - 1, 1, False, False)
            last(GROUPS)

        class Output:

            def __init__(self, sem):
                self.o_ready = sem("o_ready")
                self.OT_ready = sem("OT_ready")
                self.OT_copied = sem("OT_copied")
                self.y_ready = sem("y_ready")
                self.x_done = sem("x_done")

            def pe_OT(self, pe, g):
                pe.wait_ge(self.o_ready, TPG * g)
                for t in range(TPG):
                    mm = nc.tensor.transpose(bank[7][:, t * P:(t + 1) * P], O[:, t, :], C("ident"))
                mm.then_inc(self.OT_ready, 1)

            def act_copy_OT(self, act, g):
                act.wait_ge(self.OT_ready, g)
                nc.scalar.copy(OT[:, :], bank[7][:, :]).then_inc(self.OT_copied, 1)

            def pe_y(self, pe, g, w):
                pe.wait_ge(self.OT_copied, g)
                for t in range(TPG):
                    mm = nc.tensor.matmul(bank[7][:, t * D:(t + 1) * D], OT[:, t * P:(t + 1) * P], w, start=True, stop=True)
                mm.then_inc(self.y_ready, 1)

            def dve_add(self, dve, g, bias_added=None):
                dve.wait_ge(self.y_ready, g)
                if bias_added is not None:
                    dve.wait_ge(bias_added, g)
                nc.vector.tensor_tensor(x_group(g - 1), x_group(g - 1), bank[7][:, :].rearrange("p (t d) -> p t d", d=D), ALU.add
                                        ).then_inc(self.x_done, 1)

        class Attention(Output):

            def __init__(self, sem, softmax, causal, values):
                self.softmax, self.causal, self.values = softmax, causal, values
                self.pv_banks = [bank[7]] if softmax else [bank[5], bank[6]]
                self.logits_ready = [sem(f"logits_ready{k}") for k in range(2)]
                self.logits_used = [sem(f"logits_used{k}") for k in range(2)]
                self.exp_done = sem("exp_done")
                self.ST_ready = [sem(f"ST_ready{k}") for k in range(2)]
                self.ST_copied = [sem(f"ST_copied{k}") for k in range(2)]
                self.pv_ready = sem("pv_ready")
                Output.__init__(self, sem)
                self.steps = sem("back_steps")
                self.per = TPG * 2


            def pe_logits(self, pe, g, s, t):
                k, out_ = t % 2, bank[3 + t % 2]
                pe.wait_ge(self.logits_used[k], 2 * g + t // 2)
                if self.softmax:
                    if self.causal:
                        nc.tensor.matmul(out_[:, :], spread16[0:SEQ, :],
                                         maskneg16[0:SEQ, :].unsqueeze(1).to_broadcast([SEQ, HEADS, SEQ]),
                                         start=True, stop=True, skip_group_check=True)
                    for b in range(BPT):
                        mm = nc.tensor.matmul(out_[:, b * P:(b + 1) * P], batch_of(QX[:, s], t, b), batch_of(KX[:, s], t, b),
                                              start=not self.causal, stop=True, skip_group_check=True)
                else:
                    for b in range(BPT):
                        mm = nc.tensor.matmul(out_[:, b * P:(b + 1) * P], batch_of(KX[:, s], t, b), batch_of(QX[:, s], t, b),
                                              start=True, stop=True)
                mm.then_inc(self.logits_ready[k], 1)

            def dve_weigh(self, dve, steps, g, t):
                k, in_ = t % 2, bank[3 + t % 2]
                dve.wait_ge(self.logits_ready[k], 2 * g + t // 2 + 1)
                if self.softmax:
                    view = in_[:, :].rearrange("p (h m) -> p h m", m=SEQ)
                    steps.did(nc.vector.reduce_max(top16[:, t, :], view, AX_X))
                    steps.settle()
                    dve.wait_ge(self.ST_ready[k], 2 * g + t // 2)
                    nc.vector.tensor_tensor(S[:, k, :].rearrange("p (h m) -> p h m", m=SEQ), view,
                                            top16[:, t, :].unsqueeze(2).to_broadcast([P, HEADS, SEQ]), ALU.subtract
                                            ).then_inc(self.logits_used[k], 1)
                else:
                    if t >= 2 or not is_first(g):
                        dve.wait_ge(self.pv_ready, TPG * g + t - 1)
                    nc.vector.tensor_tensor(ST[:, k, :].rearrange("p (g l) -> p g l", l=SEQ),
                                            in_[:, :].rearrange("p (g l) -> p g l", l=SEQ),
                                            C("causal").unsqueeze(1).to_broadcast([P, HEADS, SEQ]), ALU.mult
                                            ).then_inc(self.logits_used[k], 1)

            def act_exp(self, act, g, t):
                k = t % 2
                act.wait_ge(self.logits_used[k], 2 * g + t // 2 + 1)
                nc.scalar.activation(S[:, k, :], S[:, k, :], ACT.Exp).then_inc(self.exp_done, 1)

            def pe_transpose(self, pe, g, t):
                k, out_ = t % 2, bank[5 + t % 2]
                pe.wait_ge(self.exp_done, TPG * g + t + 1)
                pe.wait_ge(self.ST_copied[k], 2 * g + t // 2)
                for b in range(BPT):
                    mm = nc.tensor.transpose(out_[:, b * P:(b + 1) * P], S[:, k, b * P:(b + 1) * P], C("ident"))
                mm.then_inc(self.ST_ready[k], 1)

            def act_copy_ST(self, act, g, t):
                k = t % 2
                act.wait_ge(self.ST_ready[k], 2 * g + t // 2 + 1)
                if t >= 2 or not is_first(g):
                    act.wait_ge(self.pv_ready, TPG * g + t - 1)
                nc.scalar.copy(ST[:, k, :], bank[5 + k][:, :]).then_inc(self.ST_copied[k], 1)

            def pe_values(self, pe, g, s, t):
                k = t % 2
                if self.softmax:
                    pe.wait_ge(self.ST_copied[k], 2 * g + t // 2 + 1)
                else:
                    pe.wait_ge(self.logits_used[k], 2 * g + t // 2 + 1)
                n = len(self.pv_banks)
                if t >= n - 1 or not is_first(g):
                    pe.wait_ge(self.o_ready, TPG * g + t + 1 - n)
                if t == (0 if self.softmax else TPG - 1):
                    pe.wait_ge(self.x_done, g)
                for q in range(Q4):
                    for b in range(BPT):
                        at = b * P + q * SEQ
                        mm = nc.tensor.matmul(self.pv_banks[t % n][b * SEQ:(b + 1) * SEQ, q * VW:(q + 1) * VW], ST[:, k, at:at + SEQ],
                                              self.values(s, t * BPT + b, q), start=True, stop=True)
                mm.then_inc(self.pv_ready, 1)

            def dve_normalise(self, dve, steps, g, t):
                pv = self.pv_banks[t % len(self.pv_banks)][:, 0:Q4 * VW].rearrange("p (q w) -> p q w", w=VW)
                dve.wait_ge(self.pv_ready, TPG * g + t + 1)
                if t == 0:
                    dve.wait_ge(self.OT_ready, g)
                rsum = rsum16[:, t, :].rearrange("p (q h) -> p q h", h=H4)
                if self.softmax:
                    steps.did(nc.vector.reciprocal(rsum, pv[:, :, QW:VW]))
                else:
                    steps.did(nc.vector.tensor_scalar(rsum, pv[:, :, QW:VW], eps16, None, ALU.add))
                    steps.settle()
                    steps.did(nc.vector.reciprocal(rsum, rsum))
                steps.settle()
                nc.vector.tensor_tensor(O[:, t, :].rearrange("p (q h d) -> p q h d", q=Q4, h=H4),
                                        pv[:, :, 0:QW].rearrange("p q (h d) -> p q h d", d=DH),
                                        rsum.unsqueeze(3).to_broadcast([P, Q4, H4, DH]), ALU.mult).then_inc(self.o_ready, 1)

        def is_first(g):
            return isinstance(g, int) and g == 0

        def pe_zT(pe, g, z_ready, bank_read, zT_ready, z=Z):
            pe.wait_ge(z_ready, TPG * g + TPG)
            pe.wait_ge(bank_read, g)
            for t in range(TPG):
                mm = nc.tensor.transpose(bank[0][:, t * P:(t + 1) * P], z[:, t, :], C("ident"))
            mm.then_inc(zT_ready, 1)

        def pe_values_of_batches(z, w, width):
            for b in range(TPG * BPT):
                for h in range(H4):
                    at = h * QW if width == QW else 0
                    mm = nc.tensor.matmul(bank[1][h * SEQ:(h + 1) * SEQ, b * width:(b + 1) * width],
                                          z[:, b * SEQ:(b + 1) * SEQ], w[:, at:at + width], start=True, stop=True)
            return mm

        def spread_values(eng, s, done):
            eng.tensor_tensor(VX[:, s, :, :, 0:QW].rearrange("p b q (h d) -> p (b q) h d", d=DH),
                              V[:, :, :, :].rearrange("p b q d -> p (b q) d").unsqueeze(2).to_broadcast([P, TPG * BPT * Q4, H4, DH]),
                              C("headcol").unsqueeze(1).unsqueeze(3).to_broadcast([P, TPG * BPT * Q4, H4, DH]),
                              ALU.mult).then_inc(done, 1)

        def act_spread_queries(s, q, mask, done):
            nc.scalar.activation(QX[:, s, :, q, :], by_batch(qT[:, :]), ACT.Copy, scale=C(mask)[:, q:q + 1]).then_inc(done, 1)

        def act_spread_keys(s, source, h, done):
            nc.scalar.activation(KX[:, s, :, h, :], by_batch(source[:, :]), ACT.Copy, scale=C("head4")[:, h:h + 1]
                                 ).then_inc(done, 1)

        def cross_attention_0():
            norm0 = norms[0]
            norms[0] += GROUPS
            with ExitStack() as mine:
                def sb(name, shape, dt=F32):
                    return mine.enter_context(nc.sbuf_tensor("c0_" + name, shape, dt))

                def sem(name):
                    return stage_sem("c0_" + name)

                att = Output(sem)
                keysN = sb("keysN", [P, TPG, BPT, 2, D])
                lastkeys = sb("lastkeys", [1, TPG * BPT * D])
                qT2 = sb("qT2", [P, 2, GT])
                qkT = sb("qkT", [P, 2, GT])
                probs = sb("probs", [P, 2, KEYS])
                probsT = sb("probsT", [P, 2, 2, P])
                lastprobT = sb("lastprobT", [1, 2, P])
                top = sb("top", [P, TPG])
                shift = sb("shift", [P, TPG])
                total = sb("total", [P, TPG])
                rtotal = sb("rtotal", [P, TPG])

                z_ready, zT_ready, zT_copied = sem("z_ready"), sem("zT_ready"), sem("zT_copied")
                q_ready, q_copied, qk_ready, qk_copied = (sem(n) for n in ("q_ready", "q_copied", "qk_ready", "qk_copied"))
                bias_added = sem("bias_added")
                keysT_loaded = [sem(f"keysT_loaded{t}") for t in range(TPG)]
                keysN_loaded = [sem(f"keysN_loaded{t}") for t in range(TPG)]
                lastkeys_loaded = sem("lastkeys_loaded")
                scores_ready = [sem(f"scores_ready{t}") for t in range(TPG)]
                shift_ready = sem("shift_ready")
                exp_done = [sem(f"exp_done{k}") for k in range(2)]
                probsT_ready = [sem(f"probsT_ready{k}") for k in range(2)]
                probsT_copied = [sem(f"probsT_copied{k}") for k in range(2)]
                tile_attended = [sem(f"tile_attended{t}") for t in range(TPG)]
                front_steps, back_steps = sem("front_steps"), sem("back_steps")

                scores_bank, probsT_bank = [bank[2], bank[3]], [bank[4], bank[5]]

                with nc.Block() as block:
                    @block.sync
                    def _(sp):
                        def load(g):
                            if not is_first(g):
                                sp.wait_ge(tile_attended[TPG - 1], g)
                            sp.dma_start(lastkeys[:, :], a["lastkeys"][:, bass.ds(g * (GT // SEQ * D), GT // SEQ * D)]
                                         ).then_inc(lastkeys_loaded, 16)

                        def load_tile(g, t):
                            b0 = g * (TPG * BPT) + t * BPT
                            if not is_first(g):
                                sp.wait_ge(scores_ready[t], g)
                            sp.dma_start(keysT[:, t, :], a["ctxT"][:, bass.ds(b0 * KEYS, BPT * KEYS)]
                                         ).then_inc(keysT_loaded[t], 16)
                            if not is_first(g):
                                sp.wait_ge(tile_attended[t], g)
                            sp.dma_start(keysN[:, t, :, :, :].rearrange("p j c d -> p (j c d)"),
                                         a["ctxN"][:, bass.ds(b0 * (2 * D), BPT * 2 * D)]
                                         ).then_inc(keysN_loaded[t], 16)

                        for t in range(TPG):
                            load_tile(0, t)
                            if t == 0:
                                sp.dma_start(X[:, GT:], a["xt"][:, GT:]).then_inc(x_loaded, 16)
                                load(0)
                        with sp.Fori(1, GROUPS) as g:
                            for t in range(TPG):
                                load_tile(g, t)
                            load(g)
                        sp.dma_start(const[:, CONST_FIRST:], a["const"][:, CONST_FIRST:]).then_inc(rest_loaded, 16)
                        sp.dma_start(small[:, SMALL_FIRST:], a["small"][:, SMALL_FIRST:]).then_inc(rest_loaded, 16)
                        sp.dma_start(ew1[:, :], a["f_w1"][:, :]).then_inc(weights_loaded, 16)
                        sp.dma_start(ew2[:, :], a["f_w2"][:, :]).then_inc(weights_loaded, 16)
                        sp.wait_ge(rest_loaded, 32)

                    @block.tensor
                    def _(pe):
                        def query(g, s):
                            pe.wait_ge(zT_copied, g + 1)
                            pe.wait_ge(qk_copied, g)
                            nc.tensor.matmul(bank[1][:, :], W("x_wqT"), zT[:, :], start=True, stop=True).then_inc(q_ready, 1)

                        def query_key(g, s):
                            pe.wait_ge(q_copied, g + 1)
                            nc.tensor.matmul(bank[1][:, :], W("x_wk"), qT2[:, s, :], start=True, stop=True).then_inc(qk_ready, 1)

                        def scores(g, s, t):
                            b = scores_bank[t % 2]
                            if t == 0:
                                pe.wait_ge(qk_copied, g + 1)
                            pe.wait_ge(keysT_loaded[t], 16 * g + 16)
                            pe.wait_ge(exp_done[t % 2], 2 * g + t // 2)
                            for j in range(BPT):
                                at = t * P + j * SEQ
                                nc.tensor.matmul(b[j * SEQ:(j + 1) * SEQ, 0:KEYS], qkT[:, s, at:at + SEQ],
                                                 keysT[:, t, j * KEYS:(j + 1) * KEYS], start=True, stop=True)
                            nc.tensor.matmul(b[:, KEYS:KEYS + 1], qT2[:, s, t * P:(t + 1) * P], W("x_bk"),
                                             start=True, stop=True).then_inc(scores_ready[t], 1)

                        def transpose_probs(g, t):
                            b = probsT_bank[t % 2]
                            pe.wait_ge(exp_done[t % 2], 2 * g + t // 2 + 1)
                            pe.wait_ge(probsT_copied[t % 2], 2 * g + t // 2)
                            for c in range(2):
                                nc.tensor.transpose(b[:, c * P:(c + 1) * P], probs[:, t % 2, c * P:(c + 1) * P], C("ident"))
                            nc.tensor.transpose(b[0:1, 2 * P:3 * P], probs[:, t % 2, KEYS - 1:KEYS], C("ident")
                                                ).then_inc(probsT_ready[t % 2], 1)

                        def attend(g, t):
                            pe.wait_ge(probsT_copied[t % 2], 2 * g + t // 2 + 1)
                            pe.wait_ge(keysN_loaded[t], 16 * g + 16)
                            if t == 0:
                                pe.wait_ge(lastkeys_loaded, 16 * g + 16)
                            pe.wait_ge(att.o_ready, TPG * g + t)
                            for c in range(3):
                                for j in range(BPT):
                                    now = slice(j * SEQ, (j + 1) * SEQ)
                                    if c < 2:
                                        ps, ks = probsT[:, t % 2, c, now], keysN[:, t, j, c, :]
                                    else:
                                        at = (t * BPT + j) * D
                                        ps, ks = lastprobT[:, t % 2, now], lastkeys[:, at:at + D]
                                    mm = nc.tensor.matmul(bank[6][now, 0:D], ps, ks, start=(c == 0), stop=(c == 2),
                                                          skip_group_check=True)
                            mm.then_inc(tile_attended[t], 1)

                        def front(g):
                            pe_zT(pe, g, z_ready, zT_copied, zT_ready)
                            query(g, 0)
                            query_key(g, 0)

                        def turn(g, s, more, ahead):
                            scores(g, s, 0)
                            scores(g, s, 1)
                            if not is_first(g):
                                att.pe_OT(pe, g)
                            if more:
                                pe_zT(pe, g + 1, z_ready, zT_copied, zT_ready)
                            transpose_probs(g, 0)
                            scores(g, s, 2)
                            if more:
                                query(g + 1, 1 - s)
                            if not is_first(g):
                                att.pe_y(pe, g, W("x_wvT"))
                            transpose_probs(g, 1)
                            attend(g, 0)
                            scores(g, s, 3)
                            transpose_probs(g, 2)
                            if more:
                                query_key(g + 1, 1 - s)
                            attend(g, 1)
                            transpose_probs(g, 3)
                            attend(g, 2)
                            attend(g, 3)
                            if not is_first(g):
                                pe.wait_ge(att.x_done, g)

                        def last(g):
                            att.pe_OT(pe, g)
                            att.pe_y(pe, g, W("x_wvT"))

                        pe.wait_ge(loaded, 32)
                        turns(pe, front, turn, last)

                    @block.scalar
                    def _(act):
                        def copy_zT(g):
                            act.wait_ge(zT_ready, g + 1)
                            act.wait_ge(q_ready, g)
                            nc.scalar.copy(zT[:, :], bank[0][:, :]).then_inc(zT_copied, 1)

                        def copy_q(g, s):
                            act.wait_ge(q_ready, g + 1)
                            if not is_first(g):
                                act.wait_ge(scores_ready[TPG - 1], g - 1)
                            nc.scalar.activation(qT2[:, s, :], bank[1][:, :], ACT.Identity, bias=W("x_bq")).then_inc(q_copied, 1)

                        def copy_qk(g, s):
                            act.wait_ge(qk_ready, g + 1)
                            nc.scalar.copy(qkT[:, s, :], bank[1][:, :]).then_inc(qk_copied, 1)

                        def exponential(g, t):
                            act.wait_ge(shift_ready, TPG * g + t + 1)
                            act.wait_ge(probsT_ready[t % 2], 2 * g + t // 2)
                            nc.scalar.activation(probs[:, t % 2, :], scores_bank[t % 2][:, 0:KEYS], ACT.Exp,
                                                 bias=shift[:, t:t + 1], accum_out=total[:, t:t + 1]
                                                 ).then_inc(exp_done[t % 2], 1)

                        def copy_probsT(g, t):
                            act.wait_ge(probsT_ready[t % 2], 2 * g + t // 2 + 1)
                            if t >= 2:
                                act.wait_ge(tile_attended[t - 2], g + 1)
                            elif not is_first(g):
                                act.wait_ge(tile_attended[t + 2], g)
                            nc.scalar.copy(lastprobT[:, t % 2, :], probsT_bank[t % 2][0:1, 2 * P:3 * P])
                            nc.scalar.copy(probsT[:, t % 2, :, :],
                                           probsT_bank[t % 2][:, 0:2 * P].rearrange("p (c k) -> p c k", c=2)
                                           ).then_inc(probsT_copied[t % 2], 1)

                        def front(g):
                            copy_zT(g)
                            copy_q(g, 0)
                            copy_qk(g, 0)

                        def turn(g, s, more, ahead):
                            exponential(g, 0)
                            if more:
                                copy_zT(g + 1)
                            exponential(g, 1)
                            if not is_first(g):
                                att.act_copy_OT(act, g)
                            exponential(g, 2)
                            copy_probsT(g, 0)
                            copy_probsT(g, 1)
                            if more:
                                copy_q(g + 1, 1 - s)
                                copy_qk(g + 1, 1 - s)
                            exponential(g, 3)
                            copy_probsT(g, 2)
                            copy_probsT(g, 3)

                        act.wait_ge(loaded, 32)
                        turns(act, front, turn, lambda g: att.act_copy_OT(act, g))

                    @block.vector
                    def _(dve):
                        fsteps = Steps(dve, front_steps, 7)
                        bsteps = Steps(dve, back_steps, 2 * TPG)

                        def moments_of_x(g):
                            fsteps.start(g)
                            layernorm_moments(dve, fsteps, lambda t: x_tile(g, t))
                            fsteps.end()

                        def normalise_x(g):
                            layernorm_output(dve, norm0 + g, lambda t: x_tile(g, t), lambda t: Z[:, t, :],
                                             lambda: dve.wait_ge(zT_ready, g), z_ready)

                        def find_shift(g, t):
                            b = scores_bank[t % 2]
                            dve.wait_ge(scores_ready[t], g + 1)
                            bsteps.did(nc.vector.reduce_max(top[:, t:t + 1], b[:, 0:KEYS], AX_X))
                            bsteps.settle()
                            nc.vector.scalar_tensor_tensor(
                                out=shift[:, t:t + 1], in0=top[:, t:t + 1], scalar=b[:, KEYS:KEYS + 1],
                                in1=b[:, KEYS:KEYS + 1], op0=ALU.add, op1=ALU.subtract, reverse1=True
                            ).then_inc(shift_ready, 1)

                        def normalise(g, t):
                            dve.wait_ge(tile_attended[t], g + 1)
                            dve.wait_ge(exp_done[t % 2], 2 * g + t // 2 + 1)
                            if t == 0:
                                dve.wait_ge(att.OT_ready, g)
                            bsteps.did(nc.vector.reciprocal(rtotal[:, t:t + 1], total[:, t:t + 1]))
                            bsteps.settle()
                            nc.vector.tensor_scalar(O[:, t, :], bank[6][:, 0:D], rtotal[:, t:t + 1], None, ALU.mult
                                                    ).then_inc(att.o_ready, 1)

                        def turn(g, s, more, ahead):
                            bsteps.start(g)
                            find_shift(g, 0)
                            find_shift(g, 1)
                            if ahead:
                                moments_of_x(g + 2)
                            find_shift(g, 2)
                            if ahead:
                                normalise_x(g + 2)
                            normalise(g, 0)
                            find_shift(g, 3)
                            if not is_first(g):
                                att.dve_add(dve, g, bias_added)
                            normalise(g, 1)
                            normalise(g, 2)
                            normalise(g, 3)
                            bsteps.end()

                        dve.wait_ge(x_first, 16)
                        dve.wait_ge(loaded, 32)
                        moments_of_x(0)
                        normalise_x(0)
                        for s in range(2):
                            nc.vector.tensor_copy(VX[:, s, :, :, QW:VW].rearrange("p b q w -> p (b q) w"),
                                                  C("headcol").unsqueeze(1).to_broadcast([P, TPG * BPT * Q4, H4]))
                        dve.wait_ge(x_loaded, 16)
                        moments_of_x(1)
                        normalise_x(1)
                        turns(dve, lambda g: None, turn, lambda g: att.dve_add(dve, g, bias_added))

                    @block.gpsimd
                    def _(pool):
                        def front(g):
                            layernorm_rstd(pool, norm0 + g, 1e-5)
                            pool.wait_ge(z_ready, TPG * g + TPG)
                            nc.gpsimd.tensor_tensor(x_group(g), x_group(g), W("x_bv").unsqueeze(1).to_broadcast([P, TPG, D]),
                                                    ALU.add).then_inc(bias_added, 1)

                        pool.wait_ge(loaded, 32)
                        front(0)
                        turns(pool, lambda g: front(1), lambda g, s, more, ahead: front(g + 2) if ahead else None, lambda g: None)

        def linear_attention():
            norm0 = norms[0]
            norms[0] += GROUPS
            with ExitStack() as mine:
                def sem(name):
                    return stage_sem("l0_" + name)

                att = Attention(sem, softmax=False, causal=True, values=lambda s, b, q: VX[:, s, b, q, :])
                z_ready, zT_ready, zT_copied = (sem(n) for n in ("z_ready", "zT_ready", "zT_copied"))
                v_ready, v_copied = sem("v_ready"), sem("v_copied")
                proj_ready = [sem(f"proj_ready{k}") for k in range(2)]
                proj_used = [sem(f"proj_used{k}") for k in range(2)]
                below_ready, exp_ready, qT_ready, kT_ready = (sem(n) for n in (
                    "below_ready", "exp_ready", "qT_ready", "kT_ready"))
                KX_ready, VX_ready, QX_ready = sem("KX_ready"), sem("VX_ready"), sem("QX_ready")
                front_steps = sem("front_steps")
                bias_added = sem("bias_added")

                with nc.Block() as block:
                    @block.tensor
                    def _(pe):
                        def project(g):
                            pe.wait_ge(zT_copied, g + 1)
                            for k in range(2):
                                if k == 0:
                                    pe.wait_ge(v_copied, g)
                                else:
                                    pe.wait_ge(proj_used[k], g)
                                nc.tensor.matmul(bank[1 + k][:, :], W("a_w")[:, k * D:(k + 1) * D], zT[:, :],
                                                 start=True, stop=True).then_inc(proj_ready[k], 1)

                        def values(g):
                            pe.wait_ge(proj_used[0], g + 1)
                            pe_values_of_batches(zT, W("a_wv"), QW).then_inc(v_ready, 1)

                        def front(g):
                            pe_zT(pe, g, z_ready, zT_copied, zT_ready)
                            project(g)
                            values(g)

                        def turn(g, s, more, ahead):
                            pe.wait_ge(QX_ready, Q4 * g + Q4)
                            pe.wait_ge(KX_ready, H4 * g + H4)
                            att.pe_logits(pe, g, s, 0)
                            if more:
                                pe_zT(pe, g + 1, z_ready, zT_copied, zT_ready)
                            att.pe_logits(pe, g, s, 1)
                            if not is_first(g):
                                att.pe_OT(pe, g)
                            if more:
                                project(g + 1)
                            if not is_first(g):
                                att.pe_y(pe, g, W("a_wo"))
                            pe.wait_ge(VX_ready, g + 1)
                            att.pe_values(pe, g, s, 0)
                            att.pe_logits(pe, g, s, 2)
                            att.pe_values(pe, g, s, 1)
                            if more:
                                values(g + 1)
                            att.pe_logits(pe, g, s, 3)
                            att.pe_values(pe, g, s, 2)
                            att.pe_values(pe, g, s, 3)

                        def last(g):
                            att.pe_OT(pe, g)
                            att.pe_y(pe, g, W("a_wo"))

                        turns(pe, front, turn, last)

                    @block.scalar
                    def _(act):
                        def front_1(g):
                            act.wait_ge(zT_ready, g + 1)
                            act.wait_ge(v_ready, g)
                            nc.scalar.copy(zT[:, :], bank[0][:, :]).then_inc(zT_copied, 1)

                        def front_2(g):
                            act.wait_ge(proj_ready[0], g + 1)
                            act.wait_ge(QX_ready, Q4 * g)
                            nc.scalar.activation(qT[:, :], bank[1][:, :], ACT.Identity, bias=W("a_bq")).then_inc(proj_used[0], 1)
                            act.wait_ge(proj_ready[1], g + 1)
                            act.wait_ge(KX_ready, H4 * g)
                            nc.scalar.activation(kT[:, :], bank[2][:, :], ACT.Identity, bias=W("a_bk")).then_inc(proj_used[1], 1)

                        def front_3(g):
                            act.wait_ge(below_ready, 2 * g + 1)
                            nc.scalar.activation(spare[:, :], spare[:, :], ACT.Exp).then_inc(exp_ready, 1)
                            act.wait_ge(below_ready, 2 * g + 2)
                            nc.scalar.activation(spare2[:, :], spare2[:, :], ACT.Exp).then_inc(exp_ready, 1)

                        def front_4(g, s):
                            act.wait_ge(qT_ready, g + 1)
                            if not is_first(g):
                                act.wait_ge(att.OT_ready, g - 1)
                            for q in range(Q4):
                                act_spread_queries(s, q, "quarter4", QX_ready)
                            act.wait_ge(kT_ready, g + 1)
                            for h in range(H4):
                                act_spread_keys(s, kT, h, KX_ready)

                        def front(g, s=0):
                            front_1(g)
                            front_2(g)
                            front_3(g)
                            front_4(g, s)

                        def turn(g, s, more, ahead):
                            if more:
                                front_1(g + 1)
                            if not is_first(g):
                                att.act_copy_OT(act, g)
                            if more:
                                front_2(g + 1)
                                front_3(g + 1)
                                front_4(g + 1, 1 - s)

                        turns(act, front, turn, lambda g: att.act_copy_OT(act, g))

                    @block.vector
                    def _(dve):
                        fsteps = Steps(dve, front_steps, 7)
                        bsteps = Steps(dve, att.steps, att.per)
                        def moments_of_x(g):
                            fsteps.start(g)
                            layernorm_moments(dve, fsteps, lambda t: x_tile(g, t))
                            fsteps.end()

                        def normalise_x(g):
                            layernorm_output(dve, norm0 + g, lambda t: x_tile(g, t), lambda t: Z[:, t, :],
                                             lambda: dve.wait_ge(zT_ready, g), z_ready)

                        def front_2(g, s):
                            for k, (x_, low) in enumerate(((qT, spare), (kT, spare2))):
                                dve.wait_ge(proj_used[k], g + 1)
                                nc.vector.tensor_scalar(low[:, :], x_[:, :], 0.0, None, ALU.min).then_inc(below_ready, 1)

                        def front_3(g, s):
                            for k, (x_, low, done) in enumerate(((qT, spare, qT_ready), (kT, spare2, kT_ready))):
                                dve.wait_ge(exp_ready, 2 * g + k + 1)
                                nc.vector.scalar_tensor_tensor(out=x_[:, :], in0=x_[:, :], scalar=0.0, in1=low[:, :],
                                                               op0=ALU.max, op1=ALU.add).then_inc(done, 1)

                        def front_4(g):
                            dve.wait_ge(v_ready, g + 1)
                            dve.wait_ge(VX_ready, g)
                            nc.vector.tensor_tensor(V[:, :, :, :].rearrange("p b q d -> p b (q d)"),
                                                    bank[1][:, :].rearrange("p (b w) -> p b w", w=QW),
                                                    W("a_bvh").unsqueeze(1).to_broadcast([P, TPG * BPT, QW]), ALU.add
                                                    ).then_inc(v_copied, 1)

                        def front(g):
                            moments_of_x(g)
                            normalise_x(g)
                            front_2(g, 0)
                            front_3(g, 0)
                            front_4(g)
                            moments_of_x(g + 1)
                            normalise_x(g + 1)

                        def turn(g, s, more, ahead):
                            bsteps.start(g)
                            att.dve_weigh(dve, bsteps, g, 1)
                            att.dve_weigh(dve, bsteps, g, 0)
                            if more:
                                front_2(g + 1, 1 - s)
                            if not is_first(g):
                                att.dve_add(dve, g, bias_added)
                            att.dve_normalise(dve, bsteps, g, 0)
                            if more:
                                front_3(g + 1, 1 - s)
                            att.dve_weigh(dve, bsteps, g, 2)
                            if ahead:
                                moments_of_x(g + 2)
                            if more:
                                front_4(g + 1)
                            att.dve_normalise(dve, bsteps, g, 1)
                            att.dve_weigh(dve, bsteps, g, 3)
                            if ahead:
                                normalise_x(g + 2)
                            att.dve_normalise(dve, bsteps, g, 2)
                            att.dve_normalise(dve, bsteps, g, 3)
                            bsteps.end()

                        turns(dve, front, turn, lambda g: att.dve_add(dve, g, bias_added))

                    @block.gpsimd
                    def _(pool):
                        def normalise(g):
                            layernorm_rstd(pool, norm0 + g, 1e-5)

                        def add_bias(g):
                            pool.wait_ge(z_ready, TPG * g + TPG)
                            nc.gpsimd.tensor_tensor(x_group(g), x_group(g), W("a_bo").unsqueeze(1).to_broadcast([P, TPG, D]),
                                                    ALU.add).then_inc(bias_added, 1)

                        def values(g, s):
                            if not is_first(g):
                                pool.wait_ge(att.OT_ready, g - 1)
                            pool.wait_ge(v_copied, g + 1)
                            spread_values(nc.gpsimd, s, VX_ready)

                        def first(g):
                            normalise(g)
                            values(g, 0)
                            normalise(g + 1)
                            add_bias(g)
                            add_bias(g + 1)

                        def turn(g, s, more, ahead):
                            if ahead:
                                normalise(g + 2)
                            if more:
                                values(g + 1, 1 - s)
                            if ahead:
                                add_bias(g + 2)

                        turns(pool, first, turn, lambda g: None)

        def experts_0():
            norm0 = norms[0]
            norms[0] += 2 * GROUPS
            with ExitStack() as mine:
                def sb(name, shape, dt=F32):
                    return mine.enter_context(nc.sbuf_tensor("f0_" + name, shape, dt))

                def sem(name):
                    return stage_sem("f0_" + name)

                Z2 = sb("Z2", [P, TPG, D])
                zT2 = sb("zT2", [P, 2, GT])
                hidden = sb("hidden", [P, 4, 2, GT])
                prob = sb("prob", [P, TPG, E0])
                left = sb("left", [P, TPG, E0])
                hit = sb("hit", [P, TPG, E0])
                first = sb("first", [P, TPG, E0])
                second = sb("second", [P, TPG, E0])
                share = sb("share", [P, 2, TPG, E0])
                shareT = sb("shareT", [E0, GT])
                one = sb("one", [P, TPG])

                z_ready, z2_ready, zT_ready, zT_copied = sem("z_ready"), sem("z2_ready"), sem("zT_ready"), sem("zT_copied")
                residual_added = sem("residual_added")
                route_ready, low_ready, exp_done = sem("route_ready"), sem("low_ready"), sem("exp_done")
                share_ready, shareT_ready, shareT_copied = sem("share_ready"), sem("shareT_ready"), sem("shareT_copied")
                bias_ready, bias_used = sem("bias_ready"), sem("bias_used")
                up_ready = [sem(f"up_ready{f}") for f in range(2)]
                gelu_done = [sem(f"gelu_done{f}") for f in range(2)]
                down_ready = [sem(f"down_ready{k}") for k in range(2)]
                down_used = [sem(f"down_used{k}") for k in range(2)]
                front_steps = sem("front_steps")

                def spread8(v):
                    return v.unsqueeze(2).to_broadcast([P, TPG, E0])


                with nc.Block() as block:
                    @block.sync
                    def _(sp):
                        sp.wait_ge(zeros_ready, 1)
                        sp.dma_start(a["rowspace"][0:E1 * CAP, :].rearrange("(p r) d -> p r d", p=P),
                                     zeros[:, :].unsqueeze(1).to_broadcast([P, E1 * CAP // P, D])).then_inc(places_cleared, 16)
                        for t in range(TPG):
                            sp.dma_start(keysT[:, t, :], a["ctxT"][:, t * (BPT * KEYS):(t + 1) * (BPT * KEYS)]
                                         ).then_inc(first_keys_loaded, 16)
                        sp.wait_ge(places_cleared, 16)

                    @block.tensor
                    def _(pe):
                        def route(g, s):
                            pe.wait_ge(zT_copied, g + 1)
                            pe.wait_ge(bias_used, g)
                            for t in range(TPG):
                                mm = nc.tensor.matmul(bank[1][:, t * E0:(t + 1) * E0], zT2[:, s, t * P:(t + 1) * P], W("f_rw"),
                                                      start=True, stop=True)
                            mm.then_inc(route_ready, 1)

                        def transpose_shares(g, s):
                            pe.wait_ge(share_ready, g + 1)
                            for t in range(TPG):
                                mm = nc.tensor.transpose(bank[1][0:E0, t * P:(t + 1) * P], share[:, s, t, :], C("ident"))
                            mm.then_inc(shareT_ready, 1)

                        def bias(g):
                            pe.wait_ge(shareT_copied, g + 1)
                            for t in range(TPG):
                                mm = nc.tensor.matmul(bank[1][:, t * D:(t + 1) * D], shareT[:, t * P:(t + 1) * P],
                                                      W("f_b2")[0:E0, :], start=True, stop=True)
                            mm.then_inc(bias_ready, 1)

                        def up(g, s, e):
                            if e == 0:
                                pe.wait_ge(zT_copied, g + 1)
                            for f in range(2):
                                if e >= 2 or not is_first(g):
                                    pe.wait_ge(gelu_done[f], E0 * g + e - 1)
                                at = e * F0 + f * P
                                nc.tensor.matmul(bank[2 + 2 * (e % 2) + f][:, :], ew1[:, at:at + P], zT2[:, s, :],
                                                 start=True, stop=True).then_inc(up_ready[f], 1)

                        def down(g, e):
                            k = e % 2
                            for f in range(2):
                                pe.wait_ge(gelu_done[f], E0 * g + e + 1)
                            pe.wait_ge(down_used[k], E0 // 2 * g + e // 2)
                            for t in range(TPG):
                                for f in range(2):
                                    at = (2 * e + f) * D
                                    mm = nc.tensor.matmul(bank[6 + k][:, t * D:(t + 1) * D],
                                                          hidden[:, e % 4, f, t * P:(t + 1) * P], ew2[:, at:at + D],
                                                          start=(f == 0), stop=(f == 1))
                            mm.then_inc(down_ready[k], 1)

                        def front(g):
                            pe_zT(pe, g, z2_ready, zT_copied, zT_ready, Z2)
                            route(g, 0)
                            pe.wait_ge(weights_loaded, 32)
                            up(g, 0, 0)
                            up(g, 0, 1)
                            transpose_shares(g, 0)

                        def turn(g, s, more, ahead):
                            for e in range(E0):
                                if e + 2 < E0:
                                    up(g, s, e + 2)
                                elif more:
                                    up(g + 1, 1 - s, e + 2 - E0)
                                down(g, e)
                                if e == 1:
                                    bias(g)
                                if more:
                                    if e == 2:
                                        pe_zT(pe, g + 1, z2_ready, zT_copied, zT_ready, Z2)
                                    if e == 3:
                                        route(g + 1, 1 - s)
                                    if e == 7:
                                        transpose_shares(g + 1, 1 - s)

                        turns(pe, front, turn, lambda g: None)

                    @block.scalar
                    def _(act):
                        def copy_zT(g, s):
                            act.wait_ge(zT_ready, g + 1)
                            if not is_first(g):
                                act.wait_ge(up_ready[1], E0 * (g - 1))
                            nc.scalar.activation(zT2[:, s, :], bank[0][:, :], ACT.Identity, bias=W("f_b"), scale=W("f_g")
                                                 ).then_inc(zT_copied, 1)

                        def exponential(g):
                            act.wait_ge(low_ready, g + 1)
                            nc.scalar.activation(prob[:, :, :], prob[:, :, :], ACT.Exp).then_inc(exp_done, 1)

                        def copy_shareT(g):
                            act.wait_ge(shareT_ready, g + 1)
                            act.wait_ge(bias_ready, g)
                            nc.scalar.copy(shareT[:, :], bank[1][0:E0, :]).then_inc(shareT_copied, 1)

                        def gelu(g, e):
                            for f in range(2):
                                act.wait_ge(up_ready[f], E0 * g + e + 1)
                                if e >= 4 or not is_first(g):
                                    act.wait_ge(down_ready[e % 2], E0 // 2 * g + e // 2 - 1)
                                nc.scalar.activation(hidden[:, e % 4, f, :], bank[2 + 2 * (e % 2) + f][:, :], ACT.Gelu,
                                                     bias=W("f_b1")[:, 2 * e + f:2 * e + f + 1]).then_inc(gelu_done[f], 1)

                        def front(g):
                            copy_zT(g, 0)
                            exponential(g)

                        def turn(g, s, more, ahead):
                            for e in range(E0):
                                gelu(g, e)
                                if e == 1:
                                    copy_shareT(g)
                                if more:
                                    if e == 4:
                                        copy_zT(g + 1, 1 - s)
                                    if e == 6:
                                        exponential(g + 1)

                        turns(act, front, turn, lambda g: None)

                    @block.vector
                    def _(dve):
                        steps = Steps(dve, front_steps, 14 + 2 + 3 + 10 + 1 + 5)

                        def do(ins):
                            steps.did(ins)
                            steps.settle()

                        def pick(values, to):
                            do(nc.vector.reduce_max(one[:, :], values[:, :, :], AX_X))
                            do(nc.vector.tensor_tensor(hit[:, :, :], values[:, :, :], spread8(one[:, :]), ALU.is_equal))
                            do(nc.vector.tensor_tensor(hit[:, :, :], hit[:, :, :],
                                                       C("rank8").unsqueeze(1).to_broadcast([P, TPG, E0]), ALU.mult))
                            do(nc.vector.reduce_max(one[:, :], hit[:, :, :], AX_X))
                            do(nc.vector.tensor_tensor(to[:, :, :], hit[:, :, :], spread8(one[:, :]), ALU.is_equal))

                        def moments_1(g):
                            steps.start(g)
                            layernorm_moments(dve, steps, lambda t: x_tile(g, t))

                        def output_1(g):
                            layernorm_output(dve, norm0 + 2 * g, lambda t: x_tile(g, t), lambda t: Z[:, t, :],
                                             lambda: dve.wait_ge(residual_added, g), z_ready)

                        def moments_2(g):
                            dve.wait_ge(z_ready, TPG * g + TPG)
                            layernorm_moments(dve, steps, lambda t: Z[:, t, :])

                        def output_2(g):
                            layernorm_output(dve, norm0 + 2 * g + 1, lambda t: Z[:, t, :], lambda t: Z2[:, t, :],
                                             lambda: dve.wait_ge(zT_ready, g), z2_ready)

                        def logits_less_peak(g):
                            dve.wait_ge(route_ready, g + 1)
                            do(nc.vector.tensor_tensor(prob[:, :, :], bank[1][:, 0:TPG * E0].rearrange("p (t e) -> p t e", e=E0),
                                                       W("f_rb").unsqueeze(1).to_broadcast([P, TPG, E0]), ALU.add))
                            do(nc.vector.reduce_max(one[:, :], prob[:, :, :], AX_X))
                            nc.vector.tensor_tensor(prob[:, :, :], prob[:, :, :], spread8(one[:, :]), ALU.subtract
                                                    ).then_inc(low_ready, 1)

                        def shares(g, s):
                            dve.wait_ge(exp_done, g + 1)
                            do(nc.vector.reduce_sum(one[:, :], prob[:, :, :], AX_X))
                            do(nc.vector.reciprocal(one[:, :], one[:, :]))
                            do(nc.vector.tensor_tensor(prob[:, :, :], prob[:, :, :], spread8(one[:, :]), ALU.mult))
                            pick(prob, first)
                            do(nc.vector.scalar_tensor_tensor(out=left[:, :, :], in0=first[:, :, :], scalar=-2.0,
                                                              in1=prob[:, :, :], op0=ALU.mult, op1=ALU.add))
                            pick(left, second)
                            do(nc.vector.tensor_tensor(first[:, :, :], first[:, :, :], second[:, :, :], ALU.add))
                            do(nc.vector.tensor_tensor(first[:, :, :], first[:, :, :], prob[:, :, :], ALU.mult))
                            do(nc.vector.reduce_sum(one[:, :], first[:, :, :], AX_X))
                            do(nc.vector.tensor_scalar(one[:, :], one[:, :], 1e-8, None, ALU.max))
                            do(nc.vector.reciprocal(one[:, :], one[:, :]))
                            nc.vector.tensor_tensor(share[:, s, :, :], first[:, :, :], spread8(one[:, :]), ALU.mult
                                                    ).then_inc(share_ready, 1)
                            steps.end()

                        def add_bias(g):
                            dve.wait_ge(bias_ready, g + 1)
                            dve.wait_ge(down_used[1], E0 // 2 * g + 1)
                            nc.vector.tensor_tensor(x_group(g), x_group(g), bank[1][:, :].rearrange("p (t d) -> p t d", d=D),
                                                    ALU.add).then_inc(bias_used, 1)

                        def mix(g, s, e):
                            k = e % 2
                            dve.wait_ge(down_ready[k], E0 // 2 * g + e // 2 + 1)
                            if e == 0:
                                dve.wait_ge(residual_added, g + 1)
                                dve.wait_ge(share_ready, g + 1)
                            else:
                                dve.wait_ge(down_used[1 - k], E0 // 2 * g + (e - 1) // 2 + 1)
                            if e == 2:
                                dve.wait_ge(bias_used, g + 1)
                            for t in range(TPG):
                                ins = nc.vector.scalar_tensor_tensor(
                                    out=x_tile(g, t), in0=bank[6 + k][:, t * D:(t + 1) * D], scalar=share[:, s, t, e:e + 1],
                                    in1=x_tile(g, t), op0=ALU.mult, op1=ALU.add)
                            ins.then_inc(down_used[k], 1)

                        def front(g):
                            moments_1(g)
                            output_1(g)
                            moments_2(g)
                            output_2(g)
                            logits_less_peak(g)
                            shares(g, 0)

                        def turn(g, s, more, ahead):
                            if more:
                                moments_1(g + 1)
                            for e in range(E0):
                                mix(g, s, e)
                                if e == 1:
                                    add_bias(g)
                                if more:
                                    if e == 0:
                                        output_1(g + 1)
                                        moments_2(g + 1)
                                    if e == 1:
                                        output_2(g + 1)
                                    if e == 3:
                                        logits_less_peak(g + 1)
                                    if e == 5:
                                        shares(g + 1, 1 - s)

                        turns(dve, front, turn, lambda g: None)

                    @block.gpsimd
                    def _(pool):
                        def front(g):
                            layernorm_rstd(pool, norm0 + 2 * g, 1e-5)
                            layernorm_rstd(pool, norm0 + 2 * g + 1, 1e-5)
                            pool.wait_ge(z_ready, TPG * g + TPG)
                            nc.gpsimd.tensor_tensor(x_group(g), x_group(g), Z[:, :, :], ALU.add).then_inc(residual_added, 1)

                        turns(pool, front, lambda g, s, more, ahead: front(g + 1) if more else None, lambda g: None)

        def cross_attention_1():
            norm0 = norms[0]
            norms[0] += GROUPS
            with ExitStack() as mine:
                def sb(name, shape, dt=F32):
                    return mine.enter_context(nc.sbuf_tensor("c1_" + name, shape, dt))

                def sem(name):
                    return stage_sem("c1_" + name)

                att = Attention(sem, softmax=True, causal=False, values=lambda s, b, q: VX[:, s, b, 0, :])
                memory = sb("memory", [P, TPG, D])
                memoryT = sb("memoryT", [P, GT])
                best = sb("best", [P, TPG, 8])
                place = sb("place", [P, TPG, 8], U32)
                keyid = sb("keyid", [P, TPG], U32)

                z_ready, zT_ready, zT_copied = sem("z_ready"), sem("zT_ready"), sem("zT_copied")
                q_ready, q_copied = sem("q_ready"), sem("q_copied")
                keys_loaded = [sem(f"keys_loaded{t}") for t in range(TPG)]
                scores_ready = [sem(f"scores_ready{k}") for k in range(2)]
                scores_used = [sem(f"scores_used{k}") for k in range(2)]
                best_found = [sem(f"best_found{t}") for t in range(TPG)]
                gathered = sem("gathered")
                memoryT_ready, memoryT_copied = sem("memoryT_ready"), sem("memoryT_copied")
                k_ready, v_ready = sem("k_ready"), sem("v_ready")
                QX_ready, KX_ready, VX_ready = (sem(n) for n in ("QX_ready", "KX_ready", "VX_ready"))
                front_steps, match_steps = sem("front_steps"), sem("match_steps")
                scores_bank = [bank[2], bank[1]]

                with nc.Block() as block:
                    @block.sync
                    def _(sp):
                        def load(g):
                            for t in range(TPG):
                                sp.wait_ge(best_found[t], g)
                                sp.dma_start(keysT[:, t, :], a["ctxT"][:, bass.ds((g * TPG + t) * (BPT * KEYS), BPT * KEYS)]
                                             ).then_inc(keys_loaded[t], 16)

                        with sp.Fori(1, GROUPS) as g:
                            load(g)

                    @block.tensor
                    def _(pe):
                        def query(g):
                            pe.wait_ge(zT_copied, g + 1)
                            pe.wait_ge(VX_ready, g)
                            nc.tensor.matmul(bank[1][:, :], W("y_wqT"), zT[:, :], start=True, stop=True).then_inc(q_ready, 1)

                        def scores(g, t):
                            pe.wait_ge(q_copied, g + 1)
                            if is_first(g):
                                pe.wait_ge(first_keys_loaded, 16 * TPG)
                            else:
                                pe.wait_ge(keys_loaded[t], 16 * g)
                            if t == 0:
                                pe.wait_ge(KX_ready, H4 * g)
                            if t >= 2:
                                pe.wait_ge(scores_used[t % 2], 2 * g + 1)
                            for j in range(BPT):
                                at = t * P + j * SEQ
                                mm = nc.tensor.matmul(scores_bank[t % 2][j * SEQ:(j + 1) * SEQ, 0:KEYS], qT[:, at:at + SEQ],
                                                      keysT[:, t, j * KEYS:(j + 1) * KEYS], start=True, stop=True)
                            mm.then_inc(scores_ready[t % 2], 1)

                        def transpose_memory(g):
                            pe.wait_ge(gathered, 16 * (TPG * g + TPG))
                            for t in range(TPG):
                                mm = nc.tensor.transpose(bank[0][:, t * P:(t + 1) * P], memory[:, t, :], C("ident"))
                            mm.then_inc(memoryT_ready, 1)

                        def keys_values(g):
                            pe.wait_ge(memoryT_copied, g + 1)
                            pe.wait_ge(scores_used[0], 2 * g + 2)
                            nc.tensor.matmul(bank[2][:, :], W("y_wkrepT"), memoryT[:, :], start=True, stop=True
                                             ).then_inc(k_ready, 1)
                            pe.wait_ge(scores_used[1], 2 * g + 2)
                            pe_values_of_batches(memoryT, W("y_wvT"), DH).then_inc(v_ready, 1)

                        def front(g):
                            pe_zT(pe, g, z_ready, memoryT_copied, zT_ready)
                            query(g)
                            for t in range(TPG):
                                scores(g, t)
                            transpose_memory(g)
                            keys_values(g)

                        def turn(g, s, more, ahead):
                            if more:
                                pe_zT(pe, g + 1, z_ready, memoryT_copied, zT_ready)
                            pe.wait_ge(QX_ready, Q4 * g + Q4)
                            pe.wait_ge(KX_ready, H4 * g + H4)
                            att.pe_logits(pe, g, s, 0)
                            if more:
                                query(g + 1)
                            if not is_first(g):
                                att.pe_OT(pe, g)
                            if more:
                                scores(g + 1, 0)
                            att.pe_logits(pe, g, s, 1)
                            if more:
                                scores(g + 1, 1)
                                scores(g + 1, 2)
                                scores(g + 1, 3)
                            att.pe_logits(pe, g, s, 2)
                            att.pe_transpose(pe, g, 0)
                            if not is_first(g):
                                att.pe_y(pe, g, W("y_wcT"))
                            att.pe_transpose(pe, g, 1)
                            att.pe_values(pe, g, s, 0)
                            att.pe_logits(pe, g, s, 3)
                            att.pe_transpose(pe, g, 2)
                            if more:
                                transpose_memory(g + 1)
                            att.pe_values(pe, g, s, 1)
                            att.pe_transpose(pe, g, 3)
                            att.pe_values(pe, g, s, 2)
                            if more:
                                keys_values(g + 1)
                            att.pe_values(pe, g, s, 3)

                        def last(g):
                            att.pe_OT(pe, g)
                            att.pe_y(pe, g, W("y_wcT"))

                        turns(pe, front, turn, last)

                    @block.scalar
                    def _(act):
                        def copy_zT(g):
                            act.wait_ge(zT_ready, g + 1)
                            act.wait_ge(q_ready, g)
                            nc.scalar.copy(zT[:, :], bank[0][:, :]).then_inc(zT_copied, 1)

                        def copy_q(g):
                            act.wait_ge(q_ready, g + 1)
                            act.wait_ge(scores_ready[1], 2 * g)
                            act.wait_ge(QX_ready, Q4 * g)
                            nc.scalar.copy(qT[:, :], bank[1][:, :]).then_inc(q_copied, 1)

                        def spread_q(g, s, q):
                            act.wait_ge(q_copied, g + 1)
                            if not is_first(g):
                                act.wait_ge(att.OT_ready, g - 1)
                            act_spread_queries(s, q, "quarter4scaled", QX_ready)

                        def copy_memory(g):
                            act.wait_ge(memoryT_ready, g + 1)
                            act.wait_ge(v_ready, g)
                            nc.scalar.copy(memoryT[:, :], bank[0][:, :]).then_inc(memoryT_copied, 1)

                        def spread_k(g, s):
                            act.wait_ge(k_ready, g + 1)
                            if not is_first(g):
                                act.wait_ge(att.OT_ready, g - 1)
                            for h in range(H4):
                                act_spread_keys(s, bank[2], h, KX_ready)

                        def front(g):
                            copy_zT(g)
                            copy_q(g)
                            for q in range(Q4):
                                spread_q(g, 0, q)
                            copy_memory(g)
                            spread_k(g, 0)

                        def turn(g, s, more, ahead):
                            if more:
                                copy_zT(g + 1)
                                copy_q(g + 1)
                            att.act_exp(act, g, 0)
                            if not is_first(g):
                                att.act_copy_OT(act, g)
                            if more:
                                spread_q(g + 1, 1 - s, 0)
                            att.act_copy_ST(act, g, 0)
                            att.act_exp(act, g, 1)
                            if more:
                                spread_q(g + 1, 1 - s, 1)
                            att.act_copy_ST(act, g, 1)
                            att.act_exp(act, g, 2)
                            att.act_copy_ST(act, g, 2)
                            if more:
                                copy_memory(g + 1)
                            att.act_exp(act, g, 3)
                            if more:
                                spread_q(g + 1, 1 - s, 2)
                                spread_q(g + 1, 1 - s, 3)
                            att.act_copy_ST(act, g, 3)
                            if more:
                                spread_k(g + 1, 1 - s)

                        turns(act, front, turn, lambda g: att.act_copy_OT(act, g))

                    @block.vector
                    def _(dve):
                        fsteps = Steps(dve, front_steps, 7)
                        msteps = Steps(dve, match_steps, TPG)
                        bsteps = Steps(dve, att.steps, att.per)

                        def normalise_x(g):
                            fsteps.start(g)
                            layernorm(dve, fsteps, norm0 + g, lambda t: x_tile(g, t), lambda t: Z[:, t, :],
                                      lambda: dve.wait_ge(zT_ready, g), z_ready)
                            fsteps.end()

                        def find_best(g, t):
                            scores = scores_bank[t % 2][:, 0:KEYS]
                            wait_alone(dve, scores_ready[t % 2], 2 * g + t // 2 + 1)
                            nc.vector.max(out=best[:, t, :], in_=scores).then_inc(best_found[t], 1)
                            wait_alone(dve, best_found[t], g + 1)
                            if t == 0:
                                msteps.start(g)
                            msteps.did(nc.vector.max_index(out=place[:, t, :], in_max=best[:, t, :], in_values=scores))
                            msteps.settle()
                            dve.wait_ge(gathered, 16 * TPG * g)
                            nc.vector.tensor_tensor(keyid[:, t:t + 1], place[:, t, 0:1],
                                                    C("keybase")[:, bass.ds(g * TPG + t, 1)], ALU.add
                                                    ).then_inc(scores_used[t % 2], 1)

                        def values(g, s):
                            dve.wait_ge(v_ready, g + 1)
                            nc.vector.tensor_tensor(
                                VX[:, s, :, 0, 0:QW].rearrange("p b (h d) -> p b h d", d=DH),
                                bank[1][:, 0:TPG * BPT * DH].rearrange("p (b d) -> p b d", d=DH).unsqueeze(2).to_broadcast(
                                    [P, TPG * BPT, H4, DH]),
                                C("headcol").unsqueeze(1).unsqueeze(3).to_broadcast([P, TPG * BPT, H4, DH]), ALU.mult
                            ).then_inc(VX_ready, 1)

                        def front(g):
                            normalise_x(g)
                            for t in range(TPG):
                                find_best(g, t)
                            normalise_x(g + 1)
                            values(g, 0)

                        def turn(g, s, more, ahead):
                            bsteps.start(g)
                            att.dve_weigh(dve, bsteps, g, 0)
                            if more:
                                find_best(g + 1, 0)
                                find_best(g + 1, 1)
                            att.dve_weigh(dve, bsteps, g, 1)
                            if more:
                                find_best(g + 1, 2)
                                find_best(g + 1, 3)
                            if not is_first(g):
                                att.dve_add(dve, g)
                            att.dve_weigh(dve, bsteps, g, 2)
                            att.dve_normalise(dve, bsteps, g, 0)
                            att.dve_weigh(dve, bsteps, g, 3)
                            att.dve_normalise(dve, bsteps, g, 1)
                            if ahead:
                                normalise_x(g + 2)
                            att.dve_normalise(dve, bsteps, g, 2)
                            if more:
                                values(g + 1, 1 - s)
                            att.dve_normalise(dve, bsteps, g, 3)
                            bsteps.end()

                        turns(dve, front, turn, lambda g: att.dve_add(dve, g))

                    @block.gpsimd
                    def _(pool):
                        def gather(g):
                            wait_alone(pool, memoryT_ready, g)
                            for t in range(TPG):
                                wait_alone(pool, scores_used[t % 2], 2 * g + t // 2 + 1)
                                nc.gpsimd.indirect_dma_start(
                                    memory[:, t, :], None, a["ctx_1024"].rearrange("b k d -> (b k) d"),
                                    bass.IndirectOffsetOnAxis(ap=keyid[:, t:t + 1], axis=0)).then_inc(gathered, 16)

                        def front(g):
                            layernorm_rstd(pool, norm0 + g, 1e-5)
                            gather(g)
                            layernorm_rstd(pool, norm0 + g + 1, 1e-5)

                        def turn(g, s, more, ahead):
                            if more:
                                gather(g + 1)
                            if ahead:
                                layernorm_rstd(pool, norm0 + g + 2, 1e-5)

                        turns(pool, front, turn, lambda g: None)

        def rotary_attention():
            norm0 = norms[0]
            norms[0] += GROUPS
            with ExitStack() as mine:
                def sem(name):
                    return stage_sem("r1_" + name)

                att = Attention(sem, softmax=True, causal=True, values=lambda s, b, q: VX[:, s, b, q, :])
                z_ready, zT_ready, zT_copied = (sem(n) for n in ("z_ready", "zT_ready", "zT_copied"))
                v_ready, v_copied, VX_ready = sem("v_ready"), sem("v_copied"), sem("VX_ready")
                proj_ready = [sem(f"proj_ready{k}") for k in range(2)]
                proj_used = [sem(f"proj_used{k}") for k in range(2)]
                rotated, QX_ready, KX_ready = sem("rotated"), sem("QX_ready"), sem("KX_ready")
                masks_ready = sem("masks_ready")
                front_steps = sem("front_steps")

                with nc.Block() as block:
                    @block.sync
                    def _(sp):
                        sp.dma_start(rw1[:, :], a["g_r1"][:, :]).then_inc(residual_loaded, 16)
                        sp.dma_start(rw2[:, :, :], a["g_r2"].rearrange("(c p) d -> p c d", p=P)).then_inc(residual_loaded, 16)

                    @block.tensor
                    def _(pe):
                        def project(g, u):
                            pe.wait_ge(zT_copied, g + 1)
                            if u == 0:
                                pe.wait_ge(v_copied, g)
                            else:
                                pe.wait_ge(proj_used[u % 2], 2 * g + u // 2)
                            nc.tensor.matmul(bank[1 + u % 2][:, :], W(("b_wqT", "b_wqsT", "b_wkT", "b_wksT")[u]), zT[:, :],
                                             start=True, stop=True).then_inc(proj_ready[u % 2], 1)

                        def values(g):
                            pe.wait_ge(proj_used[0], 2 * g + 2)
                            pe_values_of_batches(zT, W("b_wvT"), QW).then_inc(v_ready, 1)

                        def front(g):
                            pe_zT(pe, g, z_ready, zT_copied, zT_ready)
                            for u in range(4):
                                project(g, u)
                            values(g)

                        def turn(g, s, more, ahead):
                            if more:
                                pe_zT(pe, g + 1, z_ready, zT_copied, zT_ready)
                            pe.wait_ge(QX_ready, Q4 * g + Q4)
                            pe.wait_ge(KX_ready, H4 * g + H4)
                            att.pe_logits(pe, g, s, 0)
                            if more:
                                project(g + 1, 0)
                                project(g + 1, 1)
                            att.pe_logits(pe, g, s, 1)
                            if not is_first(g):
                                att.pe_OT(pe, g)
                            att.pe_transpose(pe, g, 0)
                            if more:
                                project(g + 1, 3)
                                project(g + 1, 2)
                            if not is_first(g):
                                att.pe_y(pe, g, W("b_woT"))
                            att.pe_logits(pe, g, s, 2)
                            att.pe_transpose(pe, g, 1)
                            pe.wait_ge(VX_ready, g + 1)
                            att.pe_values(pe, g, s, 0)
                            att.pe_logits(pe, g, s, 3)
                            att.pe_transpose(pe, g, 2)
                            att.pe_values(pe, g, s, 1)
                            if more:
                                values(g + 1)
                            att.pe_transpose(pe, g, 3)
                            att.pe_values(pe, g, s, 2)
                            att.pe_values(pe, g, s, 3)

                        def last(g):
                            att.pe_OT(pe, g)
                            att.pe_y(pe, g, W("b_woT"))

                        pe.wait_ge(masks_ready, 2)
                        turns(pe, front, turn, last)

                    @block.scalar
                    def _(act):
                        def front(g):
                            act.wait_ge(zT_ready, g + 1)
                            act.wait_ge(v_ready, g)
                            nc.scalar.copy(zT[:, :], bank[0][:, :]).then_inc(zT_copied, 1)

                        def copy_v(g):
                            act.wait_ge(v_ready, g + 1)
                            act.wait_ge(VX_ready, g)
                            nc.scalar.copy(V[:, :, :, :].rearrange("p b q d -> p (b q d)"), bank[1][:, :]).then_inc(v_copied, 1)

                        def spread_q(g, s, q):
                            act.wait_ge(rotated, 2 * g + 1)
                            if not is_first(g):
                                act.wait_ge(att.OT_ready, g - 1)
                            act_spread_queries(s, q, "quarter4scaled", QX_ready)

                        def spread_k(g, s, h):
                            act.wait_ge(rotated, 2 * g + 2)
                            if not is_first(g):
                                act.wait_ge(att.OT_ready, g - 1)
                            act_spread_keys(s, kT, h, KX_ready)

                        def turn(g, s, more, ahead):
                            if more:
                                front(g + 1)
                            att.act_exp(act, g, 0)
                            if not is_first(g):
                                att.act_copy_OT(act, g)
                            if more:
                                spread_q(g + 1, 1 - s, 0)
                            att.act_copy_ST(act, g, 0)
                            att.act_exp(act, g, 1)
                            if more:
                                spread_q(g + 1, 1 - s, 1)
                            att.act_copy_ST(act, g, 1)
                            att.act_exp(act, g, 2)
                            if more:
                                spread_q(g + 1, 1 - s, 2)
                                spread_q(g + 1, 1 - s, 3)
                            att.act_exp(act, g, 3)
                            att.act_copy_ST(act, g, 2)
                            if more:
                                spread_k(g + 1, 1 - s, 1)
                                spread_k(g + 1, 1 - s, 0)
                            att.act_copy_ST(act, g, 3)
                            if more:
                                copy_v(g + 1)
                                spread_k(g + 1, 1 - s, 3)
                                spread_k(g + 1, 1 - s, 2)

                        def front_0(g):
                            front(g)
                            for h in range(H4):
                                spread_q(g, 0, h)
                            for h in range(H4):
                                spread_k(g, 0, h)
                            copy_v(g)

                        turns(act, front_0, turn, lambda g: att.act_copy_OT(act, g))

                    @block.vector
                    def _(dve):
                        fsteps = Steps(dve, front_steps, 7)
                        bsteps = Steps(dve, att.steps, att.per)
                        nc.vector.tensor_copy(maskneg16[0:SEQ, :], C("maskneg")[0:SEQ, :]).then_inc(masks_ready, 1)
                        nc.vector.tensor_copy(spread16[0:SEQ, :], C("spread")[0:SEQ, :]).then_inc(masks_ready, 1)

                        def moments_of_x(g):
                            fsteps.start(g)
                            layernorm_moments(dve, fsteps, lambda t: x_tile(g, t))
                            fsteps.end()

                        def normalise_x(g):
                            layernorm_output(dve, norm0 + g, lambda t: x_tile(g, t), lambda t: Z[:, t, :],
                                             lambda: dve.wait_ge(zT_ready, g), z_ready)

                        def rotate(g, u):
                            if u == 0:
                                dve.wait_ge(QX_ready, Q4 * g)
                                dve.wait_ge(KX_ready, H4 * g)
                            for k, (to, table) in enumerate((((qT, kT)[u], "cos"), ((spare, spare2)[u], "sin"))):
                                dve.wait_ge(proj_ready[k], 2 * g + u + 1)
                                nc.vector.tensor_tensor(by_batch(to[:, :]), by_batch(bank[1 + k][:, :]),
                                                        C(table).unsqueeze(1).to_broadcast([P, TPG * BPT, SEQ]), ALU.mult
                                                        ).then_inc(proj_used[k], 1)

                        def front(g):
                            moments_of_x(g)
                            normalise_x(g)
                            rotate(g, 0)
                            rotate(g, 1)
                            moments_of_x(g + 1)
                            normalise_x(g + 1)

                        def turn(g, s, more, ahead):
                            bsteps.start(g)
                            att.dve_weigh(dve, bsteps, g, 0)
                            if more:
                                rotate(g + 1, 0)
                            att.dve_weigh(dve, bsteps, g, 1)
                            if more:
                                rotate(g + 1, 1)
                            if not is_first(g):
                                att.dve_add(dve, g)
                            att.dve_weigh(dve, bsteps, g, 2)
                            att.dve_normalise(dve, bsteps, g, 0)
                            att.dve_weigh(dve, bsteps, g, 3)
                            att.dve_normalise(dve, bsteps, g, 1)
                            if ahead:
                                moments_of_x(g + 2)
                            att.dve_normalise(dve, bsteps, g, 2)
                            if ahead:
                                normalise_x(g + 2)
                            att.dve_normalise(dve, bsteps, g, 3)
                            bsteps.end()

                        turns(dve, front, turn, lambda g: att.dve_add(dve, g))

                    @block.gpsimd
                    def _(pool):
                        def rotate(g):
                            for u, (to, part) in enumerate(((qT, spare), (kT, spare2))):
                                pool.wait_ge(proj_used[0], 2 * g + u + 1)
                                pool.wait_ge(proj_used[1], 2 * g + u + 1)
                                nc.gpsimd.tensor_tensor(to[:, :], to[:, :], part[:, :], ALU.add).then_inc(rotated, 1)

                        def values(g, s):
                            pool.wait_ge(v_copied, g + 1)
                            if not is_first(g):
                                pool.wait_ge(att.OT_ready, g - 1)
                            spread_values(nc.gpsimd, s, VX_ready)

                        def first(g):
                            layernorm_rstd(pool, norm0 + g, 1e-5)
                            rotate(g)
                            layernorm_rstd(pool, norm0 + g + 1, 1e-5)
                            values(g, 0)

                        def turn(g, s, more, ahead):
                            if more:
                                rotate(g + 1)
                            if ahead:
                                layernorm_rstd(pool, norm0 + g + 2, 1e-5)
                            if more:
                                values(g + 1, 1 - s)

                        turns(pool, first, turn, lambda g: None)

        def experts_1():
            norm0 = norms[0]
            norms[0] += 2 * GROUPS
            with ExitStack() as mine:
                def sb(name, shape, dt=F32):
                    return mine.enter_context(nc.sbuf_tensor("f1_" + name, shape, dt))

                def sem(name):
                    return stage_sem("f1_" + name)

                Z1, Z2 = sb("Z1", [P, TPG, D]), sb("Z2", [P, TPG, D])
                A = sb("A", [P, TILES * D])
                residual = sb("residual", [P, TILES * D])
                zT2 = sb("zT2", [P, 2, GT])
                logit = sb("logit", [P, TILES * 10])
                w1 = sb("w1", [P, 2, F1])
                w2 = sb("w2", [P, 2, 4, D])
                b2 = sb("b2", [P, E1, D])
                hidden = sb("hidden", [P, 2, 4, GT])
                coef = sb("coef", [P, TILES, 2])
                coef0 = sb("coef0", [P, TILES])
                moe = sb("moe", [P, TILES])
                sent_all = sb("sent_all", [P, TILES], U32)
                fetch_all = sb("fetch_all", [P, TILES], U32)
                sent = sb("sent", [P, 2, TPG], U32)
                fetch = sb("fetch", [P, 2, TPG], U32)
                sending = sb("sending", [P, 2, TPG, D])
                places = sb("places", [P, 2, TPG, D])
                placesT = sb("placesT", [P, 2, GT])
                result = sb("result", [P, 2, TPG, D])
                fetched = sb("fetched", [P, 2, TPG, D])
                rowspace = a["rowspace"]
                results = a["results"]

                front_steps = sem("front_steps")
                w1_loaded, w2_loaded = ([sem(f"{n}{k}") for k in range(2)] for n in ("w1_loaded", "w2_loaded"))
                b2_loaded = sem("b2_loaded")
                z1_ready, z2_ready, z2T_ready, z2T_copied = (sem(n) for n in (
                    "z1_ready", "z2_ready", "z2T_ready", "z2T_copied"))
                x_passed, a_scaled, a_ready = sem("x_passed"), sem("a_scaled"), sem("a_ready")
                gate_ready, gate_used = sem("gate_ready"), sem("gate_used")
                up_ready = [sem(f"up_ready{f}") for f in range(4)]
                gelu_done = [sem(f"gelu_done{f}") for f in range(4)]
                down_ready, down_used = sem("down_ready"), sem("down_used")

                def group_of(ap, g):
                    return ap[:, bass.ds(g * GT, GT)].rearrange("p (t d) -> p t d", t=TPG)

                def load_w1(sp, e, k):
                    sp.dma_start(w1[:, k, :], a["g_w1"][bass.ds(e, 1), :, :].rearrange("e p f -> p (e f)")
                                 ).then_inc(w1_loaded[k], 16)

                def load_w2(sp, e, k):
                    sp.dma_start(w2[:, k, :, :], a["g_w2"][bass.ds(e, 1), :, :].rearrange("e (c p) d -> p (e c) d", p=P)
                                 ).then_inc(w2_loaded[k], 16)

                with nc.Block() as block:
                    @block.sync
                    def _(sp):
                        for k in range(2):
                            load_w1(sp, k, k)
                            load_w2(sp, k, k)
                        sp.dma_start(b2[:, :, :], a["g_b2"].rearrange("e d -> (e d)").partition_broadcast(P)
                                     .rearrange("p (e d) -> p e d", d=D)).then_inc(b2_loaded, 16)

                    @block.vector
                    def _(dve):
                        steps = Steps(dve, front_steps, 14)

                        def layernorms(g):
                            steps.start(g)
                            layernorm(dve, steps, norm0 + 2 * g, lambda t: x_tile(g, t), lambda t: Z1[:, t, :],
                                      lambda: dve.wait_ge(x_passed, g), z1_ready)
                            dve.wait_ge(z1_ready, TPG * g + TPG)

                            def z2_free():
                                dve.wait_ge(z2T_ready, g)
                                dve.wait_ge(a_scaled, g)

                            layernorm(dve, steps, norm0 + 2 * g + 1, lambda t: Z1[:, t, :], lambda t: Z2[:, t, :],
                                      z2_free, z2_ready)
                            steps.end()

                        def keep_logits(g):
                            dve.wait_ge(gate_ready, g + 1)
                            nc.vector.tensor_copy(logit[:, bass.ds(g * (TPG * 10), TPG * 10)], bank[1][:, 0:TPG * 10]
                                                  ).then_inc(gate_used, 1)

                        def front(g):
                            layernorms(g)
                            layernorms(g + 1)
                            keep_logits(g)

                        def turn(g, s, more, ahead):
                            if ahead:
                                layernorms(g + 2)
                            if more:
                                keep_logits(g + 1)
                            dve.wait_ge(down_ready, g + 1)
                            nc.vector.tensor_tensor(group_of(residual, g), bank[6 + s][:, :].rearrange("p (t d) -> p t d", d=D),
                                                    W("g_rb2").unsqueeze(1).to_broadcast([P, TPG, D]), ALU.add
                                                    ).then_inc(down_used, 1)

                        turns(dve, front, turn, lambda g: None)

                    @block.gpsimd
                    def _(pool):
                        def layernorms(g):
                            layernorm_rstd(pool, norm0 + 2 * g, 1e-5)
                            layernorm_rstd(pool, norm0 + 2 * g + 1, 1e-12)
                            wait_alone(pool, z1_ready, TPG * g + TPG)
                            nc.gpsimd.tensor_tensor(x_group(g), x_group(g), Z1[:, :, :], ALU.add).then_inc(x_passed, 1)
                            wait_alone(pool, z2_ready, TPG * g + TPG)
                            nc.gpsimd.tensor_tensor(group_of(A, g), Z2[:, :, :], W("g_nw").unsqueeze(1).to_broadcast([P, TPG, D]),
                                                    ALU.mult).then_inc(a_scaled, 1)
                            wait_alone(pool, a_scaled, g + 1)
                            nc.gpsimd.tensor_tensor(group_of(A, g), group_of(A, g),
                                                    W("g_nb").unsqueeze(1).to_broadcast([P, TPG, D]), ALU.add
                                                    ).then_inc(a_ready, 1)

                        def front(g):
                            layernorms(g)
                            layernorms(g + 1)

                        turns(pool, front, lambda g, s, more, ahead: layernorms(g + 2) if ahead else None, lambda g: None)

                    @block.tensor
                    def _(pe):
                        def gates(g, s):
                            pe.wait_ge(z2T_copied, g + 1)
                            pe.wait_ge(gate_used, g)
                            for t in range(TPG):
                                mm = nc.tensor.matmul(bank[1][:, t * 10:(t + 1) * 10], zT2[:, s, t * P:(t + 1) * P], W("g_w"),
                                                      start=True, stop=True)
                            mm.then_inc(gate_ready, 1)

                        def front(g):
                            pe_zT(pe, g, z2_ready, z2T_copied, z2T_ready, Z2)
                            gates(g, 0)

                        def turn(g, s, more, ahead):
                            for f in range(4):
                                pe.wait_ge(gelu_done[f], g)
                                nc.tensor.matmul(bank[2 + f][:, :], rw1[:, f * P:(f + 1) * P], zT2[:, s, :],
                                                 start=True, stop=True).then_inc(up_ready[f], 1)
                            if more:
                                pe_zT(pe, g + 1, z2_ready, z2T_copied, z2T_ready, Z2)
                            for f in range(4):
                                pe.wait_ge(gelu_done[f], g + 1)
                            pe.wait_ge(down_used, g)
                            for t in range(TPG):
                                for f in range(4):
                                    mm = nc.tensor.matmul(bank[6 + s][:, t * D:(t + 1) * D],
                                                          hidden[:, 0, f, t * P:(t + 1) * P], rw2[:, f, :],
                                                          start=(f == 0), stop=(f == 3))
                            mm.then_inc(down_ready, 1)
                            if more:
                                gates(g + 1, 1 - s)

                        pe.wait_ge(residual_loaded, 32)
                        turns(pe, front, turn, lambda g: None)

                    @block.scalar
                    def _(act):
                        def copy_z2T(g, s):
                            act.wait_ge(z2T_ready, g + 1)
                            if not is_first(g):
                                act.wait_ge(up_ready[3], g - 1)
                            nc.scalar.activation(zT2[:, s, :], bank[0][:, :], ACT.Identity, bias=W("g_nbcol"), scale=W("g_nwcol")
                                                 ).then_inc(z2T_copied, 1)

                        def turn(g, s, more, ahead):
                            for f in range(4):
                                act.wait_ge(up_ready[f], g + 1)
                                act.wait_ge(down_ready, g)
                                nc.scalar.activation(hidden[:, 0, f, :], bank[2 + f][:, :], ACT.Gelu_apprx_tanh,
                                                     bias=W("g_rb1")[:, f:f + 1]).then_inc(gelu_done[f], 1)
                            if more:
                                copy_z2T(g + 1, 1 - s)

                        turns(act, lambda g: copy_z2T(g, 0), turn, lambda g: None)

                def sb8(name):
                    return sb(name, [P, TILES, E1])

                prob, hit, onehot, where = sb8("prob"), sb8("hit"), sb8("onehot"), sb8("where")
                running, place = sb("running", [P, E1 * TILES]), sb("place", [P, E1, TILES])
                peak, total, rtotal, own, kept_, slot = (sb(n, [P, TILES]) for n in (
                    "peak", "total", "rtotal", "own", "kept", "slot"))
                low_ready, exp_done, onehot_ready, counts_ready = (sem(n) for n in (
                    "low_ready", "exp_done", "onehot_ready", "counts_ready"))

                def by_tile(v):
                    return v.unsqueeze(2).to_broadcast([P, TILES, E1])

                with nc.Block() as block:
                    @block.scalar
                    def _(act):
                        act.wait_ge(low_ready, 2)
                        nc.scalar.activation(prob[:, :, :], prob[:, :, :], ACT.Exp).then_inc(exp_done, 1)
                        nc.scalar.activation(coef[:, :, :], coef[:, :, :], ACT.Exp).then_inc(exp_done, 1)

                    @block.tensor
                    def _(pe):
                        pe.wait_ge(onehot_ready, 1)
                        oh = onehot[:, :, :].rearrange("p t e -> p e t")
                        nc.tensor.matmul(bank[2][:, 0:E1 * TILES], C("before"), oh, start=True, stop=True)
                        nc.tensor.matmul(bank[3][:, 0:E1 * TILES], C("ones"), oh, start=True, stop=True).then_inc(counts_ready, 1)

                    @block.vector
                    def _(dve):
                        route_steps = sem("route_steps")
                        steps = Steps(dve, route_steps, 0)
                        steps.start(0)

                        def do(ins):
                            steps.did(ins)
                            steps.settle()

                        v = logit[:, :].rearrange("p (t w) -> p t w", w=10)
                        do(nc.vector.reduce_max(peak[:, :], v[:, :, 0:E1], AX_X))
                        nc.vector.tensor_tensor(prob[:, :, :], v[:, :, 0:E1], by_tile(peak[:, :]), ALU.subtract
                                                ).then_inc(low_ready, 1)
                        do(nc.vector.reduce_max(own[:, :], v[:, :, E1:E1 + 2], AX_X))
                        nc.vector.tensor_tensor(coef[:, :, :], v[:, :, E1:E1 + 2],
                                                own[:, :].unsqueeze(2).to_broadcast([P, TILES, 2]), ALU.subtract
                                                ).then_inc(low_ready, 1)
                        dve.wait_ge(exp_done, 2)
                        do(nc.vector.reduce_sum(total[:, :], prob[:, :, :], AX_X))
                        do(nc.vector.reciprocal(rtotal[:, :], total[:, :]))
                        do(nc.vector.tensor_tensor(prob[:, :, :], prob[:, :, :], by_tile(rtotal[:, :]), ALU.mult))
                        do(nc.vector.reduce_max(peak[:, :], prob[:, :, :], AX_X))
                        do(nc.vector.tensor_tensor(hit[:, :, :], prob[:, :, :], by_tile(peak[:, :]), ALU.is_equal))
                        do(nc.vector.tensor_tensor(hit[:, :, :], hit[:, :, :],
                                                   C("rank8").unsqueeze(1).to_broadcast([P, TILES, E1]), ALU.mult))
                        do(nc.vector.reduce_max(own[:, :], hit[:, :, :], AX_X))
                        nc.vector.tensor_tensor(onehot[:, :, :], hit[:, :, :], by_tile(own[:, :]), ALU.is_equal
                                                ).then_inc(onehot_ready, 1)
                        dve.wait_ge(counts_ready, 1)
                        dve.wait_ge(onehot_ready, 1)
                        do(nc.vector.tensor_tensor_scan(running[:, :], C("restart"), bank[3][:, 0:E1 * TILES], 0.0,
                                                        ALU.mult, ALU.add))
                        do(nc.vector.tensor_tensor(running[:, :], running[:, :], bank[3][:, 0:E1 * TILES], ALU.subtract))
                        do(nc.vector.tensor_tensor(place[:, :, :].rearrange("p e t -> p (e t)"), running[:, :],
                                                   bank[2][:, 0:E1 * TILES], ALU.add))
                        do(nc.vector.tensor_tensor(where[:, :, :], place[:, :, :].rearrange("p e t -> p t e"), onehot[:, :, :],
                                                   ALU.mult))
                        do(nc.vector.reduce_sum(own[:, :], where[:, :, :], AX_X))
                        do(nc.vector.tensor_scalar(kept_[:, :], own[:, :], float(CAP), None, ALU.is_lt))
                        do(nc.vector.tensor_tensor(hit[:, :, :], onehot[:, :, :],
                                                   C("expertbase").unsqueeze(1).to_broadcast([P, TILES, E1]), ALU.mult))
                        do(nc.vector.reduce_sum(slot[:, :], hit[:, :, :], AX_X))
                        do(nc.vector.tensor_tensor(slot[:, :], slot[:, :], own[:, :], ALU.add))
                        do(nc.vector.tensor_tensor(fetch_all[:, :], slot[:, :], kept_[:, :], ALU.mult))
                        do(nc.vector.tensor_tensor(slot[:, :], slot[:, :], C("tokenid"), ALU.subtract))
                        do(nc.vector.tensor_tensor(slot[:, :], slot[:, :], kept_[:, :], ALU.mult))
                        do(nc.vector.tensor_tensor(sent_all[:, :], slot[:, :], C("tokenid"), ALU.add))

                def groups(eng, body):
                    body(0, 0, 0)
                    body(1, 1, 0)
                    with eng.Fori(1, GROUPS // 2) as i:
                        body(2 * i, 0, i)
                        body(2 * i + 1, 1, i)

                sending_copied, sent_copied = sem("sending_copied"), sem("sent_copied")
                rows_sent = [sem(f"rows_sent{s}") for s in range(2)]
                weighted, residual_added = sem("weighted"), sem("residual_added")
                with nc.Block() as block:
                    @block.gpsimd
                    def _(pool):
                        def send(g, s, i):
                            wait_alone(pool, sending_copied, g + 1)
                            wait_alone(pool, sent_copied, g + 1)
                            for t in range(TPG):
                                nc.gpsimd.indirect_dma_start(
                                    rowspace[:, :], bass.IndirectOffsetOnAxis(ap=sent[:, s, t:t + 1], axis=0),
                                    sending[:, s, t, :], None).then_inc(rows_sent[s], 16)

                        pool.wait_ge(places_cleared, 16)
                        groups(pool, send)
                        for s in range(2):
                            pool.wait_ge(rows_sent[s], 16 * TILES // 2)

                    @block.scalar
                    def _(act):
                        def copy(g, s, i):
                            if not is_first(i):
                                act.wait_ge(rows_sent[s], 16 * TPG * i)
                            nc.scalar.copy(sending[:, s, :, :], group_of(A, g)).then_inc(sending_copied, 1)

                        groups(act, copy)

                    @block.vector
                    def _(dve):
                        weights_steps = sem("weights_steps")
                        steps = Steps(dve, weights_steps, 6)

                        def do(ins):
                            steps.did(ins)
                            steps.settle()

                        def copy_sent(g, s, i):
                            if not is_first(i):
                                dve.wait_ge(rows_sent[s], 16 * TPG * i)
                            nc.vector.tensor_copy(sent[:, s, :], sent_all[:, bass.ds(g * TPG, TPG)]).then_inc(sent_copied, 1)

                        def add_residual(g):
                            nc.vector.tensor_tensor(group_of(residual, g), group_of(residual, g),
                                                    coef0[:, bass.ds(g * TPG, TPG)].unsqueeze(2).to_broadcast([P, TPG, D]),
                                                    ALU.mult).then_inc(weighted, 1)
                            dve.wait_ge(weighted, g + 1)
                            nc.vector.tensor_tensor(x_group(g), x_group(g), group_of(residual, g), ALU.add
                                                    ).then_inc(residual_added, 1)

                        copy_sent(0, 0, 0)
                        copy_sent(1, 1, 0)
                        steps.start(0)
                        do(nc.vector.reduce_sum(total[:, :], coef[:, :, :], AX_X))
                        do(nc.vector.reciprocal(rtotal[:, :], total[:, :]))
                        do(nc.vector.tensor_tensor(coef[:, :, :], coef[:, :, :],
                                                   rtotal[:, :].unsqueeze(2).to_broadcast([P, TILES, 2]), ALU.mult))
                        do(nc.vector.tensor_copy(coef0[:, :], coef[:, :, 0]))
                        do(nc.vector.tensor_tensor(moe[:, :], peak[:, :], kept_[:, :], ALU.mult))
                        do(nc.vector.tensor_tensor(moe[:, :], moe[:, :], coef[:, :, 1], ALU.mult))
                        steps.end()
                        add_residual(0)
                        add_residual(1)
                        with dve.Fori(1, GROUPS // 2) as i:
                            for s in range(2):
                                copy_sent(2 * i + s, s, i)
                                add_residual(2 * i + s)

                places_loaded = [sem(f"places_loaded{k}") for k in range(2)]
                placesT_ready, placesT_copied = ([sem(f"{n}{k}") for k in range(2)] for n in ("placesT_ready", "placesT_copied"))
                e_up_ready = [sem(f"e_up_ready{f}") for f in range(4)]
                e_gelu_done = [sem(f"e_gelu_done{f}") for f in range(4)]
                e_down_ready = [sem(f"e_down_ready{k}") for k in range(2)]
                result_ready = [sem(f"result_ready{k}") for k in range(2)]
                result_stored = [sem(f"result_stored{k}") for k in range(2)]

                def experts(eng, body):
                    body(0, 0, 2)
                    body(0, 1, 2)
                    with eng.Fori(1, E1 // 2 - 1) as i:
                        body(i, 0, 2)
                        body(i, 1, 2)
                    body(E1 // 2 - 1, 0, 1)
                    body(E1 // 2 - 1, 1, 0)

                with nc.Block() as block:
                    @block.sync
                    def _(sp):
                        def load_places(i, k):
                            e = 2 * i + k
                            if not is_first(i):
                                sp.wait_ge(placesT_ready[k], i)
                            sp.dma_start(places[:, k, :, :], rowspace[bass.ds(e * CAP, CAP), :].rearrange("(t p) d -> p t d", p=P)
                                         ).then_inc(places_loaded[k], 16)

                        def load(i, k, ahead):
                            if ahead == 2:
                                load_places(i + 1, k)
                                sp.wait_ge(e_up_ready[3], 2 * i + k + 1)
                                load_w1(sp, 2 * i + 2 + k, k)
                                sp.wait_ge(e_down_ready[k], i + 1)
                                load_w2(sp, 2 * i + 2 + k, k)

                        load_places(0, 0)
                        load_places(0, 1)
                        experts(sp, load)

                    @block.tensor
                    def _(pe):
                        def transpose(i, k):
                            pe.wait_ge(places_loaded[k], 16 * i + 16)
                            pe.wait_ge(placesT_copied[k], i)
                            for t in range(TPG):
                                mm = nc.tensor.transpose(bank[k][:, t * P:(t + 1) * P], places[:, k, t, :], C("ident"))
                            mm.then_inc(placesT_ready[k], 1)

                        def up(i, k):
                            pe.wait_ge(placesT_copied[k], i + 1)
                            pe.wait_ge(w1_loaded[k], 16 * i + 16)
                            for f in range(4):
                                pe.wait_ge(e_gelu_done[f], 2 * i + k)
                                nc.tensor.matmul(bank[2 + f][:, :], w1[:, k, f * P:(f + 1) * P], placesT[:, k, :],
                                                 start=True, stop=True).then_inc(e_up_ready[f], 1)

                        def down(i, k):
                            for f in range(4):
                                pe.wait_ge(e_gelu_done[f], 2 * i + k + 1)
                            pe.wait_ge(w2_loaded[k], 16 * i + 16)
                            pe.wait_ge(result_ready[k], i)
                            for t in range(TPG):
                                for f in range(4):
                                    mm = nc.tensor.matmul(bank[6 + k][:, t * D:(t + 1) * D], hidden[:, k, f, t * P:(t + 1) * P],
                                                          w2[:, k, f, :], start=(f == 0), stop=(f == 3))
                            mm.then_inc(e_down_ready[k], 1)

                        def step(i, k, ahead):
                            if ahead >= 1:
                                up(i + k, 1 - k)
                            if ahead == 2:
                                transpose(i + 1, k)
                            down(i, k)

                        transpose(0, 0)
                        transpose(0, 1)
                        up(0, 0)
                        experts(pe, step)

                    @block.scalar
                    def _(act):
                        def copy_places(i, k):
                            act.wait_ge(placesT_ready[k], i + 1)
                            if not is_first(i):
                                act.wait_ge(e_up_ready[3], 2 * i + k - 1)
                            nc.scalar.copy(placesT[:, k, :], bank[k][:, :]).then_inc(placesT_copied[k], 1)

                        def step(i, k, ahead):
                            act.wait_ge(e_down_ready[k], i)
                            for f in range(4):
                                act.wait_ge(e_up_ready[f], 2 * i + k + 1)
                                nc.scalar.activation(hidden[:, k, f, :], bank[2 + f][:, :], ACT.Gelu_apprx_tanh,
                                                     bias=W("g_b1")[:, bass.ds(i * 8 + 4 * k + f, 1)]
                                                     ).then_inc(e_gelu_done[f], 1)
                            if ahead == 2:
                                copy_places(i + 1, k)

                        copy_places(0, 0)
                        copy_places(0, 1)
                        experts(act, step)

                    @block.vector
                    def _(dve):
                        def step(i, k, ahead):
                            dve.wait_ge(e_down_ready[k], i + 1)
                            dve.wait_ge(result_stored[k], 16 * i)
                            nc.vector.tensor_tensor(result[:, k, :, :], bank[6 + k][:, :].rearrange("p (t d) -> p t d", d=D),
                                                    b2[:, bass.ds(2 * i + k, 1), :].to_broadcast([P, TPG, D]), ALU.add
                                                    ).then_inc(result_ready[k], 1)

                        dve.wait_ge(b2_loaded, 16)
                        experts(dve, step)

                    @block.gpsimd
                    def _(pool):
                        def store(i, k, ahead):
                            pool.wait_ge(result_ready[k], i + 1)
                            pool.dma_start(results[bass.ds((2 * i + k) * CAP, CAP), :].rearrange("(t p) d -> p t d", p=P),
                                           result[:, k, :, :]).then_inc(result_stored[k], 16)

                        experts(pool, store)
                        for k in range(2):
                            pool.wait_ge(result_stored[k], 16 * (E1 // 2))

                fetch_ready, x_ready = sem("fetch_ready"), sem("x_ready")
                rows_fetched = [sem(f"rows_fetched{s}") for s in range(2)]
                with nc.Block() as block:
                    @block.gpsimd
                    def _(pool):
                        def gather(g, s, i):
                            wait_alone(pool, fetch_ready, g + 1)
                            if not is_first(i):
                                wait_alone(pool, x_ready, TPG * (g - 1))
                            for t in range(TPG):
                                nc.gpsimd.indirect_dma_start(
                                    fetched[:, s, t, :], None, results[:, :],
                                    bass.IndirectOffsetOnAxis(ap=fetch[:, s, t:t + 1], axis=0)).then_inc(rows_fetched[s], 16)

                        groups(pool, gather)

                    @block.vector
                    def _(dve):
                        def copy_fetch(g, s):
                            nc.vector.tensor_copy(fetch[:, s, :], fetch_all[:, bass.ds(g * TPG, TPG)]).then_inc(fetch_ready, 1)

                        def add(g, s, i):
                            dve.wait_ge(rows_fetched[s], 16 * TPG * (i + 1))
                            for t in range(TPG):
                                nc.vector.scalar_tensor_tensor(
                                    out=x_tile(g, t), in0=fetched[:, s, t, :], scalar=moe[:, bass.ds(g * TPG + t, 1)],
                                    in1=x_tile(g, t), op0=ALU.mult, op1=ALU.add).then_inc(x_ready, 1)

                        copy_fetch(0, 0)
                        copy_fetch(1, 1)
                        with dve.Fori(1, GROUPS // 2) as i:
                            for s in range(2):
                                add(2 * i - 2 + s, s, i - 1)
                                copy_fetch(2 * i + s, s)
                        for s in range(2):
                            add(GROUPS - 2 + s, s, GROUPS // 2 - 1)

                    @block.sync
                    def _(sp):
                        tiles = out.rearrange("b s d -> (b s) d").rearrange("(t p) d -> p t d", p=P)
                        with sp.Fori(0, GROUPS) as g:
                            sp.wait_ge(x_ready, TPG * g + TPG)
                            sp.dma_start(tiles[:, bass.ds(g * TPG, TPG), :], x_group(g)).then_inc(x_out, 16)
                        sp.wait_ge(x_out, 16 * GROUPS)

        def setup():
            with nc.Block() as block:
                @block.sync
                def _(sp):
                    sp.dma_start(X[:, 0:GT], a["xt"][:, 0:GT]).then_inc(x_first, 16)
                    sp.dma_start(const[:, :CONST_FIRST], a["const"][:, :CONST_FIRST]).then_inc(loaded, 16)
                    sp.dma_start(small[:, :SMALL_FIRST], a["small"][:, :SMALL_FIRST]).then_inc(loaded, 16)

                @block.gpsimd
                def _(pool):
                    nc.gpsimd.memset(zeros[:, :], 0.0).then_inc(zeros_ready, 1)

        setup()
        for stage in (cross_attention_0, linear_attention, experts_0, cross_attention_1, rotary_attention, experts_1):
            if stage is experts_1:
                attention_buffers.close()
            stage()
            nc.clear_and_free_semaphores(stage_sems)
            stage_sems.clear()
            nc.all_engine_barrier()


def constants():
    p = np.arange(P)
    c = np.zeros((P, CONST_W), np.float32)

    def put(name, v):
        at, w = CONST[name]
        c[:v.shape[0], at:at + w] = v

    put("ident", np.eye(P))
    put("quarter4", p[:, None] // QW == np.arange(4))
    put("quarter4scaled", (p[:, None] // QW == np.arange(4)) * DH ** -0.5)
    put("head4", p[:, None] % QW // DH == np.arange(4))
    put("headcol", p[:, None] // SEQ == np.arange(H4))
    put("causal", p[:, None] % SEQ <= np.arange(SEQ))
    half = (np.float32(1.0) / np.float32(10000.0) ** (np.arange(0, DH, 2, dtype=np.float32) / np.float32(DH))).astype(np.float32)
    angle = (half[p % DH // 2][:, None] * np.arange(SEQ, dtype=np.float32)).astype(np.float32)
    put("cos", np.cos(angle))
    put("sin", np.sin(angle) * np.where(p % 2 == 0, -1.0, 1.0)[:, None])
    put("maskneg", np.where(np.arange(SEQ)[None, :] > np.arange(SEQ)[:, None], -1e30, 0.0))
    put("spread", np.arange(SEQ)[:, None] == p % SEQ)
    put("minushalf", np.full((P, 4), -0.5))
    put("before", p[:, None] < p)
    put("ones", np.ones((P, P)))
    put("keybase", (np.arange(TILES) * BPT + p[:, None] // SEQ) * KEYS)
    put("rank8", np.broadcast_to(8.0 - np.arange(8), (P, 8)))
    put("expertbase", np.broadcast_to(CAP * np.arange(8.0), (P, 8)))
    put("tokenid", E1 * CAP + np.arange(TILES) * P + p[:, None])
    put("restart", np.broadcast_to(np.arange(256) % TILES != 0, (P, 256)))
    return c


def weights(v):
    s = np.zeros((P, SMALL_W), np.float32)

    def put(name, w):
        at, n = SMALL[name]
        s[:w.shape[0], at:at + n] = w

    def row(name, w):
        put(name, np.broadcast_to(w.reshape(1, -1), (P, w.size)))

    def col(name, w):
        put(name, w.reshape(P, -1) if w.ndim == 1 else w)

    put("x_wqT", v["L0_xattn_Wq"].T)
    put("x_wk", v["L0_xattn_Wk"])
    put("x_wvT", v["L0_xattn_Wv"].T)
    col("x_bq", v["L0_xattn_bq"])
    col("x_bk", v["L0_xattn_bk"])
    row("x_bv", v["L0_xattn_bv"])
    by_head = np.arange(D).reshape(Q4, H4, DH).transpose(1, 0, 2)
    put("a_w", v["L0_attn_qkv_w"][:, :2 * D])
    put("a_wv", v["L0_attn_qkv_w"][:, 2 * D:][:, by_head.ravel()])
    col("a_bq", v["L0_attn_qkv_b"][:D])
    col("a_bk", v["L0_attn_qkv_b"][D:2 * D])
    put("a_bvh", np.repeat(v["L0_attn_qkv_b"][2 * D:][by_head].reshape(H4, QW), SEQ, axis=0))
    put("a_wo", v["L0_attn_out_w"])
    row("a_bo", v["L0_attn_out_b"])
    col("f_g", v["L0_ffn_ln_g"])
    col("f_b", v["L0_ffn_ln_b"])
    put("f_rw", v["L0_ffn_rW"])
    row("f_rb", v["L0_ffn_rb"])
    put("f_b1", v["L0_ffn_b1"].reshape(E0, 2, P).transpose(2, 0, 1).reshape(P, 16))
    put("f_b2", v["L0_ffn_b2"])
    put("y_wqT", v["L1_xattn_Wq"].T)
    put("y_wkrepT", np.tile(v["L1_xattn_Wkv"][:DH].T, (1, HEADS)))
    put("y_wvT", v["L1_xattn_Wkv"][DH:].T)
    put("y_wcT", v["L1_xattn_Wc"].T)
    swap = np.arange(D) ^ 1
    put("b_wqT", v["L1_attn_Wq"].T)
    put("b_wqsT", v["L1_attn_Wq"][swap].T)
    put("b_wkT", v["L1_attn_Wk"].T)
    put("b_wksT", v["L1_attn_Wk"][swap].T)
    put("b_wvT", v["L1_attn_Wv"].T[:, by_head.ravel()])
    put("b_woT", v["L1_attn_Wo"].T)
    col("g_nwcol", v["L1_ffn_attn_nw"])
    col("g_nbcol", v["L1_ffn_attn_nb"])
    row("g_nw", v["L1_ffn_attn_nw"])
    row("g_nb", v["L1_ffn_attn_nb"])
    put("g_w", np.concatenate([v["L1_ffn_wg"], v["L1_ffn_res_coef"]], axis=1))
    put("g_rb1", v["L1_ffn_res_inter_b"].reshape(4, P).T)
    row("g_rb2", v["L1_ffn_res_output_b"])
    put("g_b1", v["L1_ffn_inter_b"].reshape(E1, 4, P).transpose(2, 0, 1).reshape(P, 32))
    return s


def kernel(**inputs):
    import concourse.bacc as bacc
    from concourse.bass_utils import run_bass_kernel_spmd

    v = {k: np.asarray(x) for k, x in inputs.items()}
    arrays = {
        "ctx_1024": v["ctx_1024"],
        "xt": np.ascontiguousarray(v["x"].reshape(TILES, P, D).transpose(1, 0, 2)).reshape(P, TILES * D),
        "ctxN": np.ascontiguousarray(v["ctx_1024"][:, :KEYS - 1].reshape(BATCH, 2, P, D).transpose(2, 0, 1, 3)
                                     ).reshape(P, BATCH * 2 * D),
        "lastkeys": np.ascontiguousarray(v["ctx_1024"][:, KEYS - 1]).reshape(1, BATCH * D),
        "ctxT": np.ascontiguousarray(v["ctx_1024"].transpose(2, 0, 1)).reshape(D, BATCH * KEYS),
        "const": constants(),
        "small": weights(v),
        "f_w1": np.ascontiguousarray(v["L0_ffn_W1"].transpose(1, 0, 2)).reshape(D, E0 * F0),
        "f_w2": np.ascontiguousarray(v["L0_ffn_W2"].reshape(E0, 2, P, D).transpose(2, 0, 1, 3)).reshape(P, E0 * 2 * D),
        "g_w1": v["L1_ffn_inter_w"],
        "g_w2": v["L1_ffn_output_w"],
        "g_b2": v["L1_ffn_output_b"],
        "g_r1": v["L1_ffn_res_inter_w"],
        "g_r2": v["L1_ffn_res_output_w"],
    }
    nc = bacc.Bacc("TRN2", target_bir_lowering=False, num_devices=1)
    aps = {}
    maps = {}
    for name, x in arrays.items():
        maps[name + "_dram"] = np.ascontiguousarray(x)
        aps[name] = nc.dram_tensor(name + "_dram", x.shape, mybir.dt.from_np(x.dtype), kind="ExternalInput").ap()
    aps["rowspace"] = nc.dram_tensor("rowspace_dram", (E1 * CAP + TOKENS, D), F32).ap()
    aps["results"] = nc.dram_tensor("results_dram", (E1 * CAP, D), F32).ap()
    out = nc.dram_tensor("out_dram", v["x"].shape, F32, kind="ExternalOutput").ap()
    build(nc, aps, out)
    r = run_bass_kernel_spmd(nc, [maps], core_ids=[0])
    return r.results[0]["out_dram"]
```
